# Optimizing a Trainium2 kernel written in Bass

```python
import numpy as np
import jax
import jax.numpy as jnp

def _softmax(x, axis=-1):
    return jax.nn.softmax(x, axis=axis)

def _gelu(x):
    return jax.nn.gelu(x, approximate=True)

def _silu(x):
    return jax.nn.silu(x)

def _sigmoid(x):
    return jax.nn.sigmoid(x)

def _layernorm(x, axis=-1, eps=1e-05):
    m = jnp.mean(x, axis=axis, keepdims=True)
    v = jnp.var(x, axis=axis, keepdims=True)
    return (x - m) / jnp.sqrt(v + eps)

def _scatter_add(tgt, idx, src, axis=0):
    return tgt.at[idx].add(src)

def _segment_sum(src, seg, n):
    return jax.ops.segment_sum(src, seg, n)
kernel_name = 'mk_macaron_d2_jaxref_r8_10a10f'

def setup_inputs(seed: int=0):
    np.random.seed(seed)
    _w = jnp.asarray

    def _L0_attn_setup():
        import jax, jax.numpy as jnp
        import numpy as np
        B, L, D = (2, 512, 128)
        DS, RK, K = (16, 64, 3)
        EPS = 1e-05
        key = jax.random.key(seed)
        ks = jax.random.split(key, 16)
        s = 0.02
        inp = {'x': jax.random.normal(ks[0], (B, L, D), jnp.float32), 'gamma': jnp.ones((D,), jnp.float32), 'beta': jnp.zeros((D,), jnp.float32), 'W_in': jax.random.normal(ks[1], (D, 2 * D), jnp.float32) * s, 'conv_w': jax.random.normal(ks[2], (K, 1, D), jnp.float32) * s, 'conv_b': jnp.zeros((D,), jnp.float32), 'W_xp': jax.random.normal(ks[3], (D, RK), jnp.float32) * s, 'W_Bg': jax.random.normal(ks[4], (D, DS), jnp.float32) * s, 'W_Cg': jax.random.normal(ks[5], (D, DS), jnp.float32) * s, 'W_dt': jax.random.normal(ks[6], (RK, D), jnp.float32) * s, 'b_dt': jnp.zeros((D,), jnp.float32), 'W_Bp': jax.random.normal(ks[7], (DS, D), jnp.float32) * s, 'W_Cp': jax.random.normal(ks[8], (DS, D), jnp.float32) * s, 'A': -jnp.exp(jax.random.normal(ks[9], (D,), jnp.float32) * 0.5), 'D_skip': jnp.ones((D,), jnp.float32), 'W_out': jax.random.normal(ks[10], (D, D), jnp.float32) * s}
        return inp
    _L0_attn_in = _L0_attn_setup()

    def _L0_ffn_setup():
        import jax, jax.numpy as jnp
        import numpy as np
        B, T, C = (2, 64, 128)
        I = 512
        E = 8
        K = 2
        key = jax.random.key(seed)
        ks = jax.random.split(key, 8)
        s = 0.02
        return {'x': jax.random.normal(ks[0], (B, T, C), jnp.float32), 'Wr1': jax.random.normal(ks[1], (C, C // 4), jnp.float32) * s, 'br1': jnp.zeros((C // 4,), jnp.float32), 'Wr2': jax.random.normal(ks[2], (C // 4, E), jnp.float32) * s, 'br2': jnp.zeros((E,), jnp.float32), 'Ws1': jax.random.normal(ks[3], (C, I), jnp.float32) * s, 'bs1': jnp.zeros((I,), jnp.float32), 'Ws2': jax.random.normal(ks[4], (I, C), jnp.float32) * s, 'bs2': jnp.zeros((C,), jnp.float32), 'We1': jax.random.normal(ks[5], (E, C, I), jnp.float32) * s, 'be1': jnp.zeros((E, I), jnp.float32), 'We2': jax.random.normal(ks[6], (E, I, C), jnp.float32) * s, 'be2': jnp.zeros((E, C), jnp.float32)}
    _L0_ffn_in = _L0_ffn_setup()

    def _L1_attn_setup():
        import jax, jax.numpy as jnp
        import numpy as np
        B, T, D, S = (4, 256, 128, 64)
        EPS = 1e-08
        key = jax.random.key(seed)
        ks = jax.random.split(key, 6)
        return {'token_embeddings': jax.random.normal(ks[0], (B, T, D), dtype=jnp.float32), 'splat_positions': jax.random.normal(ks[1], (S, D), dtype=jnp.float32), 'splat_log_scales': jax.random.uniform(ks[2], (S,), dtype=jnp.float32), 'splat_amplitudes': jax.random.uniform(ks[3], (S,), dtype=jnp.float32), 'Wv': jax.random.normal(ks[4], (D, D), dtype=jnp.float32) / np.sqrt(D).astype(np.float32), 'Wo': jax.random.normal(ks[5], (D, D), dtype=jnp.float32) / np.sqrt(D).astype(np.float32)}
    _L1_attn_in = _L1_attn_setup()

    def _L1_ffn_setup():
        import jax, jax.numpy as jnp
        import numpy as np
        DIM = 128

        def _reference_tuple_inner(x, W_r, W_k, W_v, mu_r, mu_k):
            B, T, C = x.shape
            x_prev = jnp.concatenate([jnp.zeros((B, 1, C), x.dtype), x[:, :-1, :]], axis=1)
            xr = mu_r * x + (1.0 - mu_r) * x_prev
            xk = mu_k * x + (1.0 - mu_k) * x_prev
            r = jax.nn.sigmoid(jnp.einsum('btc,dc->btd', xr, W_r))
            k = jnp.einsum('btc,dc->btd', xk, W_k)
            k_act = jnp.square(jax.nn.relu(k))
            out = r * jnp.einsum('btc,dc->btd', k_act, W_v)
            new_state = x[:, -1, :]
            return (out, new_state)
        key = jax.random.key(seed)
        ks = jax.random.split(key, 6)
        B, T, C = (8, 256, DIM)
        x = jax.random.normal(ks[0], (B, T, C), dtype=jnp.float32)
        s = 1.0 / np.sqrt(C)
        W_r = jax.random.uniform(ks[1], (C, C), jnp.float32, -s, s)
        W_k = jax.random.uniform(ks[2], (C, C), jnp.float32, -s, s)
        W_v = jax.random.uniform(ks[3], (C, C), jnp.float32, -s, s)
        mu_r = jax.random.uniform(ks[4], (C,), jnp.float32)
        mu_k = jax.random.uniform(ks[5], (C,), jnp.float32)
        return {'x': x, 'W_r': W_r, 'W_k': W_k, 'W_v': W_v, 'mu_r': mu_r, 'mu_k': mu_k}
    _L1_ffn_in = _L1_ffn_setup()
    _d = {'L0_attn_x': _L0_attn_in['x'], 'L0_attn_gamma': _L0_attn_in['gamma'], 'L0_attn_beta': _L0_attn_in['beta'], 'L0_attn_W_in': _L0_attn_in['W_in'], 'L0_attn_conv_w': _L0_attn_in['conv_w'], 'L0_attn_conv_b': _L0_attn_in['conv_b'], 'L0_attn_W_xp': _L0_attn_in['W_xp'], 'L0_attn_W_Bg': _L0_attn_in['W_Bg'], 'L0_attn_W_Cg': _L0_attn_in['W_Cg'], 'L0_attn_W_dt': _L0_attn_in['W_dt'], 'L0_attn_b_dt': _L0_attn_in['b_dt'], 'L0_attn_W_Bp': _L0_attn_in['W_Bp'], 'L0_attn_W_Cp': _L0_attn_in['W_Cp'], 'L0_attn_A': _L0_attn_in['A'], 'L0_attn_D_skip': _L0_attn_in['D_skip'], 'L0_attn_W_out': _L0_attn_in['W_out'], 'L0_ffn_Wr1': _L0_ffn_in['Wr1'], 'L0_ffn_br1': _L0_ffn_in['br1'], 'L0_ffn_Wr2': _L0_ffn_in['Wr2'], 'L0_ffn_br2': _L0_ffn_in['br2'], 'L0_ffn_Ws1': _L0_ffn_in['Ws1'], 'L0_ffn_bs1': _L0_ffn_in['bs1'], 'L0_ffn_Ws2': _L0_ffn_in['Ws2'], 'L0_ffn_bs2': _L0_ffn_in['bs2'], 'L0_ffn_We1': _L0_ffn_in['We1'], 'L0_ffn_be1': _L0_ffn_in['be1'], 'L0_ffn_We2': _L0_ffn_in['We2'], 'L0_ffn_be2': _L0_ffn_in['be2'], 'L1_attn_splat_positions': _L1_attn_in['splat_positions'], 'L1_attn_splat_log_scales': _L1_attn_in['splat_log_scales'], 'L1_attn_splat_amplitudes': _L1_attn_in['splat_amplitudes'], 'L1_attn_Wv': _L1_attn_in['Wv'], 'L1_attn_Wo': _L1_attn_in['Wo'], 'L1_ffn_W_r': _L1_ffn_in['W_r'], 'L1_ffn_W_k': _L1_ffn_in['W_k'], 'L1_ffn_W_v': _L1_ffn_in['W_v'], 'L1_ffn_mu_r': _L1_ffn_in['mu_r'], 'L1_ffn_mu_k': _L1_ffn_in['mu_k']}
    _x0 = _d['L0_attn_x']
    _d['L0_attn_x'] = jax.random.normal(jax.random.fold_in(jax.random.key(seed), 1), (8, 256, 128), dtype=_x0.dtype)
    del _x0
    return _d

def reference(L0_attn_x, L0_attn_gamma, L0_attn_beta, L0_attn_W_in, L0_attn_conv_w, L0_attn_conv_b, L0_attn_W_xp, L0_attn_W_Bg, L0_attn_W_Cg, L0_attn_W_dt, L0_attn_b_dt, L0_attn_W_Bp, L0_attn_W_Cp, L0_attn_A, L0_attn_D_skip, L0_attn_W_out, L0_ffn_Wr1, L0_ffn_br1, L0_ffn_Wr2, L0_ffn_br2, L0_ffn_Ws1, L0_ffn_bs1, L0_ffn_Ws2, L0_ffn_bs2, L0_ffn_We1, L0_ffn_be1, L0_ffn_We2, L0_ffn_be2, L1_attn_splat_positions, L1_attn_splat_log_scales, L1_attn_splat_amplitudes, L1_attn_Wv, L1_attn_Wo, L1_ffn_W_r, L1_ffn_W_k, L1_ffn_W_v, L1_ffn_mu_r, L1_ffn_mu_k):

    def _L0_attn_ref(x, gamma, beta, W_in, conv_w, conv_b, W_xp, W_Bg, W_Cg, W_dt, b_dt, W_Bp, W_Cp, A, D_skip, W_out):
        import jax, jax.numpy as jnp
        import numpy as np
        B, L, D = (2, 512, 128)
        DS, RK, K = (16, 64, 3)
        EPS = 1e-05
        d = x.shape[-1]
        mu = jnp.mean(x, -1, keepdims=True)
        var = jnp.mean(jnp.square(x - mu), -1, keepdims=True)
        xn = (x - mu) * jax.lax.rsqrt(var + EPS) * gamma + beta
        xz = xn @ W_in
        xb, z = jnp.split(xz, 2, axis=-1)
        xc = jax.lax.conv_general_dilated(xb, conv_w, window_strides=(1,), padding='SAME', dimension_numbers=('NWC', 'WIO', 'NWC'), feature_group_count=d) + conv_b
        x_act = jax.nn.silu(xc)
        delta = jax.nn.softplus(x_act @ W_xp @ W_dt + b_dt)
        Bm = x_act @ W_Bg @ W_Bp
        Cm = x_act @ W_Cg @ W_Cp
        dA = jnp.exp(delta * A)
        dBx = delta * Bm * x_act

        def step(h, ab):
            a, bx = ab
            h = a * h + bx
            return (h, h)
        h0 = jnp.zeros_like(dA[:, 0])
        _, hs = jax.lax.scan(step, h0, (dA.transpose(1, 0, 2), dBx.transpose(1, 0, 2)))
        y = Cm * hs.transpose(1, 0, 2)
        out_ssm = y + x_act * D_skip
        gated = out_ssm * jax.nn.silu(z)
        return gated @ W_out + x

    def _L0_ffn_ref(x, Wr1, br1, Wr2, br2, Ws1, bs1, Ws2, bs2, We1, be1, We2, be2):
        import jax, jax.numpy as jnp
        import numpy as np
        B, T, C = (2, 64, 128)
        I = 512
        E = 8
        K = 2
        Bb, Tt, Cc = x.shape
        xf = x.reshape(-1, Cc)
        logits = jax.nn.relu(xf @ Wr1 + br1) @ Wr2 + br2
        gates = jax.nn.softmax(logits, axis=-1)
        tg, ti = jax.lax.top_k(gates, K)
        tg = jax.nn.softmax(tg / K, axis=-1)
        out = jax.nn.silu(xf @ Ws1 + bs1) @ Ws2 + bs2
        for e in range(E):
            h = jax.nn.silu(xf @ We1[e] + be1[e]) @ We2[e] + be2[e]
            w = jnp.sum(tg * (ti == e), axis=-1)
            out = out + w[:, None] * h
        return out.reshape(Bb, Tt, Cc)

    def _L1_attn_ref(token_embeddings, splat_positions, splat_log_scales, splat_amplitudes, Wv, Wo):
        import jax, jax.numpy as jnp
        import numpy as np
        B, T, D, S = (4, 256, 128, 64)
        EPS = 1e-08
        x = token_embeddings
        p = splat_positions
        x2 = jnp.sum(x * x, axis=-1, keepdims=True)
        p2 = jnp.sum(p * p, axis=-1)
        xp = jnp.einsum('btd,sd->bts', x, p)
        d2 = jnp.maximum(x2 + p2[None, None, :] - 2.0 * xp, 0.0)
        scales = jnp.exp(splat_log_scales)
        gauss = splat_amplitudes * jnp.exp(-0.5 * d2 / (scales * scales))
        attn = jnp.einsum('bis,bjs->bij', gauss, gauss)
        attn = attn / (jnp.sum(attn, axis=-1, keepdims=True) + EPS)
        v = jnp.einsum('btd,de->bte', x, Wv)
        out = jnp.einsum('bij,bjd->bid', attn, v)
        return jnp.einsum('btd,de->bte', out, Wo)

    def _L1_ffn_ref(x, W_r, W_k, W_v, mu_r, mu_k):
        import jax, jax.numpy as jnp
        import numpy as np
        DIM = 128

        def _reference_tuple_inner(x, W_r, W_k, W_v, mu_r, mu_k):
            B, T, C = x.shape
            x_prev = jnp.concatenate([jnp.zeros((B, 1, C), x.dtype), x[:, :-1, :]], axis=1)
            xr = mu_r * x + (1.0 - mu_r) * x_prev
            xk = mu_k * x + (1.0 - mu_k) * x_prev
            r = jax.nn.sigmoid(jnp.einsum('btc,dc->btd', xr, W_r))
            k = jnp.einsum('btc,dc->btd', xk, W_k)
            k_act = jnp.square(jax.nn.relu(k))
            out = r * jnp.einsum('btc,dc->btd', k_act, W_v)
            new_state = x[:, -1, :]
            return (out, new_state)
        return _reference_tuple_inner(x, W_r, W_k, W_v, mu_r, mu_k)[0]
    x = L0_attn_x
    x = x + 0.5 * _L0_ffn_ref(_layernorm(x, axis=-1), L0_ffn_Wr1, L0_ffn_br1, L0_ffn_Wr2, L0_ffn_br2, L0_ffn_Ws1, L0_ffn_bs1, L0_ffn_Ws2, L0_ffn_bs2, L0_ffn_We1, L0_ffn_be1, L0_ffn_We2, L0_ffn_be2)
    x = x + _L0_attn_ref(_layernorm(x, axis=-1), L0_attn_gamma, L0_attn_beta, L0_attn_W_in, L0_attn_conv_w, L0_attn_conv_b, L0_attn_W_xp, L0_attn_W_Bg, L0_attn_W_Cg, L0_attn_W_dt, L0_attn_b_dt, L0_attn_W_Bp, L0_attn_W_Cp, L0_attn_A, L0_attn_D_skip, L0_attn_W_out)
    x = x + 0.5 * _L0_ffn_ref(_layernorm(x, axis=-1), L0_ffn_Wr1, L0_ffn_br1, L0_ffn_Wr2, L0_ffn_br2, L0_ffn_Ws1, L0_ffn_bs1, L0_ffn_Ws2, L0_ffn_bs2, L0_ffn_We1, L0_ffn_be1, L0_ffn_We2, L0_ffn_be2)
    x = x + 0.5 * _L1_ffn_ref(_layernorm(x, axis=-1), L1_ffn_W_r, L1_ffn_W_k, L1_ffn_W_v, L1_ffn_mu_r, L1_ffn_mu_k)
    x = x + _L1_attn_ref(_layernorm(x, axis=-1), L1_attn_splat_positions, L1_attn_splat_log_scales, L1_attn_splat_amplitudes, L1_attn_Wv, L1_attn_Wo)
    x = x + 0.5 * _L1_ffn_ref(_layernorm(x, axis=-1), L1_ffn_W_r, L1_ffn_W_k, L1_ffn_W_v, L1_ffn_mu_r, L1_ffn_mu_k)
    return x

_drawn_inputs = setup_inputs


def setup_inputs(seed=0):
    import zlib

    import numpy as np

    out = dict(_drawn_inputs(seed))
    spreads = {'L0_attn_gamma': (1.0, 0.6),
     'L0_attn_beta': (0.0, 0.8),
     'L0_attn_conv_b': (0.0, 0.8),
     'L0_attn_b_dt': (0.0, 0.8),
     'L0_attn_D_skip': (1.0, 0.6),
     'L0_ffn_br1': (0.0, 0.519),
     'L0_ffn_br2': (0.0, 0.1),
     'L0_ffn_bs1': (0.0, 0.435),
     'L0_ffn_bs2': (0.0, 0.1),
     'L0_ffn_be1': (0.0, 0.661),
     'L0_ffn_be2': (0.0, 0.1)}
    factors = {'L0_attn_W_in': 8.0,
     'L0_attn_conv_w': 8.0,
     'L0_attn_W_xp': 8.0,
     'L0_attn_W_Bg': 8.0,
     'L0_attn_W_Cg': 8.0,
     'L0_attn_W_dt': 8.0,
     'L0_attn_W_Bp': 8.0,
     'L0_attn_W_Cp': 8.0,
     'L0_attn_A': 8.0,
     'L0_attn_W_out': 8.0,
     'L1_ffn_W_r': 30.785,
     'L1_ffn_mu_r': 56.367,
     'L1_attn_splat_positions': 8.0,
     'L1_attn_splat_log_scales': 8.0,
     'L1_attn_splat_amplitudes': 8.0,
     'L1_attn_Wv': 8.0,
     'L1_attn_Wo': 8.0,
     'L1_ffn_W_k': 4.04,
     'L1_ffn_W_v': 3.543,
     'L1_ffn_mu_k': 6.268}
    for name, (base, spread) in spreads.items():
        noise = np.random.default_rng([zlib.crc32(name.encode()), seed]).standard_normal(out[name].shape)
        drawn = base * np.exp(spread * noise) if base else spread * noise
        out[name] = jnp.asarray(drawn.astype(out[name].dtype))
    for name, factor in factors.items():
        out[name] = (out[name] * factor).astype(out[name].dtype)
    return out
```

```python
from contextlib import ExitStack

import concourse.bass as bass
from concourse import mybir

ALU = mybir.AluOpType
ACT = mybir.ActivationFunctionType
AX = mybir.AxisListType
F32 = mybir.dt.float32
F32R = mybir.dt.float32r
U32 = mybir.dt.uint32

P = 128
CHUNK = 512
TILES = CHUNK // P
SEQ = 256
SEQS = CHUNK // SEQ
EPS = 1e-5
EPS_ATTN = 1e-8
LOOKAHEAD = 3
Z_BANKS = 4
H_BUFS = 4
Y_BANKS = 2


def hi_on_vector(k):
    return k % 3 == 1


def hi_before(k):
    return sum(not hi_on_vector(i) for i in range(k))


SF_PREP = ["T", "R", "L", "W"]
SF_FULL = ["b0", "b1", "b2", "T", "b3", "R", "b4", "L", "b5", "b6", "b7", "W"]
SF_LAST = [f"b{q}" for q in range(8)]
SA_SETUP = ["cols", "small", "ffn1", "products"]
SA_A = ["T", "xb", "z", "dt", "B", "C", "out"]
SA_R = ["T", "k", "r", "v"]
SA_L = ["T", "xp", "Et", "MT", "B", "sum", "out"]


def macaron_kernel(nc, d, out):
    x_in = d["L0_attn_x"]
    C = x_in.shape[2]
    N_TOK = x_in.shape[0] * x_in.shape[1]
    N_CHUNK = N_TOK // CHUNK
    E, _, I = d["L0_ffn_We1"].shape
    RH = d["L0_ffn_Wr1"].shape[1]
    Q = E + 1
    IT = I // P
    STEPS = Q * IT
    N_SLOT = 2 * N_CHUNK
    RK, DS = d["L0_attn_W_dt"].shape[0], d["L0_attn_W_Bp"].shape[0]
    S = d["L1_attn_splat_positions"].shape[0]
    assert C == P and x_in.shape[1] == SEQ and E == 8 and STEPS % Z_BANKS == 0 and STEPS % H_BUFS == 0

    with ExitStack() as ctx:
        def sb(name, shape, dt=F32):
            return ctx.enter_context(nc.sbuf_tensor(name, shape, dt))

        def sem(name):
            return ctx.enter_context(nc.semaphore(name))

        def bank(name):
            return ctx.enter_context(nc.psum_tensor(name, [P, CHUNK], F32))

        x = sb("x_res", [P, N_TOK])
        w1_raw = sb("w1_raw", [P, Q, I])
        w2_raw = sb("w2_raw", [P, Q, IT, C])
        w1_hi, w1_lo = sb("w1_hi", [P, Q, I], F32R), sb("w1_lo", [P, Q, I], F32R)
        w2_hi, w2_lo = sb("w2_hi", [P, Q, IT, C], F32R), sb("w2_lo", [P, Q, IT, C], F32R)
        ident = sb("ident", [P, P])
        f_stat, f_mv, f_rstd = sb("f_stat", [P, TILES, 6]), sb("f_mv", [P, TILES, 2]), sb("f_rstd", [P, TILES])
        f_xh = sb("f_xh", [P, CHUNK])
        xT_hi, xT_lo = sb("xT_hi", [P, 2, CHUNK], F32R), sb("xT_lo", [P, 2, CHUNK], F32R)
        h = [sb(f"h{i}", [P, CHUNK]) for i in range(H_BUFS)]
        h_hi = [sb(f"h_hi{i}", [P, CHUNK], F32R) for i in range(H_BUFS)]
        h_lo = [sb(f"h_lo{i}", [P, CHUNK], F32R) for i in range(H_BUFS)]
        acc = sb("acc", [P, CHUNK])
        weighted = [sb(f"weighted{i}", [P, CHUNK]) for i in range(2)]
        w_bc = [sb(f"w_bc{i}", [P, CHUNK]) for i in range(2)]
        wr1_raw = sb("wr1_raw", [P, P])
        wr1_hi, wr1_lo = sb("wr1_hi", [P, P], F32R), sb("wr1_lo", [P, P], F32R)
        wr2 = sb("wr2", [RH + 1, E])
        br1 = sb("br1", [RH, 1])
        r1 = sb("r1", [RH + 1, CHUNK])
        lg_max, ex = sb("lg_max", [P, TILES]), sb("ex", [P, TILES, E])
        lg = sb("lg", [P, TILES, E])
        ex_sum, ex_rec = sb("ex_sum", [P, TILES]), sb("ex_rec", [P, TILES])
        gates, top = sb("gates", [P, TILES, E]), sb("top", [P, TILES, 8])
        top_at, top_atf = sb("top_at", [P, TILES, 8], U32), sb("top_atf", [P, TILES, 2])
        diff, ratio, ratio1 = sb("diff", [P, TILES]), sb("ratio", [P, TILES]), sb("ratio1", [P, TILES])
        tw = sb("tw", [P, TILES, 2])
        expert_no_i, expert_no = sb("expert_no_i", [P, E], mybir.dt.int32), sb("expert_no", [P, E])
        pick = [sb(f"pick{i}", [P, TILES, E]) for i in range(2)]
        pickw = [sb(f"pickw{i}", [P, TILES, E]) for i in range(2)]
        w_tok = sb("w_tok", [P, TILES, E])
        wT = sb("wT", [40, CHUNK], F32R)
        sel = sb("sel", [40, E, P], F32R)
        sel_raw = sb("sel_raw", [40, E, P])
        zero_row = sb("zero_row", [40, CHUNK])
        ROWS = IT * Q + Q + 11
        rows = sb("rows", [ROWS, P])
        cols = sb("cols", [P, ROWS])
        w_in = sb("w_in", [P, 2 * C])
        w_xp, w_bg, w_cg = sb("w_xp", [P, RK]), sb("w_bg", [P, DS]), sb("w_cg", [P, DS])
        w_dt, w_bp, w_cp = sb("w_dt", [RK, C]), sb("w_bp", [DS, C]), sb("w_cp", [DS, C])
        w_out = sb("w_out", [P, C])
        small = sb("small", [P, S + 3 * P])
        pT = small[:, 0:S]
        w_xpT, w_bgT, w_cgT = small[0:RK, S:S + P], small[0:DS, S + P:S + 2 * P], small[0:DS, S + 2 * P:S + 3 * P]
        ffn_raw = sb("ffn_raw", [P, 4, P])
        ffnT = sb("ffnT", [P, 4, P])
        wo = sb("wo", [P, P])
        prod = sb("prod", [P, 4, P])
        pos = sb("pos", [S, P])
        pos_sq = sb("pos_sq", [S, P])
        nhalf_p2, logs, amp = sb("nhalf_p2", [S, 1]), sb("logs", [S, 1]), sb("amp", [S, 1])
        amp2, inv_s2 = sb("amp2", [S, 1]), sb("inv_s2", [S, 1])
        one_mu = sb("one_mu", [P, 2])
        nhalf = sb("nhalf", [P, S])
        mhalf_exp = sb("mhalf_exp", [P, TILES])
        s_stat, s_mv = sb("s_stat", [P, TILES, 6]), sb("s_mv", [P, TILES, 2])
        s_r1, s_r2, s_v2 = sb("s_r1", [P, TILES]), sb("s_r2", [P, TILES]), sb("s_v2", [P, TILES])
        assert I == CHUNK
        side = [w1_raw[:, q, :] for q in range(Q)] + [sb(f"side{i}", [P, CHUNK])[:, :] for i in range(3)]
        xb_pad = sb("xb_pad", [P, SEQS, SEQ + 2])
        xT_pad = sb("xT_pad", [P, SEQS, SEQ + 1])
        a_xh1, a_xh2, a_xnT, a_c, a_xact, a_sz, a_u, a_l, a_dl, a_dA, a_dB, a_h = side
        r_xh, r_tk, r_tr, r_xk, r_xr, r_rk, r_ka, r_rr, r_t = side[0:9]
        l_xh, l_xT, l_sq, l_dd, l_E, l_Et, l_MT, l_R2 = side[1:9]
        gsum, gsum2 = sb("gsum", [S, SEQS]), sb("gsum2", [S, SEQS])
        den, rden = sb("den", [P, TILES]), sb("rden", [P, TILES])

        z = [bank(f"z{i}") for i in range(Z_BANKS)]
        y = [bank(f"y{i}") for i in range(Y_BANKS)]
        SF, SA = bank("SF"), bank("SA")

        at = {}
        row_loads = []
        r0 = 0
        for name, view, n in [
            ("bs1", d["L0_ffn_bs1"].rearrange("(a b) -> a b", b=P), IT),
            ("be1", d["L0_ffn_be1"].rearrange("e (a b) -> (e a) b", b=P), E * IT),
            ("bs2", d["L0_ffn_bs2"].rearrange("(a b) -> a b", b=P), 1),
            ("be2", d["L0_ffn_be2"], E),
            ("conv_w", d["L0_attn_conv_w"].rearrange("k a c -> (k a) c"), 3),
            ("gamma", d["L0_attn_gamma"].rearrange("(a b) -> a b", b=P), 1),
            ("beta", d["L0_attn_beta"].rearrange("(a b) -> a b", b=P), 1),
            ("conv_b", d["L0_attn_conv_b"].rearrange("(a b) -> a b", b=P), 1),
            ("b_dt", d["L0_attn_b_dt"].rearrange("(a b) -> a b", b=P), 1),
            ("A", d["L0_attn_A"].rearrange("(a b) -> a b", b=P), 1),
            ("D", d["L0_attn_D_skip"].rearrange("(a b) -> a b", b=P), 1),
            ("mu_k", d["L1_ffn_mu_k"].rearrange("(a b) -> a b", b=P), 1),
            ("mu_r", d["L1_ffn_mu_r"].rearrange("(a b) -> a b", b=P), 1),
        ]:
            at[name] = r0
            row_loads.append((r0, n, view))
            r0 += n
        assert r0 == ROWS

        def col(name, i=0):
            return cols[:, at[name] + i:at[name] + i + 1]

        def col_of(name, k):
            return cols[:, at[name] + k:at[name] + k + 1]

        x_loaded = [sem(f"x_loaded{c}") for c in range(N_CHUNK)]
        w_loaded = [sem(f"w_loaded{q}") for q in range(Q)]
        rows_loaded, router_loaded, side_loaded = sem("rows_loaded"), sem("router_loaded"), sem("side_loaded")
        consts_made = sem("consts_made")
        dve_consts = sem("dve_consts")
        w_hi_made, w_split = sem("w_hi_made"), sem("w_split")
        router_hi, router_split = sem("router_hi"), sem("router_split")
        setup_act = sem("setup_act")
        f_bn, f_stats, f_rstd_in, f_rstd_done, f_xh_done = (sem(n) for n in (
            "f_bn", "f_stats", "f_rstd_in", "f_rstd_done", "f_xh_done"))
        s_bn, s_stats, s_rstd_steps, s_rstd_done, s_xh_done = (sem(n) for n in (
            "s_bn", "s_stats", "s_rstd_steps", "s_rstd_done", "s_xh_done"))
        sf_written, sf_read = sem("sf_written"), sem("sf_read")
        sa_written, sa_read = sem("sa_written"), sem("sa_read")
        xT_hi_made, wT_hi_made = sem("xT_hi_made"), sem("wT_hi_made")
        gate_step, gate_exp, gate_ratio, gate_diff, gate_w = (sem(n) for n in (
            "gate_step", "gate_exp", "gate_ratio", "gate_diff", "gate_w"))
        z_ready, h_ready, hi_ready, lo_ready, y_step = (sem(n) for n in (
            "z_ready", "h_ready", "hi_ready", "lo_ready", "y_step"))
        y_read, acc_added, accT_ready = sem("y_read"), sem("acc_added"), sem("accT_ready")
        a_res, a_mid, a_conv, a_act, a_soft, a_relu, a_delta, a_decay, a_drive, a_scan, a_y, a_gated = (sem(n) for n in (
            "a_res", "a_mid", "a_conv", "a_act", "a_soft", "a_relu", "a_delta", "a_decay", "a_drive",
            "a_scan", "a_y", "a_gated"))
        r_prev, r_mixed, r_sq, r_prod, r_done = (sem(n) for n in ("r_prev", "r_mixed", "r_sq", "r_prod", "r_done"))
        l_sq_done, l_exp, l_gs, l_rec = (sem(n) for n in ("l_sq_done", "l_exp", "l_gs", "l_rec"))
        stored = sem("stored")
        wait_carried = sem("wait_carried")

        def wait(eng, s, value):
            if not isinstance(value, int) or value > 0:
                eng.wait_ge(s, value)

        def wait_apart(eng, s, value):
            wait(eng, s, value)
            if not isinstance(value, int):
                eng.sem_inc(wait_carried, 1)

        def sf_at(s, use):
            if isinstance(s, int) and s == -1:
                return SF_PREP.index(use)
            order = SF_LAST if isinstance(s, int) and s == N_SLOT - 1 else SF_FULL
            return len(SF_FULL) * s + len(SF_PREP) + order.index(use)

        SA_A0 = len(SA_SETUP)
        SA_T0 = SA_A0 + N_CHUNK * len(SA_A)
        SA_T = 2 * len(SA_R) + len(SA_L)

        def sa_setup(use):
            return SA_SETUP.index(use)

        def sa_a(j, use):
            return j * len(SA_A) + SA_A0 + SA_A.index(use)

        def sa_r(j, o, use):
            return j * SA_T + SA_T0 + o * (len(SA_R) + len(SA_L)) + SA_R.index(use)

        def sa_l(j, use):
            return j * SA_T + SA_T0 + len(SA_R) + SA_L.index(use)

        def xs(c, t=None):
            if t is None:
                return x[:, bass.ds(c * CHUNK, CHUNK)]
            return x[:, bass.ds(c * CHUNK + t * P, P)]

        def tile(a, t):
            return a[:, t * P:(t + 1) * P]

        def prepared(s):
            return sf_at(s - 1, "T") + 1

        block = ctx.enter_context(nc.Block())

        def at_step(plan, k, *args):
            for step, work in plan:
                if step == k:
                    work(*args)

        @block.sync
        def _(sp):
            tok = x_in.rearrange("b s c -> (b s) c").rearrange("(c t p) f -> c p t f", p=P, t=TILES)

            def load_x(c):
                sp.dma_start(x[:, c * CHUNK:(c + 1) * CHUNK].rearrange("p (t f) -> p t f", f=C), tok[c])\
                    .then_inc(x_loaded[c], 16)

            def load_expert(q):
                w1 = d["L0_ffn_Ws1"] if q == 0 else d["L0_ffn_We1"][q - 1]
                w2 = d["L0_ffn_Ws2"] if q == 0 else d["L0_ffn_We2"][q - 1]
                sp.dma_start(w1_raw[:, q, :], w1).then_inc(w_loaded[q], 16)
                sp.dma_start(w2_raw[:, q, :, :], w2.rearrange("(i p) c -> p i c", p=P)).then_inc(w_loaded[q], 16)

            load_x(0)
            load_expert(0)
            for r, n, view in row_loads:
                sp.dma_start(rows[r:r + n, :], view).then_inc(rows_loaded, 16)
            load_expert(1)
            load_x(1)
            load_expert(2)
            load_expert(3)
            load_x(2)
            load_x(3)
            for q in range(4, Q):
                load_expert(q)
            res = out.rearrange("b s c -> (b s) c").rearrange("(c t p) f -> c p t f", p=P, t=TILES)
            for c in range(N_CHUNK):
                sp.wait_ge(r_done, 2 * c + 2)
                sp.dma_start(res[c], x[:, c * CHUNK:(c + 1) * CHUNK].rearrange("p (t f) -> p t f", f=C))\
                    .then_inc(stored, 16)
            sp.wait_ge(stored, 16 * N_CHUNK)

        SIDE_LOADS = [
            (w_in[:, :], d["L0_attn_W_in"]), (w_xp[:, :], d["L0_attn_W_xp"]), (w_bg[:, :], d["L0_attn_W_Bg"]),
            (w_cg[:, :], d["L0_attn_W_Cg"]), (w_dt[:, :], d["L0_attn_W_dt"]), (w_bp[:, :], d["L0_attn_W_Bp"]),
            (w_cp[:, :], d["L0_attn_W_Cp"]), (w_out[:, :], d["L0_attn_W_out"]),
            (ffn_raw[:, 0, :], d["L1_ffn_W_k"]), (ffn_raw[:, 1, :], d["L1_ffn_W_r"]),
            (ffn_raw[:, 2, :], d["L1_ffn_W_v"]), (ffn_raw[:, 3, :], d["L1_attn_Wv"]), (wo[:, :], d["L1_attn_Wo"]),
            (pos[:, :], d["L1_attn_splat_positions"]),
            (logs[:, :], d["L1_attn_splat_log_scales"].rearrange("(a b) -> a b", b=1)),
            (amp[:, :], d["L1_attn_splat_amplitudes"].rearrange("(a b) -> a b", b=1)),
        ]

        @block.gpsimd
        def _(pool):
            made = 0

            def const(ins):
                nonlocal made
                made += 1
                ins.then_inc(consts_made, 1)
                pool.wait_ge(consts_made, made)

            const(pool.memset(ident[:, :], 0.0))
            const(pool.affine_select(out=ident[:, :], in_=ident[:, :], compare_op=ALU.not_equal, fill=1.0, base=0,
                                     pattern=[[-1, P]], channel_multiplier=1))
            const(pool.memset(mhalf_exp[:, :], -0.5))
            const(pool.memset(wr1_raw[:, RH:P], 0.0))
            const(pool.memset(r1[RH:RH + 1, :], 1.0))
            const(pool.iota(expert_no_i[:, :], pattern=[[1, E]], base=0, channel_multiplier=0))
            const(pool.memset(sel_raw[:, :, :], 0.0))
            for off in (0, 32):
                const(pool.affine_select(out=sel_raw[:, :, :], in_=sel_raw[:, :, :], compare_op=ALU.not_equal,
                                         fill=1.0, base=-off, pattern=[[-1, E], [0, P]], channel_multiplier=1))
            const(pool.memset(zero_row[:, :], 0.0))
            const(pool.memset(xb_pad[:, :, :], 0.0))
            const(pool.memset(xT_pad[:, :, :], 0.0))
            const(pool.memset(nhalf[:, :], -0.5))
            for dst, src in ((wr1_raw[:, 0:RH], d["L0_ffn_Wr1"]), (wr2[0:RH, :], d["L0_ffn_Wr2"]),
                             (wr2[RH:RH + 1, :], d["L0_ffn_br2"].rearrange("(a b) -> a b", a=1)),
                             (br1[:, :], d["L0_ffn_br1"].rearrange("(a b) -> a b", b=1))):
                pool.dma_start(dst, src).then_inc(router_loaded, 16)

            def f_rstd_of(n):
                wait_apart(pool, f_stats, n + 1)
                pool.tensor_scalar(f_rstd[:, :], f_mv[:, :, 1], EPS, None, ALU.add).then_inc(f_rstd_in, 1)
                wait(pool, f_rstd_in, n + 1)
                pool.tensor_tensor(f_rstd[:, :], f_rstd[:, :], mhalf_exp[:, :], ALU.pow).then_inc(f_rstd_done, 1)

            def add(s, q):
                wait(pool, y_read, s * (Q + 1) + q + 1)
                wait(pool, acc_added, s * E + q - 1)
                pool.tensor_tensor(acc[:, :], acc[:, :], weighted[q % 2][:, :], ALU.add).then_inc(acc_added, 1)

            def split_hi(q):
                pool.wait_ge(w_loaded[q], 32)
                pool.tensor_copy(w1_hi[:, q, :], w1_raw[:, q, :]).then_inc(w_hi_made, 1)
                pool.tensor_copy(w2_hi[:, q, :, :], w2_raw[:, q, :, :]).then_inc(w_hi_made, 1)

            def a_rstd(j):
                n = j * 6
                wait_apart(pool, s_stats, j + 1)
                pool.tensor_scalar(s_r1[:, :], s_mv[:, :, 1], EPS, None, ALU.add).then_inc(s_rstd_steps, 1)
                wait(pool, s_rstd_steps, n + 1)
                pool.tensor_tensor(s_r1[:, :], s_r1[:, :], mhalf_exp[:, :], ALU.pow).then_inc(s_rstd_steps, 1)
                wait(pool, s_rstd_steps, n + 2)
                pool.tensor_tensor(s_v2[:, :], s_r1[:, :], s_r1[:, :], ALU.mult).then_inc(s_rstd_steps, 1)
                wait(pool, s_rstd_steps, n + 3)
                pool.tensor_tensor(s_v2[:, :], s_v2[:, :], s_mv[:, :, 1], ALU.mult).then_inc(s_rstd_steps, 1)
                wait_apart(pool, s_rstd_steps, n + 4)
                pool.tensor_scalar(s_v2[:, :], s_v2[:, :], EPS, None, ALU.add).then_inc(s_rstd_steps, 1)
                wait(pool, s_rstd_steps, n + 5)
                pool.tensor_tensor(s_v2[:, :], s_v2[:, :], mhalf_exp[:, :], ALU.pow).then_inc(s_rstd_steps, 1)
                wait(pool, s_rstd_steps, n + 6)
                pool.tensor_tensor(s_r2[:, :], s_v2[:, :], s_r1[:, :], ALU.mult).then_inc(s_rstd_done, 1)

            def a_residual(j):
                wait(pool, s_xh_done, j + 1)
                pool.tensor_tensor(xs(j), xs(j), a_xh1[:, :], ALU.add).then_inc(a_res, 1)

            def a_conv_mid(j):
                wait_apart(pool, sa_read, sa_a(j, "xb") + 1)
                pool.tensor_scalar(a_c[:, :].rearrange("p (b s) -> p b s", b=SEQS), xb_pad[:, :, 1:SEQ + 1],
                                   col("conv_w", 1), col("conv_b"), ALU.mult, ALU.add).then_inc(a_mid, 1)

            def a_relu_u(j):
                wait_apart(pool, sa_read, sa_a(j, "dt") + 1)
                pool.tensor_scalar(a_dl[:, :], a_u[:, :], 0.0, None, ALU.max).then_inc(a_relu, 1)

            def a_delta_sum(j):
                wait(pool, a_soft, 3 * j + 3)
                wait(pool, a_relu, j + 1)
                pool.tensor_tensor(a_dl[:, :], a_dl[:, :], a_l[:, :], ALU.add).then_inc(a_delta, 1)

            def a_drive_x(j):
                wait(pool, sa_read, sa_a(j, "B") + 1)
                wait(pool, a_act, j + 1)
                pool.tensor_tensor(a_dB[:, :], a_dB[:, :], a_xact[:, :], ALU.mult).then_inc(a_drive, 1)

            def a_gate(j):
                wait(pool, a_y, j + 1)
                wait(pool, sa_read, sa_a(j, "z") + 1)
                pool.tensor_tensor(a_h[:, :], a_h[:, :], a_sz[:, :], ALU.mult).then_inc(a_gated, 1)

            A_POOL = [(5, a_rstd), (7, a_residual), (14, a_conv_mid), (20, a_relu_u), (23, a_delta_sum),
                      (26, a_drive_x), (31, a_gate)]

            def t_rstd(j, o):
                n = 6 * N_CHUNK + (j * 3 + o) * 1
                wait_apart(pool, s_stats, N_CHUNK + j * 3 + o + 1)
                pool.tensor_scalar(s_r1[:, :], s_mv[:, :, 1], EPS, None, ALU.add).then_inc(s_rstd_steps, 1)
                wait(pool, s_rstd_steps, n + 1)
                pool.tensor_tensor(s_r1[:, :], s_r1[:, :], mhalf_exp[:, :], ALU.pow).then_inc(s_rstd_done, 1)

            def r_shift(o2):
                def work(j):
                    wait_apart(pool, sa_read, sa_r(j, o2, "T") + 1)
                    prev = xT_pad[:, :, 0:SEQ]
                    for n, dst in ((0, r_tk), (1, r_tr)):
                        pool.tensor_scalar(dst[:, :].rearrange("p (b s) -> p b s", b=SEQS), prev,
                                           one_mu[:, n:n + 1], None, ALU.mult).then_inc(r_prev, 1)
                return work

            def r_square(o2):
                def work(j):
                    wait(pool, sa_read, sa_r(j, o2, "k") + 1)
                    pool.tensor_tensor(r_ka[:, :], r_rk[:, :], r_rk[:, :], ALU.mult).then_inc(r_sq, 1)
                return work

            def l_square(j):
                wait(pool, sa_read, sa_l(j, "T") + 1)
                pool.tensor_tensor(l_sq[:, :], l_xT[:, :], l_xT[:, :], ALU.mult).then_inc(l_sq_done, 1)

            T_POOL = [(5, lambda j: t_rstd(j, 0)), (8, r_shift(0)), (11, r_square(0)),
                      (16, lambda j: t_rstd(j, 1)), (18, l_square),
                      (28, lambda j: t_rstd(j, 2)), (30, r_shift(1)), (33, r_square(1))]

            def slot(s, prep, side):
                for k in range(STEPS):
                    if k == 1 and not (isinstance(s, int) and s == 0):
                        add(s - 1, E)
                    if k % IT == 1 and 2 <= k // IT:
                        add(s, k // IT - 1)
                    if prep and k == 8:
                        f_rstd_of(s + 1)
                    if isinstance(s, int) and s == 0 and k % IT == 2 and k // IT + 2 < Q:
                        split_hi(k // IT + 2)
                    if side == "A":
                        at_step(A_POOL, k, s - 1)
                    if side == "T":
                        at_step(T_POOL, k, s - (N_CHUNK + 1))

            pool.wait_ge(router_loaded, 16 * 4)
            pool.tensor_copy(wr1_hi[:, :], wr1_raw[:, :]).then_inc(router_hi, 1)
            f_rstd_of(0)
            split_hi(0)
            split_hi(1)
            slot(0, True, None)
            with pool.Fori(1, N_CHUNK + 1) as s:
                slot(s, True, "A")
            with pool.Fori(N_CHUNK + 1, N_SLOT - 1) as s:
                slot(s, True, "T")
            slot(N_SLOT - 1, False, "T")
            add(N_SLOT - 1, E)
            for _, work in T_POOL:
                work(N_CHUNK - 1)

        @block.scalar
        def _(act):
            for dst, src in SIDE_LOADS:
                act.dma_start(dst, src).then_inc(side_loaded, 16)

            def silu(s, k):
                n = s * STEPS + k
                wait(act, z_ready, n + 1)
                wait(act, lo_ready, n + 1 - H_BUFS)
                if not hi_on_vector(k):
                    wait(act, y_step, n + 1 - H_BUFS)
                    act.activation(h_hi[k % H_BUFS][:, :], z[k % Z_BANKS][:, :], ACT.Silu,
                                   bias=col_of("bs1", k))
                act.activation(h[k % H_BUFS][:, :], z[k % Z_BANKS][:, :], ACT.Silu,
                               bias=col_of("bs1", k)).then_inc(h_ready, 1)

            def spread(s, q):
                wait(act, sf_written, sf_at(s, f"b{q}") + 1)
                wait(act, y_read, s * (Q + 1) + (q if q >= 2 else q - 2))
                act.activation(w_bc[q % 2][:, :], SF[:, :], ACT.Copy).then_inc(sf_read, 1)

            def router_relu(n):
                wait(act, sf_written, sf_at(n - 1, "R") + 1)
                act.activation(r1[0:RH, :], SF[0:RH, :], ACT.Relu, bias=br1[:, :]).then_inc(sf_read, 1)

            def gate_exponent(n):
                wait(act, sf_read, sf_at(n - 1, "L") + 1)
                act.activation(ex[:, :, :], lg[:, :, :], ACT.Exp).then_inc(gate_exp, 1)

            def gate_ratio_of(n):
                wait(act, gate_diff, n + 1)
                act.activation(ratio[:, :], diff[:, :], ACT.Exp, scale=0.5).then_inc(gate_ratio, 1)

            def a_silu_z(j):
                wait(act, sa_written, sa_a(j, "z") + 1)
                act.activation(a_sz[:, :], SA[:, :], ACT.Silu).then_inc(sa_read, 1)

            def a_silu_x(j):
                wait(act, a_conv, 2 * j + 2)
                act.activation(a_xact[:, :], a_c[:, :], ACT.Silu).then_inc(a_act, 1)

            def a_softplus(j):
                wait(act, sa_read, sa_a(j, "dt") + 1)
                act.activation(a_l[:, :], a_u[:, :], ACT.Abs).then_inc(a_soft, 1)
                wait(act, a_soft, 3 * j + 1)
                act.activation(a_l[:, :], a_l[:, :], ACT.Exp, scale=-1.0).then_inc(a_soft, 1)
                wait(act, a_soft, 3 * j + 2)
                act.activation(a_l[:, :], a_l[:, :], ACT.Ln, bias=1.0).then_inc(a_soft, 1)

            def a_decay_of(j):
                wait(act, a_delta, j + 1)
                act.activation(a_dA[:, :], a_dl[:, :], ACT.Exp, scale=col("A")).then_inc(a_decay, 1)

            A_ACT = [(16, a_silu_z), (18, a_silu_x), (21, a_softplus), (24, a_decay_of)]

            def r_evac(o2):
                def work(j):
                    wait(act, sa_written, sa_r(j, o2, "T") + 1)
                    act.activation(xT_pad[:, :, 1:SEQ + 1], SA[:, :].rearrange("p (b s) -> p b s", b=SEQS),
                                   ACT.Copy).then_inc(sa_read, 1)
                return work

            def r_relu(o2):
                def work(j):
                    wait(act, sa_written, sa_r(j, o2, "k") + 1)
                    act.activation(r_rk[:, :], SA[:, :], ACT.Relu).then_inc(sa_read, 1)
                return work

            def r_sigmoid(o2):
                def work(j):
                    wait(act, sa_written, sa_r(j, o2, "r") + 1)
                    act.activation(r_rr[:, :], SA[:, :], ACT.Sigmoid).then_inc(sa_read, 1)
                return work

            def l_evac(j):
                wait(act, sa_written, sa_l(j, "T") + 1)
                act.activation(l_xT[:, :], SA[:, :], ACT.Copy).then_inc(sa_read, 1)

            def l_gauss(j):
                wait(act, sa_read, sa_l(j, "xp") + 1)
                for b in range(SEQS):
                    act.activation(l_E[0:S, b * SEQ:(b + 1) * SEQ], l_dd[0:S, b * SEQ:(b + 1) * SEQ], ACT.Exp,
                                   scale=inv_s2[:, :], accum_out=gsum[:, b:b + 1]).then_inc(l_exp, 1)

            def l_evac_E(j):
                wait(act, sa_written, sa_l(j, "Et") + 1)
                act.activation(l_Et[:, 0:TILES * S], SA[:, 0:TILES * S], ACT.Copy).then_inc(sa_read, 1)

            T_ACT = [(8, r_evac(0)), (11, r_relu(0)), (12, r_sigmoid(0)),
                     (17, l_evac), (20, l_gauss), (22, l_evac_E),
                     (30, r_evac(1)), (33, r_relu(1)), (34, r_sigmoid(1))]

            def slot(s, prep, side):
                for k in range(STEPS):
                    silu(s, k)
                    if prep and k == 16:
                        router_relu(s + 1)
                    if k % IT == 3 and k // IT < E:
                        spread(s, k // IT)
                    if prep and k == 21:
                        gate_exponent(s + 1)
                    if prep and k == 24:
                        gate_ratio_of(s + 1)
                    if side == "A":
                        at_step(A_ACT, k, s - 1)
                    if side == "T":
                        at_step(T_ACT, k, s - (N_CHUNK + 1))

            act.wait_ge(router_loaded, 16 * 4)
            router_relu(0)
            gate_exponent(0)
            gate_ratio_of(0)
            act.wait_ge(side_loaded, 16 * len(SIDE_LOADS))
            act.activation(inv_s2[:, :], logs[:, :], ACT.Exp, scale=-2.0).then_inc(setup_act, 1)
            act.wait_ge(sa_read, sa_setup("cols") + 1)
            slot(0, True, None)
            with act.Fori(1, N_CHUNK + 1) as s:
                slot(s, True, "A")
            with act.Fori(N_CHUNK + 1, N_SLOT - 1) as s:
                slot(s, True, "T")
            slot(N_SLOT - 1, False, "T")
            for _, work in T_ACT:
                work(N_CHUNK - 1)

        @block.vector
        def _(dve):
            def norm_stats(c, stat, mv, bn, stats, count):
                for t in range(TILES):
                    last = dve.bn_stats(stat[:, t, :], xs(c, t))
                last.then_inc(bn, 1)
                wait_apart(dve, bn, count + 1)
                for t in range(TILES):
                    last = dve.bn_aggr(mv[:, t, :], stat[:, t, :])
                last.then_inc(stats, 1)

            def norm_apply(c, dst, mv, rstd):
                for t in range(TILES):
                    last = dve.tensor_scalar(tile(dst, t), xs(c, t), mv[:, t, 0:1], rstd[:, t:t + 1],
                                             ALU.subtract, ALU.mult)
                return last

            def chunk_of(n):
                return n % N_CHUNK if isinstance(n, int) else n & (N_CHUNK - 1)

            def f_moments(n):
                norm_stats(chunk_of(n), f_stat, f_mv, f_bn, f_stats, n)

            def f_norm(n):
                wait(dve, f_rstd_done, n + 1)
                norm_apply(chunk_of(n), f_xh, f_mv, f_rstd).then_inc(f_xh_done, 1)

            def f_split(n):
                wait(dve, sf_written, sf_at(n - 1, "T") + 1)
                par = n % 2 if isinstance(n, int) else n & 1
                dve.tensor_copy(xT_hi[:, par, :], SF[:, :]).then_inc(xT_hi_made, 1)
                wait(dve, xT_hi_made, n + 1)
                dve.tensor_tensor(xT_lo[:, par, :], SF[:, :], xT_hi[:, par, :].bitcast(F32), ALU.subtract)\
                    .then_inc(sf_read, 1)

            GATE = 16

            def gate_logits(n):
                wait(dve, sf_written, sf_at(n - 1, "L") + 1)
                logits = SF[:, 0:TILES * E].rearrange("p (t e) -> p t e", e=E)
                dve.tensor_reduce(lg_max[:, :], logits, AX.X, ALU.max).then_inc(gate_step, 1)
                wait(dve, gate_step, GATE * n + 1)
                dve.tensor_tensor(lg[:, :, :], logits, lg_max[:, :].unsqueeze(2).to_broadcast([P, TILES, E]),
                                  ALU.subtract).then_inc(sf_read, 1)

            def gate_top(n):
                g = GATE * n
                wait(dve, gate_exp, n + 1)
                dve.tensor_reduce(ex_sum[:, :], ex[:, :, :], AX.X, ALU.add).then_inc(gate_step, 1)
                wait(dve, gate_step, g + 2)
                dve.reciprocal(ex_rec[:, :], ex_sum[:, :]).then_inc(gate_step, 1)
                wait(dve, gate_step, g + 3)
                dve.tensor_tensor(gates[:, :, :], ex[:, :, :], ex_rec[:, :].unsqueeze(2).to_broadcast([P, TILES, E]),
                                  ALU.mult).then_inc(gate_step, 1)
                wait_apart(dve, gate_step, g + 4)
                for t in range(TILES):
                    last = dve.max(top[:, t, :], gates[:, t, :])
                last.then_inc(gate_step, 1)
                wait(dve, gate_step, g + 5)
                dve.tensor_tensor(diff[:, :], top[:, :, 1], top[:, :, 0], ALU.subtract).then_inc(gate_diff, 1)
                for t in range(TILES):
                    last = dve.max_index(top_at[:, t, :], top[:, t, :], gates[:, t, :])
                last.then_inc(gate_step, 1)
                wait(dve, gate_step, g + 6)
                dve.tensor_copy(top_atf[:, :, :], top_at[:, :, 0:2]).then_inc(gate_step, 1)
                wait(dve, gate_step, g + 7)
                for i in range(2):
                    dve.tensor_tensor(pick[i][:, :, :], expert_no[:, :].unsqueeze(1).to_broadcast([P, TILES, E]),
                                      top_atf[:, :, i:i + 1].to_broadcast([P, TILES, E]), ALU.is_equal)\
                        .then_inc(gate_step, 1)

            def gate_weights(n):
                g = GATE * n + 9
                wait(dve, gate_ratio, n + 1)
                dve.tensor_scalar(ratio1[:, :], ratio[:, :], 1.0, None, ALU.add).then_inc(gate_step, 1)
                wait(dve, gate_step, g + 1)
                dve.reciprocal(tw[:, :, 0], ratio1[:, :]).then_inc(gate_step, 1)
                wait(dve, gate_step, g + 2)
                dve.tensor_tensor(tw[:, :, 1], tw[:, :, 0], ratio[:, :], ALU.mult).then_inc(gate_step, 1)
                wait(dve, gate_step, g + 3)
                for i in range(2):
                    dve.tensor_tensor(pickw[i][:, :, :], pick[i][:, :, :], tw[:, :, i:i + 1].to_broadcast([P, TILES, E]),
                                      ALU.mult).then_inc(gate_step, 1)
                wait(dve, gate_step, g + 5)
                dve.tensor_tensor(w_tok[:, :, :], pickw[0][:, :, :], pickw[1][:, :, :], ALU.add).then_inc(gate_w, 1)
                dve.tensor_scalar(lg_max[:, :], lg_max[:, :], 0.0, None, ALU.mult).then_inc(gate_step, 2)

            def gate_split(n):
                wait(dve, sf_written, sf_at(n - 1, "W") + 1)
                dve.tensor_copy(wT[0:E, :], SF[0:E, :]).then_inc(wT_hi_made, 1)
                wait(dve, wT_hi_made, n + 1)
                dve.tensor_tensor(wT[32:32 + E, :], SF[0:E, :], wT[0:E, :].bitcast(F32), ALU.subtract)\
                    .then_inc(sf_read, 1)

            def lo(s, k):
                n = s * STEPS + k
                wait(dve, h_ready, n + 1)
                wait(dve, y_step, n + 1 - H_BUFS)
                if hi_on_vector(k):
                    dve.tensor_copy(h_hi[k % H_BUFS][:, :], h[k % H_BUFS][:, :]).then_inc(hi_ready, 1)
                    wait(dve, hi_ready, s * (STEPS - hi_before(STEPS)) + k - hi_before(k) + 1)
                dve.tensor_tensor(h_lo[k % H_BUFS][:, :], h[k % H_BUFS][:, :], h_hi[k % H_BUFS][:, :].bitcast(F32),
                                  ALU.subtract).then_inc(lo_ready, 1)

            def combine(s, q):
                wait(dve, y_step, s * STEPS + IT * (q + 1))
                if q == 0:
                    dve.tensor_scalar(acc[:, :], y[0][:, :], col("bs2"), None, ALU.add).then_inc(y_read, 1)
                    return
                wait(dve, sf_read, sf_at(s, f"b{q - 1}") + 1)
                wait(dve, acc_added, s * E + q - 2)
                dve.scalar_tensor_tensor(weighted[q % 2][:, :], y[q % Y_BANKS][:, :], col_of("bs2", q),
                                         w_bc[(q - 1) % 2][:, :], ALU.add, ALU.mult).then_inc(y_read, 1)

            def finish(s):
                wait(dve, accT_ready, s + 1)
                dve.scalar_tensor_tensor(xs(chunk_of(s)), y[1][:, :], 0.5, xs(chunk_of(s)), ALU.mult, ALU.add)\
                    .then_inc(y_read, 1)

            def split_lo(q):
                wait(dve, w_hi_made, 2 * q + 1)
                dve.tensor_tensor(w1_lo[:, q, :], w1_raw[:, q, :], w1_hi[:, q, :].bitcast(F32), ALU.subtract)\
                    .then_inc(w_split, 1)
                wait(dve, w_hi_made, 2 * q + 2)
                dve.tensor_tensor(w2_lo[:, q, :, :], w2_raw[:, q, :, :], w2_hi[:, q, :, :].bitcast(F32), ALU.subtract)\
                    .then_inc(w_split, 1)

            def setup_small():
                dve.wait_ge(sa_written, sa_setup("small") + 1)
                dve.tensor_copy(small[:, 0:S], SA[:, 0:S])
                dve.tensor_copy(w_xpT, SA[0:RK, S:S + P])
                dve.tensor_copy(w_bgT, SA[0:DS, S + P:S + 2 * P])
                dve.tensor_copy(w_cgT, SA[0:DS, S + 2 * P:S + 3 * P]).then_inc(sa_read, 1)

            def setup_ffn1():
                dve.wait_ge(sa_written, sa_setup("ffn1") + 1)
                dve.tensor_copy(ffnT[:, :, :], SA[:, :].rearrange("p (a b) -> p a b", a=4)).then_inc(sa_read, 1)

            def setup_products():
                dve.wait_ge(sa_written, sa_setup("products") + 1)
                dve.tensor_copy(prod[:, :, :], SA[:, :].rearrange("p (a b) -> p a b", a=4)).then_inc(sa_read, 1)

            def setup_scalars():
                dve.wait_ge(side_loaded, 16 * len(SIDE_LOADS))
                dve.tensor_scalar(one_mu[:, 0:1], col("mu_k"), -1.0, 1.0, ALU.mult, ALU.add)
                dve.tensor_scalar(one_mu[:, 1:2], col("mu_r"), -1.0, 1.0, ALU.mult, ALU.add)
                dve.tensor_tensor(amp2[:, :], amp[:, :], amp[:, :], ALU.mult)
                dve.tensor_tensor(pos_sq[:, :], pos[:, :], pos[:, :], ALU.mult).then_inc(dve_consts, 1)
                dve.wait_ge(dve_consts, 3)
                dve.tensor_reduce(nhalf_p2[:, :], pos_sq[:, :], AX.X, ALU.add).then_inc(dve_consts, 1)
                dve.wait_ge(dve_consts, 4)
                dve.tensor_scalar(nhalf_p2[:, :], nhalf_p2[:, :], -0.5, None, ALU.mult).then_inc(dve_consts, 1)

            SETUP_DVE = [(8, setup_small), (11, setup_ffn1), (14, setup_scalars), (17, setup_products)]

            def a_moments(j):
                wait_apart(dve, y_read, (Q + 1) * (j + 1))
                dve.wait_ge(w_split, 2 * Q)
                norm_stats(j, s_stat, s_mv, s_bn, s_stats, j)

            def a_norm(j):
                wait(dve, s_rstd_done, j + 1)
                norm_apply(j, a_xh2, s_mv, s_r2)
                norm_apply(j, a_xh1, s_mv, s_r1).then_inc(s_xh_done, 1)

            def a_affine(j):
                wait(dve, sa_written, sa_a(j, "T") + 1)
                dve.tensor_scalar(a_xnT[:, :], SA[:, :], col("gamma"), col("beta"), ALU.mult, ALU.add)\
                    .then_inc(sa_read, 1)

            def a_pad(j):
                wait(dve, sa_written, sa_a(j, "xb") + 1)
                dve.tensor_copy(xb_pad[:, :, 1:SEQ + 1], SA[:, :].rearrange("p (b s) -> p b s", b=SEQS))\
                    .then_inc(sa_read, 1)

            def a_conv_sides(j):
                c = a_c[:, :].rearrange("p (b s) -> p b s", b=SEQS)
                wait(dve, a_mid, j + 1)
                dve.scalar_tensor_tensor(c, xb_pad[:, :, 0:SEQ], col("conv_w", 0), c, ALU.mult, ALU.add)\
                    .then_inc(a_conv, 1)
                wait(dve, a_conv, 2 * j + 1)
                dve.scalar_tensor_tensor(c, xb_pad[:, :, 2:SEQ + 2], col("conv_w", 2), c, ALU.mult, ALU.add)\
                    .then_inc(a_conv, 1)

            def a_dt(j):
                wait(dve, sa_written, sa_a(j, "dt") + 1)
                dve.tensor_scalar(a_u[:, :], SA[:, :], col("b_dt"), None, ALU.add).then_inc(sa_read, 1)

            def a_times_B(j):
                wait(dve, sa_written, sa_a(j, "B") + 1)
                wait(dve, a_delta, j + 1)
                dve.tensor_tensor(a_dB[:, :], SA[:, :], a_dl[:, :], ALU.mult).then_inc(sa_read, 1)

            def a_recurrence(j):
                wait(dve, a_drive, j + 1)
                wait(dve, a_decay, j + 1)
                for b in range(SEQS):
                    last = dve.tensor_tensor_scan(a_h[:, b * SEQ:(b + 1) * SEQ], a_dA[:, b * SEQ:(b + 1) * SEQ],
                                                  a_dB[:, b * SEQ:(b + 1) * SEQ], 0.0, ALU.mult, ALU.add)
                last.then_inc(a_scan, 1)

            def a_times_C(j):
                wait(dve, sa_written, sa_a(j, "C") + 1)
                wait(dve, a_scan, j + 1)
                dve.tensor_tensor(a_h[:, :], SA[:, :], a_h[:, :], ALU.mult).then_inc(sa_read, 1)
                wait(dve, sa_read, sa_a(j, "C") + 1)
                dve.scalar_tensor_tensor(a_h[:, :], a_xact[:, :], col("D"), a_h[:, :], ALU.mult, ALU.add)\
                    .then_inc(a_y, 1)

            def a_add(j):
                wait(dve, sa_written, sa_a(j, "out") + 1)
                wait(dve, a_res, j + 1)
                dve.tensor_tensor(xs(j), SA[:, :], xs(j), ALU.add).then_inc(sa_read, 1)

            A_DVE = [(4, a_moments), (6, a_norm), (9, a_affine), (12, a_pad), (15, a_conv_sides), (20, a_dt),
                     (25, a_times_B), (28, a_recurrence), (30, a_times_C), (35, a_add)]

            def t_moments(j, o, before):
                before(j)
                norm_stats(j, s_stat, s_mv, s_bn, s_stats, N_CHUNK + j * 3 + o)

            def t_norm(j, o, dst):
                wait(dve, s_rstd_done, N_CHUNK + j * 3 + o + 1)
                norm_apply(j, dst, s_mv, s_r1).then_inc(s_xh_done, 1)

            def r_first(j):
                wait_apart(dve, y_read, (Q + 1) * (j + N_CHUNK + 1))
                wait(dve, sa_read, SA_T0)

            def r_mix(o2):
                def work(j):
                    now = xT_pad[:, :, 1:SEQ + 1]
                    for n, (t, dst, mu) in enumerate(((r_tk, r_xk, "mu_k"), (r_tr, r_xr, "mu_r"))):
                        wait(dve, r_prev, 4 * j + 2 * o2 + n + 1)
                        dve.scalar_tensor_tensor(dst[:, :].rearrange("p (b s) -> p b s", b=SEQS), now, col(mu),
                                                 t[:, :].rearrange("p (b s) -> p b s", b=SEQS), ALU.mult, ALU.add)\
                            .then_inc(r_mixed, 1)
                return work

            def r_out(o2):
                def work(j):
                    wait(dve, sa_written, sa_r(j, o2, "v") + 1)
                    wait(dve, sa_read, sa_r(j, o2, "r") + 1)
                    dve.tensor_tensor(r_t[:, :], SA[:, :], r_rr[:, :], ALU.mult).then_inc(sa_read, 1)
                    wait(dve, sa_read, sa_r(j, o2, "v") + 1)
                    dve.scalar_tensor_tensor(xs(j), r_t[:, :], 0.5, xs(j), ALU.mult, ALU.add).then_inc(r_done, 1)
                return work

            def l_distance(j):
                wait(dve, sa_written, sa_l(j, "xp") + 1)
                dve.tensor_scalar(l_dd[0:S, :], SA[0:S, :], nhalf_p2[:, :], 0.0, ALU.add, ALU.min)\
                    .then_inc(sa_read, 1)

            def l_evac_M(j):
                wait(dve, sa_written, sa_l(j, "MT") + 1)
                dve.tensor_copy(l_MT[:, 0:SEQS * S], SA[:, 0:SEQS * S]).then_inc(sa_read, 1)
                wait(dve, l_exp, 2 * j + 2)
                dve.tensor_scalar(gsum2[:, :], gsum[:, :], amp2[:, :], None, ALU.mult).then_inc(l_gs, 1)

            def l_evac_B(j):
                wait(dve, sa_written, sa_l(j, "B") + 1)
                dve.tensor_scalar(l_R2[0:S, 0:SEQS * P], SA[0:S, 0:SEQS * P], amp2[:, :], None, ALU.mult)\
                    .then_inc(sa_read, 1)

            def l_sums(j):
                wait(dve, sa_written, sa_l(j, "sum") + 1)
                dve.tensor_scalar(den[:, :], SA[:, 0:TILES], EPS_ATTN, None, ALU.add).then_inc(sa_read, 1)
                wait(dve, sa_read, sa_l(j, "sum") + 1)
                dve.reciprocal(rden[:, :], den[:, :]).then_inc(l_rec, 1)

            def l_out(j):
                wait(dve, sa_written, sa_l(j, "out") + 1)
                wait(dve, l_rec, j + 1)
                for t in range(TILES):
                    last = dve.scalar_tensor_tensor(xs(j, t), tile(SA, t), rden[:, t:t + 1], xs(j, t),
                                                    ALU.mult, ALU.add)
                last.then_inc(sa_read, 1)

            T_DVE = [(4, lambda j: t_moments(j, 0, r_first)), (6, lambda j: t_norm(j, 0, r_xh)), (9, r_mix(0)),
                     (14, r_out(0)),
                     (15, lambda j: t_moments(j, 1, lambda j: wait_apart(dve, r_done, 2 * j + 1))),
                     (16, lambda j: t_norm(j, 1, l_xh)), (19, l_distance), (23, l_evac_M), (24, l_evac_B),
                     (25, l_sums), (26, l_out),
                     (27, lambda j: t_moments(j, 2, lambda j: wait_apart(dve, sa_read, sa_l(j, "out") + 1))),
                     (28, lambda j: t_norm(j, 2, r_xh)), (31, r_mix(1)), (35, r_out(1))]

            def slot(s, prep, side):
                first = isinstance(s, int) and s == 0
                for k in range(STEPS):
                    lo(s, k)
                    if k == 1 and not first:
                        combine(s - 1, E)
                    if k == 3 and not first:
                        finish(s - 1)
                    if k % IT == 1 and 1 <= k // IT:
                        combine(s, k // IT - 1)
                    if first and k % IT == 3 and k // IT + 2 < Q:
                        split_lo(k // IT + 2)
                    if prep:
                        if k == 7:
                            if first:
                                for c in range(1, N_CHUNK):
                                    dve.wait_ge(x_loaded[c], 16)
                            elif side == "A":
                                wait_apart(dve, sa_read, sa_a(s - 1, "T"))
                            else:
                                wait(dve, sa_read, SA_T0)
                            f_moments(s + 1)
                        if k == 9:
                            f_norm(s + 1)
                        if k == 13:
                            f_split(s + 1)
                        if k == 20:
                            gate_logits(s + 1)
                        if k == 22:
                            gate_top(s + 1)
                        if k == 26:
                            gate_weights(s + 1)
                        if k == 34:
                            gate_split(s + 1)
                    if first:
                        at_step(SETUP_DVE, k)
                    if side == "A":
                        at_step(A_DVE, k, s - 1)
                    if side == "T":
                        at_step(T_DVE, k, s - (N_CHUNK + 1))

            dve.wait_ge(x_loaded[0], 16)
            f_moments(0)
            f_norm(0)
            dve.wait_ge(consts_made, 13)
            dve.tensor_copy(expert_no[:, :], expert_no_i[:, :])
            dve.tensor_copy(sel[:, :, :], sel_raw[:, :, :])
            dve.tensor_copy(wT[:, :], zero_row[:, :]).then_inc(dve_consts, 1)
            f_split(0)
            dve.wait_ge(sa_written, sa_setup("cols") + 1)
            dve.tensor_copy(cols[:, :], SA[:, 0:ROWS]).then_inc(sa_read, 1)
            dve.wait_ge(router_hi, 1)
            dve.tensor_tensor(wr1_lo[:, :], wr1_raw[:, :], wr1_hi[:, :].bitcast(F32), ALU.subtract)\
                .then_inc(router_split, 1)
            dve.wait_ge(dve_consts, 1)
            split_lo(0)
            gate_logits(0)
            gate_top(0)
            gate_weights(0)
            gate_split(0)
            split_lo(1)
            dve.tensor_copy(lg_max[:, 0:1], ident[:, 0:1]).then_inc(dve_consts, 1)
            slot(0, True, None)
            with dve.Fori(1, N_CHUNK + 1) as s:
                slot(s, True, "A")
            with dve.Fori(N_CHUNK + 1, N_SLOT - 1) as s:
                slot(s, True, "T")
            slot(N_SLOT - 1, False, "T")
            combine(N_SLOT - 1, E)
            finish(N_SLOT - 1)
            for _, work in T_DVE:
                work(N_CHUNK - 1)

        @block.tensor
        def _(pe):
            def parity(s):
                return s % 2 if isinstance(s, int) else s & 1

            def three(dst, w_hi, w_lo, m_hi, m_lo, start, stop):
                pe.matmul(dst, w_hi, m_hi, start=start, stop=False)
                pe.matmul(dst, w_hi, m_lo, start=False, stop=False)
                return pe.matmul(dst, w_lo, m_hi, start=False, stop=stop)

            def z_tile(s, k):
                q, i = divmod(k, IT)
                if k == 0:
                    wait(pe, sf_read, prepared(s))
                if isinstance(s, int) and s == 0 and i == 0:
                    pe.wait_ge(w_split, 2 * q + 1)
                wait(pe, h_ready, s * STEPS + k + 1 - Z_BANKS)
                par = parity(s)
                three(z[k % Z_BANKS][:, :], w1_hi[:, q, i * P:(i + 1) * P], w1_lo[:, q, i * P:(i + 1) * P],
                      xT_hi[:, par, :], xT_lo[:, par, :], True, True).then_inc(z_ready, 1)

            def y_tile(s, k):
                q, i = divmod(k, IT)
                if isinstance(s, int) and s == 0 and i == 0:
                    pe.wait_ge(w_split, 2 * q + 2)
                if i == 0:
                    wait(pe, y_read, s * (Q + 1) + q + 1 - Y_BANKS)
                wait(pe, lo_ready, s * STEPS + k + 1)
                three(y[q % Y_BANKS][:, :], w2_hi[:, q, i, :], w2_lo[:, q, i, :],
                      h_hi[k % H_BUFS][:, :], h_lo[k % H_BUFS][:, :], i == 0, i == IT - 1).then_inc(y_step, 1)

            def turn_acc(s):
                wait(pe, acc_added, E * (s + 1))
                wait(pe, y_read, s * (Q + 1) + Q - 1)
                for t in range(TILES):
                    last = pe.transpose(tile(y[1], t), tile(acc, t), ident[:, :])
                last.then_inc(accT_ready, 1)

            def use_sf(s, use):
                wait(pe, sf_read, sf_at(s, use))

            def bc(s, q):
                use_sf(s, f"b{q}")
                pe.matmul(SF[:, :], sel[:, q, :], wT[:, :], start=True, stop=True).then_inc(sf_written, 1)

            def f_turn(n):
                use_sf(n - 1, "T")
                wait(pe, f_xh_done, n + 1)
                for t in range(TILES):
                    last = pe.transpose(tile(SF, t), tile(f_xh, t), ident[:, :])
                last.then_inc(sf_written, 1)

            def f_router(n):
                use_sf(n - 1, "R")
                par = parity(n)
                three(SF[:, :], wr1_hi[:, :], wr1_lo[:, :], xT_hi[:, par, :], xT_lo[:, par, :], True, True)\
                    .then_inc(sf_written, 1)

            def f_logits(n):
                use_sf(n - 1, "L")
                for t in range(TILES):
                    last = pe.matmul(SF[:, t * E:(t + 1) * E], tile(r1, t), wr2[:, :], start=True, stop=True)
                last.then_inc(sf_written, 1)

            def f_turn_w(n):
                use_sf(n - 1, "W")
                wait(pe, gate_w, n + 1)
                for t in range(TILES):
                    last = pe.transpose(SF[0:E, t * P:(t + 1) * P], w_tok[:, t, :], ident[:, :])
                last.then_inc(sf_written, 1)

            def turn_cols():
                pe.wait_ge(rows_loaded, 16 * len(row_loads))
                pe.transpose(SA[:, 0:ROWS], rows[:, :], ident[0:ROWS, 0:ROWS]).then_inc(sa_written, 1)

            def turn_small():
                pe.wait_ge(side_loaded, 16 * len(SIDE_LOADS))
                pe.wait_ge(sa_read, sa_setup("small"))
                pe.transpose(SA[:, 0:S], pos[:, :], ident[0:S, 0:S])
                pe.transpose(SA[0:RK, S:S + P], w_xp[:, :], ident[:, :])
                pe.transpose(SA[0:DS, S + P:S + 2 * P], w_bg[:, :], ident[:, :])
                pe.transpose(SA[0:DS, S + 2 * P:S + 3 * P], w_cg[:, :], ident[:, :]).then_inc(sa_written, 1)

            def turn_ffn1():
                pe.wait_ge(sa_read, sa_setup("ffn1"))
                for n in range(4):
                    last = pe.transpose(tile(SA, n), ffn_raw[:, n, :], ident[:, :])
                last.then_inc(sa_written, 1)

            def make_products():
                pe.wait_ge(sa_read, sa_setup("products"))
                for n, (wT_, w_) in enumerate(((w_xpT, w_dt[:, :]), (w_bgT, w_bp[:, :]), (w_cgT, w_cp[:, :]),
                                               (ffnT[:, 3, :], wo[:, :]))):
                    last = pe.matmul(tile(SA, n), wT_, w_, start=True, stop=True)
                last.then_inc(sa_written, 1)

            SETUP_PE = [(6, turn_small), (9, turn_ffn1), (13, make_products)]

            def a_turn(j):
                wait(pe, sa_read, sa_a(j, "T"))
                wait(pe, s_xh_done, j + 1)
                for t in range(TILES):
                    last = pe.transpose(tile(SA, t), tile(a_xh2, t), ident[:, :])
                last.then_inc(sa_written, 1)

            def a_project(use, w, src):
                def work(j):
                    wait(pe, sa_read, sa_a(j, use))
                    if use == "dt":
                        wait(pe, a_act, j + 1)
                    pe.matmul(SA[:, :], w, src[:, :], start=True, stop=True).then_inc(sa_written, 1)
                return work

            def a_output(j):
                wait(pe, a_gated, j + 1)
                wait(pe, sa_read, sa_a(j, "out"))
                for t in range(TILES):
                    last = pe.matmul(tile(SA, t), tile(a_h, t), w_out[:, :], start=True, stop=True)
                last.then_inc(sa_written, 1)

            A_PE = [(7, a_turn), (10, a_project("xb", w_in[:, 0:C], a_xnT)),
                    (14, a_project("z", w_in[:, C:2 * C], a_xnT)),
                    (18, a_project("dt", prod[:, 0, :], a_xact)), (22, a_project("B", prod[:, 1, :], a_xact)),
                    (26, a_project("C", prod[:, 2, :], a_xact)), (32, a_output)]

            def t_turn(src, at_use, o):
                def work(j):
                    wait(pe, sa_read, at_use(j))
                    wait(pe, s_xh_done, N_CHUNK + j * 3 + o + 1)
                    for t in range(TILES):
                        last = pe.transpose(tile(SA, t), tile(src, t), ident[:, :])
                    last.then_inc(sa_written, 1)
                return work

            def r_key(o2):
                def work(j):
                    wait(pe, sa_read, sa_r(j, o2, "k"))
                    wait(pe, r_mixed, 4 * j + 2 * o2 + 1)
                    pe.matmul(SA[:, :], ffnT[:, 0, :], r_xk[:, :], start=True, stop=True).then_inc(sa_written, 1)
                return work

            def r_receptance(o2):
                def work(j):
                    wait(pe, sa_read, sa_r(j, o2, "r"))
                    wait(pe, r_mixed, 4 * j + 2 * o2 + 2)
                    for t in range(TILES):
                        last = pe.matmul(tile(SA, t), tile(r_xr, t), ffnT[:, 1, :], start=True, stop=True)
                    last.then_inc(sa_written, 1)
                return work

            def r_value(o2):
                def work(j):
                    wait(pe, sa_read, sa_r(j, o2, "v"))
                    wait(pe, r_sq, 2 * j + o2 + 1)
                    for t in range(TILES):
                        last = pe.matmul(tile(SA, t), tile(r_ka, t), ffnT[:, 2, :], start=True, stop=True)
                    last.then_inc(sa_written, 1)
                return work

            def l_products(j):
                wait(pe, sa_read, sa_l(j, "xp"))
                pe.matmul(SA[0:S, :], pT, l_xT[:, :], start=True, stop=False)
                wait(pe, l_sq_done, j + 1)
                pe.matmul(SA[0:S, :], nhalf[:, :], l_sq[:, :], start=False, stop=True).then_inc(sa_written, 1)

            def l_turn_E(j):
                wait(pe, sa_read, sa_l(j, "Et"))
                wait_apart(pe, l_exp, 2 * j + 2)
                for t in range(TILES):
                    last = pe.transpose(SA[:, t * S:(t + 1) * S], l_E[0:S, t * P:(t + 1) * P], ident[0:S, 0:S])
                last.then_inc(sa_written, 1)

            def l_moment(j):
                wait(pe, sa_read, sa_l(j, "MT"))
                for t in range(TILES):
                    b, i = divmod(t, SEQ // P)
                    last = pe.matmul(SA[:, b * S:(b + 1) * S], tile(l_xh, t), l_Et[:, t * S:(t + 1) * S],
                                     start=(i == 0), stop=(i == SEQ // P - 1))
                last.then_inc(sa_written, 1)

            def l_values(j):
                wait(pe, sa_read, sa_l(j, "B"))
                for b in range(SEQS):
                    last = pe.matmul(SA[0:S, b * P:(b + 1) * P], l_MT[:, b * S:(b + 1) * S], prod[:, 3, :],
                                     start=True, stop=True)
                last.then_inc(sa_written, 1)

            def l_row_sums(j):
                wait(pe, sa_read, sa_l(j, "sum"))
                wait(pe, l_gs, j + 1)
                for t in range(TILES):
                    b = t // (SEQ // P)
                    last = pe.matmul(SA[:, t:t + 1], l_E[0:S, t * P:(t + 1) * P], gsum2[:, b:b + 1],
                                     start=True, stop=True)
                last.then_inc(sa_written, 1)

            def l_output(j):
                wait(pe, sa_read, sa_l(j, "out"))
                for t in range(TILES):
                    b = t // (SEQ // P)
                    last = pe.matmul(tile(SA, t), l_E[0:S, t * P:(t + 1) * P], l_R2[0:S, b * P:(b + 1) * P],
                                     start=True, stop=True)
                last.then_inc(sa_written, 1)

            T_PE = [(6, t_turn(r_xh, lambda j: sa_r(j, 0, "T"), 0)), (9, r_key(0)), (10, r_receptance(0)),
                    (12, r_value(0)),
                    (16, t_turn(l_xh, lambda j: sa_l(j, "T"), 1)), (18, l_products), (20, l_turn_E), (22, l_moment),
                    (23, l_values), (24, l_row_sums), (25, l_output),
                    (28, t_turn(r_xh, lambda j: sa_r(j, 1, "T"), 2)), (31, r_key(1)), (32, r_receptance(1)),
                    (34, r_value(1))]

            def slot(s, prep, side, more):
                first = isinstance(s, int) and s == 0
                for k in range(STEPS):
                    if k + LOOKAHEAD < STEPS:
                        z_tile(s, k + LOOKAHEAD)
                    elif more:
                        z_tile(s + 1, k + LOOKAHEAD - STEPS)
                    y_tile(s, k)
                    if k == 2 and not first:
                        turn_acc(s - 1)
                    if k % IT == 1 and k // IT < E:
                        bc(s, k // IT)
                    if prep:
                        if k == 11:
                            f_turn(s + 1)
                        if k == 15:
                            f_router(s + 1)
                        if k == 19:
                            f_logits(s + 1)
                        if k == 32:
                            f_turn_w(s + 1)
                    if first:
                        at_step(SETUP_PE, k)
                    if side == "A":
                        at_step(A_PE, k, s - 1)
                    if side == "T":
                        at_step(T_PE, k, s - (N_CHUNK + 1))

            pe.wait_ge(consts_made, 5)
            f_turn(0)
            turn_cols()
            pe.wait_ge(router_split, 1)
            f_router(0)
            for k in range(LOOKAHEAD):
                z_tile(0, k)
            f_logits(0)
            pe.wait_ge(dve_consts, 1)
            f_turn_w(0)
            slot(0, True, None, True)
            with pe.Fori(1, N_CHUNK + 1) as s:
                slot(s, True, "A", True)
            with pe.Fori(N_CHUNK + 1, N_SLOT - 1) as s:
                slot(s, True, "T", True)
            slot(N_SLOT - 1, False, "T", False)
            turn_acc(N_SLOT - 1)
            for _, work in T_PE:
                work(N_CHUNK - 1)


_INS = [
    "L0_attn_x", "L0_attn_gamma", "L0_attn_beta", "L0_attn_W_in", "L0_attn_conv_w", "L0_attn_conv_b",
    "L0_attn_W_xp", "L0_attn_W_Bg", "L0_attn_W_Cg", "L0_attn_W_dt", "L0_attn_b_dt", "L0_attn_W_Bp",
    "L0_attn_W_Cp", "L0_attn_A", "L0_attn_D_skip", "L0_attn_W_out", "L0_ffn_Wr1", "L0_ffn_br1", "L0_ffn_Wr2",
    "L0_ffn_br2", "L0_ffn_Ws1", "L0_ffn_bs1", "L0_ffn_Ws2", "L0_ffn_bs2", "L0_ffn_We1", "L0_ffn_be1",
    "L0_ffn_We2", "L0_ffn_be2", "L1_attn_splat_positions", "L1_attn_splat_log_scales",
    "L1_attn_splat_amplitudes", "L1_attn_Wv", "L1_attn_Wo", "L1_ffn_W_r", "L1_ffn_W_k", "L1_ffn_W_v",
    "L1_ffn_mu_r", "L1_ffn_mu_k",
]


def kernel(**inputs):
    import numpy as _np
    import concourse.bacc as _bacc
    from concourse import mybir as _mybir
    from concourse.bass_utils import run_bass_kernel_spmd as _run

    nc = _bacc.Bacc("TRN2", target_bir_lowering=False, num_devices=1)
    arrays, aps = {}, {}
    for name in _INS:
        a = _np.ascontiguousarray(inputs[name])
        arrays[f"in_{name}_dram"] = a
        aps[name] = nc.dram_tensor(f"in_{name}_dram", a.shape, _mybir.dt.from_np(a.dtype),
                                   kind="ExternalInput").ap()
    x = arrays["in_L0_attn_x_dram"]
    out = nc.dram_tensor("out_0_dram", x.shape, _mybir.dt.from_np(x.dtype), kind="ExternalOutput").ap()
    macaron_kernel(nc, aps, out)
    r = _run(nc, [arrays], core_ids=[0])
    return r.results[0]["out_0_dram"]
```

```python
import math
from contextlib import ExitStack

import concourse.bass as bass
from concourse import mybir

ALU = mybir.AluOpType
ACT = mybir.ActivationFunctionType
AX = mybir.AxisListType
F32 = mybir.dt.float32
F32R = mybir.dt.float32r
U32 = mybir.dt.uint32

P = 128
CHUNK = 512
TILES = CHUNK // P
SEQ = 256
SEQS = CHUNK // SEQ
EPS = 1e-5
EPS_ATTN = 1e-8
LOOKAHEAD = 3
Z_BANKS = 4
H_BUFS = 4
Y_BANKS = 2


def hi_on_vector(k):
    return k % 3 == 1


def hi_before(k):
    return sum(not hi_on_vector(i) for i in range(k))


SF_PREP = ["T", "R", "L", "W"]
SF_LAST = [f"b{q}" for q in range(8)]
SA_SETUP = ["biases", "cols", "small", "ffn1", "products"]
SA_A = ["T", "xb", "z", "dt", "B", "C", "out"]
SA_R = ["T", "k", "r", "v"]
SA_L = ["T", "xp", "Et", "MT", "B", "sum", "out"]


STEP = {
    "pool a_rstd": 8,
    "pool a_residual": 8,
    "pool a_conv_mid": 8,
    "pool a_drive_x": 24,
    "pool a_gate": 29,
    "pool t_rstd0": 3,
    "pool r_shift0": 5,
    "pool r_square0": 6,
    "pool t_rstd1": 10,
    "pool l_square": 15,
    "pool t_rstd2": 25,
    "pool r_shift1": 25,
    "pool r_square1": 28,
    "act a_silu_z": 20,
    "act a_silu_x": 22,
    "act a_softplus": 24,
    "act r_evac0": 8,
    "act r_relu0": 11,
    "act r_sigmoid0": 13,
    "act l_evac": 18,
    "act l_gauss": 20,
    "act l_evac_E": 21,
    "act r_evac1": 30,
    "act r_relu1": 34,
    "act r_sigmoid1": 35,
    "dve setup_cols": 4,
    "dve setup_small": 7,
    "dve setup_ffn1": 15,
    "dve setup_scalars": 15,
    "dve setup_products": 17,
    "dve a_moments": 6,
    "dve a_norm": 12,
    "dve a_affine": 13,
    "dve a_pad": 16,
    "dve a_conv_sides": 18,
    "dve a_dt": 21,
    "dve a_delta_sum": 23,
    "dve a_times_B": 27,
    "dve a_recurrence": 29,
    "dve a_times_C": 30,
    "dve a_add": 34,
    "dve t_moments0": 4,
    "dve t_norm0": 6,
    "dve r_mix0": 9,
    "dve r_out0": 14,
    "dve t_moments1": 14,
    "dve t_norm1": 16,
    "dve l_distance": 19,
    "dve l_evac_M": 21,
    "dve l_evac_B": 23,
    "dve l_sums": 25,
    "dve l_out": 27,
    "dve t_moments2": 27,
    "dve t_norm2": 28,
    "dve r_mix1": 31,
    "dve r_out1": 35,
    "pe turn_cols": 0,
    "pe turn_small": 6,
    "pe turn_ffn1": 10,
    "pe make_products": 16,
    "pe a_turn": 12,
    "pe a_xb": 14,
    "pe a_z": 15,
    "pe a_dt": 21,
    "pe a_B": 21,
    "pe a_C": 28,
    "pe a_output": 32,
    "pe t_turn0": 6,
    "pe r_key0": 9,
    "pe r_receptance0": 10,
    "pe r_value0": 12,
    "pe t_turn1": 16,
    "pe l_products": 17,
    "pe l_turn_E": 20,
    "pe l_moment": 21,
    "pe l_values": 22,
    "pe l_row_sums": 23,
    "pe l_output": 25,
    "pe t_turn2": 28,
    "pe r_key1": 31,
    "pe r_receptance1": 32,
    "pe r_value1": 33,
    "pool f_rstd": [6, 1, 6],
    "pool gate_exponent": [19, 14, 17],
    "pool gate_ratio": [24, 19, 19],
    "act router_relu": [19, 19, 16],
    "act spread": 3,
    "act spread0": 6,
    "act setup_scales": 33,
    "pe f_turn_w0": 4,
    "dve gate_top0": 2,
    "dve gate_weights0": 3,
    "dve gate_split0": 4,
    "dve f_moments": [0, 7, 7],
    "dve f_norm": [9, 9, 10],
    "dve f_split": [10, 13, 14],
    "dve gate_logits": [18, 19, 20],
    "dve gate_top": [22, 24, 26],
    "dve gate_weights": [25, 27, 29],
    "dve gate_split": [33, 35, 35],
    "pe f_turn": [10, 11, 12],
    "pe f_router": [16, 16, 14],
    "pe f_logits": [17, 18, 20],
    "pe f_turn_w": [30, 30, 32],
    "pe bc": 1,
    "pe turn_acc": 2,
    "dve finish": 3,
}


def sf_order(phase):
    uses = [(4 * q + STEP["pe bc"], 0, f"b{q}") for q in range(8)]
    uses += [(STEP[name][phase], 1, use) for name, use in (
        ("pe f_turn", "T"), ("pe f_router", "R"), ("pe f_logits", "L"), ("pe f_turn_w", "W"))]
    return [use for _, _, use in sorted(uses)]


def macaron_kernel(nc, d, out):
    x_in = d["L0_attn_x"]
    C = x_in.shape[2]
    N_TOK = x_in.shape[0] * x_in.shape[1]
    N_CHUNK = N_TOK // CHUNK
    E, _, I = d["L0_ffn_We1"].shape
    RH = d["L0_ffn_Wr1"].shape[1]
    Q = E + 1
    IT = I // P
    STEPS = Q * IT
    N_SLOT = 2 * N_CHUNK
    RK, DS = d["L0_attn_W_dt"].shape[0], d["L0_attn_W_Bp"].shape[0]
    S = d["L1_attn_splat_positions"].shape[0]
    assert C == P and x_in.shape[1] == SEQ and E == 8 and STEPS % Z_BANKS == 0 and STEPS % H_BUFS == 0

    with ExitStack() as ctx:
        def sb(name, shape, dt=F32):
            return ctx.enter_context(nc.sbuf_tensor(name, shape, dt))

        def sem(name):
            return ctx.enter_context(nc.semaphore(name))

        def bank(name):
            return ctx.enter_context(nc.psum_tensor(name, [P, CHUNK], F32))

        x = sb("x_res", [P, N_TOK])
        w1_raw = sb("w1_raw", [P, Q, I])
        w2_raw = sb("w2_raw", [P, Q, IT, C])
        w1_hi, w1_lo = sb("w1_hi", [P, Q, I], F32R), sb("w1_lo", [P, Q, I], F32R)
        w2_hi, w2_lo = sb("w2_hi", [P, Q, IT, C], F32R), sb("w2_lo", [P, Q, IT, C], F32R)
        ident = sb("ident", [P, P])
        f_stat, f_mv, f_rstd = sb("f_stat", [P, TILES, 6]), sb("f_mv", [P, TILES, 2]), sb("f_rstd", [P, TILES])
        f_xh = sb("f_xh", [P, CHUNK])
        xT_hi, xT_lo = sb("xT_hi", [P, 2, CHUNK], F32R), sb("xT_lo", [P, 2, CHUNK], F32R)
        h = [sb(f"h{i}", [P, CHUNK]) for i in range(H_BUFS)]
        h_hi = [sb(f"h_hi{i}", [P, CHUNK], F32R) for i in range(H_BUFS)]
        h_lo = [sb(f"h_lo{i}", [P, CHUNK], F32R) for i in range(H_BUFS)]
        acc = sb("acc", [P, CHUNK])
        weighted = [sb(f"weighted{i}", [P, CHUNK]) for i in range(2)]
        w_bc = [sb(f"w_bc{i}", [P, CHUNK]) for i in range(2)]
        wr1_raw = sb("wr1_raw", [P, P])
        wr1_hi, wr1_lo = sb("wr1_hi", [P, P], F32R), sb("wr1_lo", [P, P], F32R)
        wr2 = sb("wr2", [RH + 1, E])
        br1 = sb("br1", [RH, 1])
        r1 = sb("r1", [RH + 1, CHUNK])
        base_e, base_root_e = sb("base_e", [P, TILES, E]), sb("base_root_e", [P, TILES])
        lg_max, ex = sb("lg_max", [P, TILES]), sb("ex", [P, TILES, E])
        lg = sb("lg", [P, TILES, E])
        ex_sum, ex_rec = sb("ex_sum", [P, TILES]), sb("ex_rec", [P, TILES])
        gates, top = sb("gates", [P, TILES, E]), sb("top", [P, TILES, 8])
        top_at, top_atf = sb("top_at", [P, TILES, 8], U32), sb("top_atf", [P, TILES, 2])
        diff, ratio, ratio1 = sb("diff", [P, TILES]), sb("ratio", [P, TILES]), sb("ratio1", [P, TILES])
        tw = sb("tw", [P, TILES, 2])
        expert_no_i, expert_no = sb("expert_no_i", [P, E], mybir.dt.int32), sb("expert_no", [P, E])
        pick = [sb(f"pick{i}", [P, TILES, E]) for i in range(2)]
        pickw = [sb(f"pickw{i}", [P, TILES, E]) for i in range(2)]
        w_tok = sb("w_tok", [P, TILES, E])
        wT = sb("wT", [40, CHUNK], F32R)
        sel = sb("sel", [40, E, P], F32R)
        sel_raw = sb("sel_raw", [40, E, P])
        zero_row = sb("zero_row", [40, CHUNK])
        ROWS = IT * Q + Q + 11
        bias_rows, rows = sb("bias_rows", [IT * Q, P]), sb("rows", [ROWS - IT * Q, P])
        cols = sb("cols", [P, ROWS])
        w_in = sb("w_in", [P, 2 * C])
        w_xp, w_bg, w_cg = sb("w_xp", [P, RK]), sb("w_bg", [P, DS]), sb("w_cg", [P, DS])
        w_dt, w_bp, w_cp = sb("w_dt", [RK, C]), sb("w_bp", [DS, C]), sb("w_cp", [DS, C])
        w_out = sb("w_out", [P, C])
        small = sb("small", [P, S + 3 * P])
        pT = small[:, 0:S]
        w_xpT, w_bgT, w_cgT = small[0:RK, S:S + P], small[0:DS, S + P:S + 2 * P], small[0:DS, S + 2 * P:S + 3 * P]
        ffn_raw = sb("ffn_raw", [P, 4, P])
        ffnT = sb("ffnT", [P, 4, P])
        wo = sb("wo", [P, P])
        prod = sb("prod", [P, 4, P])
        pos = sb("pos", [S, P])
        pos_sq = sb("pos_sq", [S, P])
        nhalf_p2, logs, amp = sb("nhalf_p2", [S, 1]), sb("logs", [S, 1]), sb("amp", [S, 1])
        amp2, inv_s2 = sb("amp2", [S, 1]), sb("inv_s2", [S, 1])
        one_mu = sb("one_mu", [P, 2])
        nhalf = sb("nhalf", [P, S])
        mhalf_exp = sb("mhalf_exp", [P, TILES])
        s_stat, s_mv = sb("s_stat", [P, TILES, 6]), sb("s_mv", [P, TILES, 2])
        s_r1, s_r2, s_v2 = sb("s_r1", [P, TILES]), sb("s_r2", [P, TILES]), sb("s_v2", [P, TILES])
        assert I == CHUNK
        side = [w1_raw[:, q, :] for q in range(Q)] + [sb(f"side{i}", [P, CHUNK])[:, :] for i in range(3)]
        xb_pad = sb("xb_pad", [P, SEQS, SEQ + 2])
        xT_pad = sb("xT_pad", [P, SEQS, SEQ + 1])
        a_xh1, a_xh2, a_xnT, a_c, a_xact, a_sz, a_u, a_l, a_dl, a_dA, a_dB, a_h = side
        r_xh, r_tk, r_tr, r_xk, r_xr, r_rk, r_ka, r_rr, r_t = side[0:9]
        l_xh, l_xT, l_sq, l_dd, l_E, l_Et, l_MT, l_R2 = side[1:9]
        gsum, gsum2 = sb("gsum", [S, SEQS]), sb("gsum2", [S, SEQS])
        den, rden = sb("den", [P, TILES]), sb("rden", [P, TILES])

        z = [bank(f"z{i}") for i in range(Z_BANKS)]
        y = [bank(f"y{i}") for i in range(Y_BANKS)]
        SF, SA = bank("SF"), bank("SA")

        at = {}
        row_loads = []
        r0 = 0
        for name, view, n in [
            ("bs1", d["L0_ffn_bs1"].rearrange("(a b) -> a b", b=P), IT),
            ("be1", d["L0_ffn_be1"].rearrange("e (a b) -> (e a) b", b=P), E * IT),
            ("bs2", d["L0_ffn_bs2"].rearrange("(a b) -> a b", b=P), 1),
            ("be2", d["L0_ffn_be2"], E),
            ("conv_w", d["L0_attn_conv_w"].rearrange("k a c -> (k a) c"), 3),
            ("gamma", d["L0_attn_gamma"].rearrange("(a b) -> a b", b=P), 1),
            ("beta", d["L0_attn_beta"].rearrange("(a b) -> a b", b=P), 1),
            ("conv_b", d["L0_attn_conv_b"].rearrange("(a b) -> a b", b=P), 1),
            ("b_dt", d["L0_attn_b_dt"].rearrange("(a b) -> a b", b=P), 1),
            ("A", d["L0_attn_A"].rearrange("(a b) -> a b", b=P), 1),
            ("D", d["L0_attn_D_skip"].rearrange("(a b) -> a b", b=P), 1),
            ("mu_k", d["L1_ffn_mu_k"].rearrange("(a b) -> a b", b=P), 1),
            ("mu_r", d["L1_ffn_mu_r"].rearrange("(a b) -> a b", b=P), 1),
        ]:
            at[name] = r0
            row_loads.append((r0, n, view))
            r0 += n
        assert r0 == ROWS

        def col(name, i=0):
            return cols[:, at[name] + i:at[name] + i + 1]

        def col_of(name, k):
            return cols[:, at[name] + k:at[name] + k + 1]

        x_loaded, x_rest_loaded = sem("x_loaded"), sem("x_rest_loaded")
        LOTS = [0, 1, 2, 3, 4, 6, Q]
        w_loaded = {q: sem(f"w_loaded{q}") for q in LOTS[:-1]}
        biases_loaded, rows_loaded = sem("biases_loaded"), sem("rows_loaded")
        router_loaded, side_loaded = sem("router_loaded"), sem("side_loaded")
        consts_made = sem("consts_made")
        dve_consts, dve_zeros = sem("dve_consts"), sem("dve_zeros")
        w0_hi_made = sem("w0_hi_made")
        w_hi_made, w_split = sem("w_hi_made"), sem("w_split")
        router_hi, router_split = sem("router_hi"), sem("router_split")
        setup_act = sem("setup_act")
        f_bn, f_stats, f_rstd_in, f_rstd_done, f_xh_done = (sem(n) for n in (
            "f_bn", "f_stats", "f_rstd_in", "f_rstd_done", "f_xh_done"))
        s_bn, s_stats, s_rstd_steps, s_rstd_done, s_xh_done = (sem(n) for n in (
            "s_bn", "s_stats", "s_rstd_steps", "s_rstd_done", "s_xh_done"))
        sf_written, sf_read = sem("sf_written"), sem("sf_read")
        sa_written, sa_read = sem("sa_written"), sem("sa_read")
        xT_hi_made, wT_hi_made = sem("xT_hi_made"), sem("wT_hi_made")
        gate_step, gate_exp, gate_ratio, gate_diff, gate_w = (sem(n) for n in (
            "gate_step", "gate_exp", "gate_ratio", "gate_diff", "gate_w"))
        z_ready, h_ready, hi_ready, lo_ready, y_step = (sem(n) for n in (
            "z_ready", "h_ready", "hi_ready", "lo_ready", "y_step"))
        y_read, acc_added, accT_ready = sem("y_read"), sem("acc_added"), sem("accT_ready")
        a_abs = sem("a_abs")
        a_res, a_mid, a_conv, a_act, a_soft, a_relu, a_delta, a_decay, a_drive, a_scan, a_y, a_gated = (sem(n) for n in (
            "a_res", "a_mid", "a_conv", "a_act", "a_soft", "a_relu", "a_delta", "a_decay", "a_drive",
            "a_scan", "a_y", "a_gated"))
        r_prev, r_mixed, r_sq, r_prod, r_done = (sem(n) for n in ("r_prev", "r_mixed", "r_sq", "r_prod", "r_done"))
        l_sq_done, l_exp, l_gs, l_rec = (sem(n) for n in ("l_sq_done", "l_exp", "l_gs", "l_rec"))
        stored = sem("stored")
        wait_carried = sem("wait_carried")

        def wait(eng, s, value):
            if not isinstance(value, int) or value > 0:
                eng.wait_ge(s, value)

        def wait_apart(eng, s, value):
            wait(eng, s, value)
            if not isinstance(value, int):
                eng.sem_inc(wait_carried, 1)

        def sf_at(s, use):
            if isinstance(s, int) and s == -1:
                return SF_PREP.index(use)
            order = SF_LAST if isinstance(s, int) and s == N_SLOT - 1 else SF_FULL
            return len(SF_FULL) * s + len(SF_PREP) + order.index(use)

        SA_A0 = len(SA_SETUP)
        SA_T0 = SA_A0 + N_CHUNK * len(SA_A)
        SA_T = 2 * len(SA_R) + len(SA_L)

        def sa_setup(use):
            return SA_SETUP.index(use)

        def sa_a(j, use):
            return j * len(SA_A) + SA_A0 + SA_A.index(use)

        def sa_r(j, o, use):
            return j * SA_T + SA_T0 + o * (len(SA_R) + len(SA_L)) + SA_R.index(use)

        def sa_l(j, use):
            return j * SA_T + SA_T0 + len(SA_R) + SA_L.index(use)

        def xs(c, t=None):
            if t is None:
                return x[:, bass.ds(c * CHUNK, CHUNK)]
            return x[:, bass.ds(c * CHUNK + t * P, P)]

        def tile(a, t):
            return a[:, t * P:(t + 1) * P]

        def prepared(s):
            return sf_at(s - 1, "T") + 1

        SF_FULL = sf_order(0)
        assert SF_FULL == sf_order(1) == sf_order(2)

        block = ctx.enter_context(nc.Block())

        def at_step(plan, k, *args):
            for name, work in plan:
                if STEP[name] == k:
                    work(*args)

        def at_prep_step(plan, k, side, *args):
            for name, work in plan:
                if STEP[name][(None, "A", "T").index(side)] == k:
                    work(*args)

        SIDE_LOADS = [
            (w_in[:, :], d["L0_attn_W_in"]), (w_xp[:, :], d["L0_attn_W_xp"]), (w_bg[:, :], d["L0_attn_W_Bg"]),
            (w_cg[:, :], d["L0_attn_W_Cg"]), (w_dt[:, :], d["L0_attn_W_dt"]), (w_bp[:, :], d["L0_attn_W_Bp"]),
            (w_cp[:, :], d["L0_attn_W_Cp"]), (w_out[:, :], d["L0_attn_W_out"]),
            (ffn_raw[:, 0, :], d["L1_ffn_W_k"]), (ffn_raw[:, 1, :], d["L1_ffn_W_r"]),
            (ffn_raw[:, 2, :], d["L1_ffn_W_v"]), (ffn_raw[:, 3, :], d["L1_attn_Wv"]), (wo[:, :], d["L1_attn_Wo"]),
            (pos[:, :], d["L1_attn_splat_positions"]),
            (logs[:, :], d["L1_attn_splat_log_scales"].rearrange("(a b) -> a b", b=1)),
            (amp[:, :], d["L1_attn_splat_amplitudes"].rearrange("(a b) -> a b", b=1)),
        ]

        @block.sync
        def _(sp):
            tok = x_in.rearrange("b s c -> (b s) c").rearrange("(t p) f -> p t f", p=P)

            def load_x(t0, t1, s):
                sp.dma_start(x[:, t0 * C:t1 * C].rearrange("p (t f) -> p t f", f=C), tok[:, t0:t1]).then_inc(s, 16)

            def load_experts(q0, q1):
                if q0 == 0:
                    sp.dma_start(w1_raw[:, 0, :], d["L0_ffn_Ws1"]).then_inc(w_loaded[0], 16)
                    sp.dma_start(w2_raw[:, 0, :, :], d["L0_ffn_Ws2"].rearrange("(i p) c -> p i c", p=P))\
                        .then_inc(w_loaded[0], 16)
                    return
                sp.dma_start(w1_raw[:, q0:q1, :], d["L0_ffn_We1"][q0 - 1:q1 - 1].rearrange("e p i -> p e i"))\
                    .then_inc(w_loaded[q0], 16)
                w2 = d["L0_ffn_We2"][q0 - 1:q1 - 1].rearrange("e (i p) c -> p (e i) c", p=P)
                sp.dma_start(w2_raw[:, q0:q1, :, :].rearrange("p e i c -> p (e i) c"), w2)\
                    .then_inc(w_loaded[q0], 16)

            load_x(0, TILES, x_loaded)
            load_experts(0, 1)
            load_experts(1, 2)
            load_x(TILES, N_TOK // P, x_rest_loaded)
            for q0, q1 in zip(LOTS[2:-1], LOTS[3:]):
                load_experts(q0, q1)
            for dst, src in SIDE_LOADS:
                sp.dma_start(dst, src).then_inc(side_loaded, 16)
            res = out.rearrange("b s c -> (b s) c").rearrange("(c t p) f -> c p t f", p=P, t=TILES)
            for c in range(N_CHUNK):
                sp.wait_ge(r_done, 2 * c + 2)
                sp.dma_start(res[c], x[:, c * CHUNK:(c + 1) * CHUNK].rearrange("p (t f) -> p t f", f=C))\
                    .then_inc(stored, 16)
            sp.wait_ge(stored, 16 * N_CHUNK)

        @block.gpsimd
        def _(pool):
            made = 0

            def const(ins):
                nonlocal made
                made += 1
                ins.then_inc(consts_made, 1)
                pool.wait_ge(consts_made, made)

            const(pool.memset(ident[:, :], 0.0))
            const(pool.affine_select(out=ident[:, :], in_=ident[:, :], compare_op=ALU.not_equal, fill=1.0, base=0,
                                     pattern=[[-1, P]], channel_multiplier=1))

            def late_consts():
                const(pool.memset(sel_raw[:, :, :], 0.0))
                for off in (0, 32):
                    const(pool.affine_select(out=sel_raw[:, :, :], in_=sel_raw[:, :, :], compare_op=ALU.not_equal,
                                             fill=1.0, base=-off, pattern=[[-1, E], [0, P]], channel_multiplier=1))
                const(pool.iota(expert_no_i[:, :], pattern=[[1, E]], base=0, channel_multiplier=0))

            def f_rstd_of(n):
                wait_apart(pool, f_stats, n + 1)
                pool.tensor_scalar(f_rstd[:, :], f_mv[:, :, 1], EPS, None, ALU.add).then_inc(f_rstd_in, 1)
                wait(pool, f_rstd_in, n + 1)
                pool.tensor_tensor(f_rstd[:, :], f_rstd[:, :], mhalf_exp[:, :], ALU.pow).then_inc(f_rstd_done, 1)

            def gate_exponent(n):
                wait(pool, sf_read, sf_at(n - 1, "L") + 1)
                pool.tensor_tensor(ex[:, :, :], base_e[:, :, :], lg[:, :, :], ALU.pow).then_inc(gate_exp, 1)

            def gate_ratio_of(n):
                wait(pool, gate_diff, n + 1)
                pool.tensor_tensor(ratio[:, :], base_root_e[:, :], diff[:, :], ALU.pow).then_inc(gate_ratio, 1)

            def add(s, q):
                wait(pool, y_read, s * (Q + 1) + q + 1)
                wait(pool, acc_added, s * E + q - 1)
                pool.tensor_tensor(acc[:, :], acc[:, :], weighted[q % 2][:, :], ALU.add).then_inc(acc_added, 1)

            def split_hi(q):
                if q in LOTS:
                    pool.wait_ge(w_loaded[q], 32)
                pool.tensor_copy(w1_hi[:, q, :], w1_raw[:, q, :]).then_inc(w_hi_made, 1)
                pool.tensor_copy(w2_hi[:, q, :, :], w2_raw[:, q, :, :]).then_inc(w_hi_made, 1)

            def a_rstd(j):
                n = j * 6
                wait_apart(pool, s_stats, j + 1)
                pool.tensor_scalar(s_r1[:, :], s_mv[:, :, 1], EPS, None, ALU.add).then_inc(s_rstd_steps, 1)
                wait(pool, s_rstd_steps, n + 1)
                pool.tensor_tensor(s_r1[:, :], s_r1[:, :], mhalf_exp[:, :], ALU.pow).then_inc(s_rstd_steps, 1)
                wait(pool, s_rstd_steps, n + 2)
                pool.tensor_tensor(s_v2[:, :], s_r1[:, :], s_r1[:, :], ALU.mult).then_inc(s_rstd_steps, 1)
                wait(pool, s_rstd_steps, n + 3)
                pool.tensor_tensor(s_v2[:, :], s_v2[:, :], s_mv[:, :, 1], ALU.mult).then_inc(s_rstd_steps, 1)
                wait_apart(pool, s_rstd_steps, n + 4)
                pool.tensor_scalar(s_v2[:, :], s_v2[:, :], EPS, None, ALU.add).then_inc(s_rstd_steps, 1)
                wait(pool, s_rstd_steps, n + 5)
                pool.tensor_tensor(s_v2[:, :], s_v2[:, :], mhalf_exp[:, :], ALU.pow).then_inc(s_rstd_steps, 1)
                wait(pool, s_rstd_steps, n + 6)
                pool.tensor_tensor(s_r2[:, :], s_v2[:, :], s_r1[:, :], ALU.mult).then_inc(s_rstd_done, 1)

            def a_residual(j):
                wait(pool, s_xh_done, j + 1)
                pool.tensor_tensor(xs(j), xs(j), a_xh1[:, :], ALU.add).then_inc(a_res, 1)

            def a_conv_mid(j):
                wait_apart(pool, sa_read, sa_a(j, "xb") + 1)
                pool.tensor_scalar(a_c[:, :].rearrange("p (b s) -> p b s", b=SEQS), xb_pad[:, :, 1:SEQ + 1],
                                   col("conv_w", 1), col("conv_b"), ALU.mult, ALU.add).then_inc(a_mid, 1)

            def a_drive_x(j):
                wait(pool, sa_read, sa_a(j, "B") + 1)
                wait(pool, a_act, j + 1)
                pool.tensor_tensor(a_dB[:, :], a_dB[:, :], a_xact[:, :], ALU.mult).then_inc(a_drive, 1)

            def a_gate(j):
                wait(pool, a_y, j + 1)
                wait(pool, sa_read, sa_a(j, "z") + 1)
                pool.tensor_tensor(a_h[:, :], a_h[:, :], a_sz[:, :], ALU.mult).then_inc(a_gated, 1)

            A_POOL = [
                ("pool a_rstd", a_rstd),
                ("pool a_residual", a_residual),
                ("pool a_conv_mid", a_conv_mid),
                ("pool a_drive_x", a_drive_x),
                ("pool a_gate", a_gate),
            ]

            def t_rstd(j, o):
                n = 6 * N_CHUNK + (j * 3 + o) * 1
                wait_apart(pool, s_stats, N_CHUNK + j * 3 + o + 1)
                pool.tensor_scalar(s_r1[:, :], s_mv[:, :, 1], EPS, None, ALU.add).then_inc(s_rstd_steps, 1)
                wait(pool, s_rstd_steps, n + 1)
                pool.tensor_tensor(s_r1[:, :], s_r1[:, :], mhalf_exp[:, :], ALU.pow).then_inc(s_rstd_done, 1)

            def r_shift(o2):
                def work(j):
                    wait_apart(pool, sa_read, sa_r(j, o2, "T") + 1)
                    prev = xT_pad[:, :, 0:SEQ]
                    for n, dst in ((0, r_tk), (1, r_tr)):
                        pool.tensor_scalar(dst[:, :].rearrange("p (b s) -> p b s", b=SEQS), prev,
                                           one_mu[:, n:n + 1], None, ALU.mult).then_inc(r_prev, 1)
                return work

            def r_square(o2):
                def work(j):
                    wait(pool, sa_read, sa_r(j, o2, "k") + 1)
                    pool.tensor_tensor(r_ka[:, :], r_rk[:, :], r_rk[:, :], ALU.mult).then_inc(r_sq, 1)
                return work

            def l_square(j):
                wait(pool, sa_read, sa_l(j, "T") + 1)
                pool.tensor_tensor(l_sq[:, :], l_xT[:, :], l_xT[:, :], ALU.mult).then_inc(l_sq_done, 1)

            T_POOL = [
                ("pool t_rstd0", lambda j: t_rstd(j, 0)),
                ("pool r_shift0", r_shift(0)),
                ("pool r_square0", r_square(0)),
                ("pool t_rstd1", lambda j: t_rstd(j, 1)),
                ("pool l_square", l_square),
                ("pool t_rstd2", lambda j: t_rstd(j, 2)),
                ("pool r_shift1", r_shift(1)),
                ("pool r_square1", r_square(1)),
            ]

            PREP_POOL = [
                ("pool f_rstd", f_rstd_of),
                ("pool gate_exponent", gate_exponent),
                ("pool gate_ratio", gate_ratio_of),
            ]

            def slot(s, prep, side):
                for k in range(STEPS):
                    if k == 1 and not (isinstance(s, int) and s == 0):
                        add(s - 1, E)
                    if k % IT == 1 and 2 <= k // IT:
                        add(s, k // IT - 1)
                    if prep:
                        at_prep_step(PREP_POOL, k, side, s + 1)
                    if isinstance(s, int) and s == 0 and k % IT == 2 and k // IT + 2 < Q:
                        split_hi(k // IT + 2)
                    if side == "A":
                        at_step(A_POOL, k, s - 1)
                    if side == "T":
                        at_step(T_POOL, k, s - (N_CHUNK + 1))

            pool.wait_ge(dve_zeros, 1)
            f_rstd_of(0)
            pool.wait_ge(router_loaded, 16 * 4)
            pool.tensor_copy(wr1_hi[:, :], wr1_raw[:, :]).then_inc(router_hi, 1)
            late_consts()
            split_hi(1)
            gate_exponent(0)
            gate_ratio_of(0)
            slot(0, True, None)
            with pool.Fori(1, N_CHUNK + 1) as s:
                slot(s, True, "A")
            with pool.Fori(N_CHUNK + 1, N_SLOT - 1) as s:
                slot(s, True, "T")
            slot(N_SLOT - 1, False, "T")
            add(N_SLOT - 1, E)
            for _, work in T_POOL:
                work(N_CHUNK - 1)

        @block.scalar
        def _(act):
            for r, n, view in row_loads[0:2]:
                act.dma_start(bias_rows[r:r + n, :], view).then_inc(biases_loaded, 16)
            for dst, src in ((wr1_raw[:, 0:RH], d["L0_ffn_Wr1"]),
                             (br1[:, :], d["L0_ffn_br1"].rearrange("(a b) -> a b", b=1)),
                             (wr2[0:RH, :], d["L0_ffn_Wr2"]),
                             (wr2[RH:RH + 1, :], d["L0_ffn_br2"].rearrange("(a b) -> a b", a=1))):
                act.dma_start(dst, src).then_inc(router_loaded, 16)
            for r, n, view in row_loads[2:]:
                act.dma_start(rows[r - IT * Q:r - IT * Q + n, :], view).then_inc(rows_loaded, 16)

            def silu(s, k):
                n = s * STEPS + k
                wait(act, z_ready, n + 1)
                wait(act, lo_ready, n + 1 - H_BUFS)
                if not hi_on_vector(k):
                    wait(act, y_step, n + 1 - H_BUFS)
                    act.activation(h_hi[k % H_BUFS][:, :], z[k % Z_BANKS][:, :], ACT.Silu,
                                   bias=col_of("bs1", k))
                act.activation(h[k % H_BUFS][:, :], z[k % Z_BANKS][:, :], ACT.Silu,
                               bias=col_of("bs1", k)).then_inc(h_ready, 1)

            def spread(s, q):
                wait(act, sf_written, sf_at(s, f"b{q}") + 1)
                wait(act, y_read, s * (Q + 1) + (q if q >= 2 else q - 2))
                act.activation(w_bc[q % 2][:, :], SF[:, :], ACT.Copy).then_inc(sf_read, 1)

            def router_relu(n):
                wait(act, sf_written, sf_at(n - 1, "R") + 1)
                act.activation(r1[0:RH, :], SF[0:RH, :], ACT.Relu, bias=br1[:, :]).then_inc(sf_read, 1)

            def a_silu_z(j):
                wait(act, sa_written, sa_a(j, "z") + 1)
                act.activation(a_sz[:, :], SA[:, :], ACT.Silu).then_inc(sa_read, 1)

            def a_silu_x(j):
                wait(act, a_conv, 2 * j + 2)
                act.activation(a_xact[:, :], a_c[:, :], ACT.Silu).then_inc(a_act, 1)

            def a_softplus(j):
                act.preload_act_table_set("natural_log_exp_and_others")
                wait(act, a_abs, j + 1)
                act.activation(a_l[:, :], a_l[:, :], ACT.Exp).then_inc(a_soft, 1)
                wait(act, a_soft, 2 * j + 1)
                act.activation(a_l[:, :], a_l[:, :], ACT.Ln, bias=1.0).then_inc(a_soft, 1)
                wait(act, a_delta, j + 1)
                act.activation(a_dA[:, :], a_dl[:, :], ACT.Exp, scale=col("A")).then_inc(a_decay, 1)

            A_ACT = [
                ("act a_silu_z", a_silu_z),
                ("act a_silu_x", a_silu_x),
                ("act a_softplus", a_softplus),
            ]

            def r_evac(o2):
                def work(j):
                    wait(act, sa_written, sa_r(j, o2, "T") + 1)
                    act.activation(xT_pad[:, :, 1:SEQ + 1], SA[:, :].rearrange("p (b s) -> p b s", b=SEQS),
                                   ACT.Copy).then_inc(sa_read, 1)
                return work

            def r_relu(o2):
                def work(j):
                    wait(act, sa_written, sa_r(j, o2, "k") + 1)
                    act.activation(r_rk[:, :], SA[:, :], ACT.Relu).then_inc(sa_read, 1)
                return work

            def r_sigmoid(o2):
                def work(j):
                    wait(act, sa_written, sa_r(j, o2, "r") + 1)
                    act.activation(r_rr[:, :], SA[:, :], ACT.Tanh, scale=0.5).then_inc(sa_read, 1)
                return work

            def l_evac(j):
                wait(act, sa_written, sa_l(j, "T") + 1)
                act.activation(l_xT[:, :], SA[:, :], ACT.Copy).then_inc(sa_read, 1)

            def l_gauss(j):
                wait(act, sa_read, sa_l(j, "xp") + 1)
                for b in range(SEQS):
                    act.activation(l_E[0:S, b * SEQ:(b + 1) * SEQ], l_dd[0:S, b * SEQ:(b + 1) * SEQ], ACT.Exp,
                                   scale=inv_s2[:, :], accum_out=gsum[:, b:b + 1]).then_inc(l_exp, 1)

            def l_evac_E(j):
                wait(act, sa_written, sa_l(j, "Et") + 1)
                act.activation(l_Et[:, 0:TILES * S], SA[:, 0:TILES * S], ACT.Copy).then_inc(sa_read, 1)

            T_ACT = [
                ("act r_evac0", r_evac(0)),
                ("act r_relu0", r_relu(0)),
                ("act r_sigmoid0", r_sigmoid(0)),
                ("act l_evac", l_evac),
                ("act l_gauss", l_gauss),
                ("act l_evac_E", l_evac_E),
                ("act r_evac1", r_evac(1)),
                ("act r_relu1", r_relu(1)),
                ("act r_sigmoid1", r_sigmoid(1)),
            ]

            def slot(s, prep, side):
                for k in range(STEPS):
                    silu(s, k)
                    if prep:
                        at_prep_step([("act router_relu", router_relu)], k, side, s + 1)
                    if isinstance(s, int) and s == 0 and k == STEP["act setup_scales"]:
                        act.wait_ge(side_loaded, 16 * len(SIDE_LOADS))
                        act.activation(inv_s2[:, :], logs[:, :], ACT.Exp, scale=-2.0).then_inc(setup_act, 1)
                    if isinstance(s, int) and s == 0 and k == STEP["act spread0"]:
                        spread(s, 0)
                    q = (k - STEP["act spread"]) // IT
                    if (k - STEP["act spread"]) % IT == 0 and 0 <= q < E and not (isinstance(s, int) and s + q == 0):
                        spread(s, q)
                    if side == "A":
                        at_step(A_ACT, k, s - 1)
                    if side == "T":
                        at_step(T_ACT, k, s - (N_CHUNK + 1))

            act.wait_ge(w_loaded[0], 32)
            act.activation(w1_hi[:, 0, :], w1_raw[:, 0, :], ACT.Copy).then_inc(w0_hi_made, 1)
            act.activation(w2_hi[:, 0, :, :], w2_raw[:, 0, :, :], ACT.Copy).then_inc(w0_hi_made, 1)
            act.wait_ge(router_loaded, 16 * 4)
            router_relu(0)
            act.wait_ge(sa_read, sa_setup("biases") + 1)
            slot(0, True, None)
            with act.Fori(1, N_CHUNK + 1) as s:
                slot(s, True, "A")
            with act.Fori(N_CHUNK + 1, N_SLOT - 1) as s:
                slot(s, True, "T")
            slot(N_SLOT - 1, False, "T")
            for _, work in T_ACT:
                work(N_CHUNK - 1)

        @block.vector
        def _(dve):
            def norm_stats(c, stat, mv, bn, stats, count):
                for t in range(TILES):
                    last = dve.bn_stats(stat[:, t, :], xs(c, t))
                last.then_inc(bn, 1)
                wait_apart(dve, bn, count + 1)
                for t in range(TILES):
                    last = dve.bn_aggr(mv[:, t, :], stat[:, t, :])
                last.then_inc(stats, 1)

            def norm_apply(c, dst, mv, rstd):
                for t in range(TILES):
                    last = dve.tensor_scalar(tile(dst, t), xs(c, t), mv[:, t, 0:1], rstd[:, t:t + 1],
                                             ALU.subtract, ALU.mult)
                return last

            def chunk_of(n):
                return n % N_CHUNK if isinstance(n, int) else n & (N_CHUNK - 1)

            def f_moments(n):
                norm_stats(chunk_of(n), f_stat, f_mv, f_bn, f_stats, n)

            def f_norm(n):
                wait(dve, f_rstd_done, n + 1)
                norm_apply(chunk_of(n), f_xh, f_mv, f_rstd).then_inc(f_xh_done, 1)

            def f_split(n):
                wait(dve, sf_written, sf_at(n - 1, "T") + 1)
                par = n % 2 if isinstance(n, int) else n & 1
                dve.tensor_copy(xT_hi[:, par, :], SF[:, :]).then_inc(xT_hi_made, 1)
                wait(dve, xT_hi_made, n + 1)
                dve.tensor_tensor(xT_lo[:, par, :], SF[:, :], xT_hi[:, par, :].bitcast(F32), ALU.subtract)\
                    .then_inc(sf_read, 1)

            GATE = 16

            def gate_logits(n):
                wait(dve, sf_written, sf_at(n - 1, "L") + 1)
                logits = SF[:, 0:TILES * E].rearrange("p (t e) -> p t e", e=E)
                dve.tensor_reduce(lg_max[:, :], logits, AX.X, ALU.max).then_inc(gate_step, 1)
                wait(dve, gate_step, GATE * n + 1)
                dve.tensor_tensor(lg[:, :, :], logits, lg_max[:, :].unsqueeze(2).to_broadcast([P, TILES, E]),
                                  ALU.subtract).then_inc(sf_read, 1)

            def gate_top(n):
                g = GATE * n
                wait(dve, gate_exp, n + 1)
                dve.tensor_reduce(ex_sum[:, :], ex[:, :, :], AX.X, ALU.add).then_inc(gate_step, 1)
                wait(dve, gate_step, g + 2)
                dve.reciprocal(ex_rec[:, :], ex_sum[:, :]).then_inc(gate_step, 1)
                wait(dve, gate_step, g + 3)
                dve.tensor_tensor(gates[:, :, :], ex[:, :, :], ex_rec[:, :].unsqueeze(2).to_broadcast([P, TILES, E]),
                                  ALU.mult).then_inc(gate_step, 1)
                wait_apart(dve, gate_step, g + 4)
                for t in range(TILES):
                    last = dve.max(top[:, t, :], gates[:, t, :])
                last.then_inc(gate_step, 1)
                wait(dve, gate_step, g + 5)
                dve.tensor_tensor(diff[:, :], top[:, :, 1], top[:, :, 0], ALU.subtract).then_inc(gate_diff, 1)
                for t in range(TILES):
                    last = dve.max_index(top_at[:, t, :], top[:, t, :], gates[:, t, :])
                last.then_inc(gate_step, 1)
                wait(dve, gate_step, g + 6)
                dve.tensor_copy(top_atf[:, :, :], top_at[:, :, 0:2]).then_inc(gate_step, 1)
                wait(dve, gate_step, g + 7)
                for i in range(2):
                    dve.tensor_tensor(pick[i][:, :, :], expert_no[:, :].unsqueeze(1).to_broadcast([P, TILES, E]),
                                      top_atf[:, :, i:i + 1].to_broadcast([P, TILES, E]), ALU.is_equal)\
                        .then_inc(gate_step, 1)

            def gate_weights(n):
                g = GATE * n + 9
                wait(dve, gate_ratio, n + 1)
                dve.tensor_scalar(ratio1[:, :], ratio[:, :], 1.0, None, ALU.add).then_inc(gate_step, 1)
                wait(dve, gate_step, g + 1)
                dve.reciprocal(tw[:, :, 0], ratio1[:, :]).then_inc(gate_step, 1)
                wait(dve, gate_step, g + 2)
                dve.tensor_tensor(tw[:, :, 1], tw[:, :, 0], ratio[:, :], ALU.mult).then_inc(gate_step, 1)
                wait(dve, gate_step, g + 3)
                for i in range(2):
                    dve.tensor_tensor(pickw[i][:, :, :], pick[i][:, :, :], tw[:, :, i:i + 1].to_broadcast([P, TILES, E]),
                                      ALU.mult).then_inc(gate_step, 1)
                wait(dve, gate_step, g + 5)
                dve.tensor_tensor(w_tok[:, :, :], pickw[0][:, :, :], pickw[1][:, :, :], ALU.add).then_inc(gate_w, 1)
                dve.tensor_scalar(lg_max[:, :], lg_max[:, :], 0.0, None, ALU.mult).then_inc(gate_step, 2)

            def gate_split(n):
                wait(dve, sf_written, sf_at(n - 1, "W") + 1)
                dve.tensor_copy(wT[0:E, :], SF[0:E, :]).then_inc(wT_hi_made, 1)
                wait(dve, wT_hi_made, n + 1)
                dve.tensor_tensor(wT[32:32 + E, :], SF[0:E, :], wT[0:E, :].bitcast(F32), ALU.subtract)\
                    .then_inc(sf_read, 1)

            def lo(s, k):
                n = s * STEPS + k
                wait(dve, h_ready, n + 1)
                wait(dve, y_step, n + 1 - H_BUFS)
                if hi_on_vector(k):
                    dve.tensor_copy(h_hi[k % H_BUFS][:, :], h[k % H_BUFS][:, :]).then_inc(hi_ready, 1)
                    wait(dve, hi_ready, s * (STEPS - hi_before(STEPS)) + k - hi_before(k) + 1)
                dve.tensor_tensor(h_lo[k % H_BUFS][:, :], h[k % H_BUFS][:, :], h_hi[k % H_BUFS][:, :].bitcast(F32),
                                  ALU.subtract).then_inc(lo_ready, 1)

            def combine(s, q):
                wait(dve, y_step, s * STEPS + IT * (q + 1))
                if q == 0:
                    if isinstance(s, int) and s == 0:
                        dve.wait_ge(sa_read, sa_setup("cols") + 1)
                    dve.tensor_scalar(acc[:, :], y[0][:, :], col("bs2"), None, ALU.add).then_inc(y_read, 1)
                    return
                wait(dve, sf_read, sf_at(s, f"b{q - 1}") + 1)
                wait(dve, acc_added, s * E + q - 2)
                dve.scalar_tensor_tensor(weighted[q % 2][:, :], y[q % Y_BANKS][:, :], col_of("bs2", q),
                                         w_bc[(q - 1) % 2][:, :], ALU.add, ALU.mult).then_inc(y_read, 1)

            def finish(s):
                wait(dve, accT_ready, s + 1)
                dve.scalar_tensor_tensor(xs(chunk_of(s)), y[1][:, :], 0.5, xs(chunk_of(s)), ALU.mult, ALU.add)\
                    .then_inc(y_read, 1)

            def split_lo(q):
                hi_made, n = (w0_hi_made, 0) if q == 0 else (w_hi_made, 2 * (q - 1))
                wait(dve, hi_made, n + 1)
                dve.tensor_tensor(w1_lo[:, q, :], w1_raw[:, q, :], w1_hi[:, q, :].bitcast(F32), ALU.subtract)\
                    .then_inc(w_split, 1)
                wait(dve, hi_made, n + 2)
                dve.tensor_tensor(w2_lo[:, q, :, :], w2_raw[:, q, :, :], w2_hi[:, q, :, :].bitcast(F32), ALU.subtract)\
                    .then_inc(w_split, 1)

            def setup_cols():
                dve.wait_ge(sa_written, sa_setup("cols") + 1)
                dve.tensor_copy(cols[:, IT * Q:ROWS], SA[:, 0:ROWS - IT * Q]).then_inc(sa_read, 1)

            def setup_small():
                dve.wait_ge(sa_written, sa_setup("small") + 1)
                dve.tensor_copy(small[:, 0:S], SA[:, 0:S])
                dve.tensor_copy(w_xpT, SA[0:RK, S:S + P])
                dve.tensor_copy(w_bgT, SA[0:DS, S + P:S + 2 * P])
                dve.tensor_copy(w_cgT, SA[0:DS, S + 2 * P:S + 3 * P]).then_inc(sa_read, 1)

            def setup_ffn1():
                dve.wait_ge(sa_written, sa_setup("ffn1") + 1)
                dve.tensor_copy(ffnT[:, :, :], SA[:, :].rearrange("p (a b) -> p a b", a=4)).then_inc(sa_read, 1)

            def setup_products():
                dve.wait_ge(sa_written, sa_setup("products") + 1)
                dve.tensor_copy(prod[:, :, :], SA[:, :].rearrange("p (a b) -> p a b", a=4)).then_inc(sa_read, 1)

            def setup_scalars():
                dve.wait_ge(side_loaded, 16 * len(SIDE_LOADS))
                dve.wait_ge(sa_read, sa_setup("cols") + 1)
                dve.tensor_scalar(one_mu[:, 0:1], col("mu_k"), -1.0, 1.0, ALU.mult, ALU.add)
                dve.tensor_scalar(one_mu[:, 1:2], col("mu_r"), -1.0, 1.0, ALU.mult, ALU.add)
                dve.tensor_tensor(amp2[:, :], amp[:, :], amp[:, :], ALU.mult)
                dve.tensor_tensor(pos_sq[:, :], pos[:, :], pos[:, :], ALU.mult).then_inc(dve_consts, 1)
                dve.wait_ge(dve_consts, 2)
                dve.tensor_reduce(nhalf_p2[:, :], pos_sq[:, :], AX.X, ALU.add).then_inc(dve_consts, 1)
                dve.wait_ge(dve_consts, 3)
                dve.tensor_scalar(nhalf_p2[:, :], nhalf_p2[:, :], -0.5, None, ALU.mult).then_inc(dve_consts, 1)

            SETUP_DVE = [
                ("dve setup_cols", setup_cols),
                ("dve setup_small", setup_small),
                ("dve setup_ffn1", setup_ffn1),
                ("dve setup_scalars", setup_scalars),
                ("dve setup_products", setup_products),
            ]

            def a_moments(j):
                wait_apart(dve, y_read, (Q + 1) * (j + 1))
                dve.wait_ge(w_split, 2 * Q)
                norm_stats(j, s_stat, s_mv, s_bn, s_stats, j)

            def a_norm(j):
                wait(dve, s_rstd_done, j + 1)
                norm_apply(j, a_xh2, s_mv, s_r2)
                norm_apply(j, a_xh1, s_mv, s_r1).then_inc(s_xh_done, 1)

            def a_affine(j):
                wait(dve, sa_written, sa_a(j, "T") + 1)
                dve.tensor_scalar(a_xnT[:, :], SA[:, :], col("gamma"), col("beta"), ALU.mult, ALU.add)\
                    .then_inc(sa_read, 1)

            def a_pad(j):
                wait(dve, sa_written, sa_a(j, "xb") + 1)
                dve.tensor_copy(xb_pad[:, :, 1:SEQ + 1], SA[:, :].rearrange("p (b s) -> p b s", b=SEQS))\
                    .then_inc(sa_read, 1)

            def a_conv_sides(j):
                c = a_c[:, :].rearrange("p (b s) -> p b s", b=SEQS)
                wait(dve, a_mid, j + 1)
                dve.scalar_tensor_tensor(c, xb_pad[:, :, 0:SEQ], col("conv_w", 0), c, ALU.mult, ALU.add)\
                    .then_inc(a_conv, 1)
                wait(dve, a_conv, 2 * j + 1)
                dve.scalar_tensor_tensor(c, xb_pad[:, :, 2:SEQ + 2], col("conv_w", 2), c, ALU.mult, ALU.add)\
                    .then_inc(a_conv, 1)

            def a_dt(j):
                wait(dve, sa_written, sa_a(j, "dt") + 1)
                dve.tensor_scalar(a_u[:, :], SA[:, :], col("b_dt"), None, ALU.add).then_inc(sa_read, 1)
                wait(dve, sa_read, sa_a(j, "dt") + 1)
                dve.scalar_tensor_tensor(a_l[:, :], a_u[:, :], -1.0, a_u[:, :], ALU.mult, ALU.min).then_inc(a_abs, 1)
                dve.tensor_scalar(a_dl[:, :], a_u[:, :], 0.0, None, ALU.max).then_inc(a_relu, 1)

            def a_delta_sum(j):
                wait(dve, a_soft, 2 * j + 2)
                wait(dve, a_relu, j + 1)
                dve.tensor_tensor(a_dl[:, :], a_dl[:, :], a_l[:, :], ALU.add).then_inc(a_delta, 1)

            def a_times_B(j):
                wait(dve, sa_written, sa_a(j, "B") + 1)
                wait(dve, a_delta, j + 1)
                dve.tensor_tensor(a_dB[:, :], SA[:, :], a_dl[:, :], ALU.mult).then_inc(sa_read, 1)

            def a_recurrence(j):
                wait(dve, a_drive, j + 1)
                wait(dve, a_decay, j + 1)
                for b in range(SEQS):
                    last = dve.tensor_tensor_scan(a_h[:, b * SEQ:(b + 1) * SEQ], a_dA[:, b * SEQ:(b + 1) * SEQ],
                                                  a_dB[:, b * SEQ:(b + 1) * SEQ], 0.0, ALU.mult, ALU.add)
                last.then_inc(a_scan, 1)

            def a_times_C(j):
                wait(dve, sa_written, sa_a(j, "C") + 1)
                wait(dve, a_scan, j + 1)
                dve.tensor_tensor(a_h[:, :], SA[:, :], a_h[:, :], ALU.mult).then_inc(sa_read, 1)
                wait(dve, sa_read, sa_a(j, "C") + 1)
                dve.scalar_tensor_tensor(a_h[:, :], a_xact[:, :], col("D"), a_h[:, :], ALU.mult, ALU.add)\
                    .then_inc(a_y, 1)

            def a_add(j):
                wait(dve, sa_written, sa_a(j, "out") + 1)
                wait(dve, a_res, j + 1)
                dve.tensor_tensor(xs(j), SA[:, :], xs(j), ALU.add).then_inc(sa_read, 1)

            A_DVE = [
                ("dve a_moments", a_moments),
                ("dve a_norm", a_norm),
                ("dve a_affine", a_affine),
                ("dve a_pad", a_pad),
                ("dve a_conv_sides", a_conv_sides),
                ("dve a_dt", a_dt),
                ("dve a_delta_sum", a_delta_sum),
                ("dve a_times_B", a_times_B),
                ("dve a_recurrence", a_recurrence),
                ("dve a_times_C", a_times_C),
                ("dve a_add", a_add),
            ]

            def t_moments(j, o, before):
                before(j)
                norm_stats(j, s_stat, s_mv, s_bn, s_stats, N_CHUNK + j * 3 + o)

            def t_norm(j, o, dst):
                wait(dve, s_rstd_done, N_CHUNK + j * 3 + o + 1)
                norm_apply(j, dst, s_mv, s_r1).then_inc(s_xh_done, 1)

            def r_first(j):
                wait_apart(dve, y_read, (Q + 1) * (j + N_CHUNK + 1))
                wait(dve, sa_read, SA_T0)

            def r_mix(o2):
                def work(j):
                    now = xT_pad[:, :, 1:SEQ + 1]
                    for n, (t, dst, mu) in enumerate(((r_tk, r_xk, "mu_k"), (r_tr, r_xr, "mu_r"))):
                        wait(dve, r_prev, 4 * j + 2 * o2 + n + 1)
                        dve.scalar_tensor_tensor(dst[:, :].rearrange("p (b s) -> p b s", b=SEQS), now, col(mu),
                                                 t[:, :].rearrange("p (b s) -> p b s", b=SEQS), ALU.mult, ALU.add)\
                            .then_inc(r_mixed, 1)
                return work

            def r_out(o2):
                def work(j):
                    wait(dve, sa_written, sa_r(j, o2, "v") + 1)
                    wait(dve, sa_read, sa_r(j, o2, "r") + 1)
                    dve.scalar_tensor_tensor(r_t[:, :], r_rr[:, :], 1.0, SA[:, :], ALU.add, ALU.mult)\
                        .then_inc(sa_read, 1)
                    wait(dve, sa_read, sa_r(j, o2, "v") + 1)
                    dve.scalar_tensor_tensor(xs(j), r_t[:, :], 0.25, xs(j), ALU.mult, ALU.add).then_inc(r_done, 1)
                return work

            def l_distance(j):
                wait(dve, sa_written, sa_l(j, "xp") + 1)
                dve.tensor_scalar(l_dd[0:S, :], SA[0:S, :], nhalf_p2[:, :], 0.0, ALU.add, ALU.min)\
                    .then_inc(sa_read, 1)

            def l_evac_M(j):
                wait(dve, sa_written, sa_l(j, "MT") + 1)
                dve.tensor_copy(l_MT[:, 0:SEQS * S], SA[:, 0:SEQS * S]).then_inc(sa_read, 1)
                wait(dve, l_exp, 2 * j + 2)
                dve.tensor_scalar(gsum2[:, :], gsum[:, :], amp2[:, :], None, ALU.mult).then_inc(l_gs, 1)

            def l_evac_B(j):
                wait(dve, sa_written, sa_l(j, "B") + 1)
                dve.tensor_scalar(l_R2[0:S, 0:SEQS * P], SA[0:S, 0:SEQS * P], amp2[:, :], None, ALU.mult)\
                    .then_inc(sa_read, 1)

            def l_sums(j):
                wait(dve, sa_written, sa_l(j, "sum") + 1)
                dve.tensor_scalar(den[:, :], SA[:, 0:TILES], EPS_ATTN, None, ALU.add).then_inc(sa_read, 1)
                wait(dve, sa_read, sa_l(j, "sum") + 1)
                dve.reciprocal(rden[:, :], den[:, :]).then_inc(l_rec, 1)

            def l_out(j):
                wait(dve, sa_written, sa_l(j, "out") + 1)
                wait(dve, l_rec, j + 1)
                for t in range(TILES):
                    last = dve.scalar_tensor_tensor(xs(j, t), tile(SA, t), rden[:, t:t + 1], xs(j, t),
                                                    ALU.mult, ALU.add)
                last.then_inc(sa_read, 1)

            T_DVE = [
                ("dve t_moments0", lambda j: t_moments(j, 0, r_first)),
                ("dve t_norm0", lambda j: t_norm(j, 0, r_xh)),
                ("dve r_mix0", r_mix(0)),
                ("dve r_out0", r_out(0)),
                ("dve t_moments1", lambda j: t_moments(j, 1, lambda j: wait_apart(dve, r_done, 2 * j + 1))),
                ("dve t_norm1", lambda j: t_norm(j, 1, l_xh)),
                ("dve l_distance", l_distance),
                ("dve l_evac_M", l_evac_M),
                ("dve l_evac_B", l_evac_B),
                ("dve l_sums", l_sums),
                ("dve l_out", l_out),
                ("dve t_moments2", lambda j: t_moments(j, 2, lambda j: wait_apart(dve, sa_read, sa_l(j, "out") + 1))),
                ("dve t_norm2", lambda j: t_norm(j, 2, r_xh)),
                ("dve r_mix1", r_mix(1)),
                ("dve r_out1", r_out(1)),
            ]

            def f_moments_next(n, side):
                if side is None:
                    dve.wait_ge(x_rest_loaded, 16)
                elif side == "A":
                    wait_apart(dve, sa_read, sa_a(n - 2, "T"))
                else:
                    dve.wait_ge(sa_read, SA_T0)
                f_moments(n)

            PREP_DVE = [
                ("dve f_moments", f_moments_next),
                ("dve f_norm", lambda n, side: f_norm(n)),
                ("dve f_split", lambda n, side: f_split(n)),
                ("dve gate_logits", lambda n, side: gate_logits(n)),
                ("dve gate_top", lambda n, side: gate_top(n)),
                ("dve gate_weights", lambda n, side: gate_weights(n)),
                ("dve gate_split", lambda n, side: gate_split(n)),
            ]

            def slot(s, prep, side):
                first = isinstance(s, int) and s == 0
                for k in range(STEPS):
                    lo(s, k)
                    if k == 1 and not first:
                        combine(s - 1, E)
                    if k == STEP["dve finish"] and not first:
                        finish(s - 1)
                    if k % IT == 1 and 1 <= k // IT:
                        combine(s, k // IT - 1)
                    if first:
                        at_step([("dve gate_top0", gate_top), ("dve gate_weights0", gate_weights),
                                 ("dve gate_split0", gate_split)], k, 0)
                        if k % IT == 0 and k // IT + 1 < Q:
                            split_lo(k // IT + 1)
                    if prep:
                        at_prep_step(PREP_DVE, k, side, s + 1, side)
                    if first:
                        at_step(SETUP_DVE, k)
                    if side == "A":
                        at_step(A_DVE, k, s - 1)
                    if side == "T":
                        at_step(T_DVE, k, s - (N_CHUNK + 1))

            for ap, value in ((mhalf_exp[:, :], -0.5), (base_e[:, :, :], math.e), (base_root_e[:, :], math.exp(0.5)),
                              (wr1_raw[:, RH:P], 0.0), (nhalf[:, :], -0.5), (r1[RH:RH + 1, :], 1.0)):
                last = dve.memset(ap, value)
            last.then_inc(dve_zeros, 1)
            dve.wait_ge(x_loaded, 16)
            f_moments(0)
            f_norm(0)
            f_split(0)
            dve.wait_ge(sa_written, sa_setup("biases") + 1)
            dve.tensor_copy(cols[:, 0:IT * Q], SA[:, 0:IT * Q]).then_inc(sa_read, 1)
            dve.wait_ge(router_hi, 1)
            dve.tensor_tensor(wr1_lo[:, :], wr1_raw[:, :], wr1_hi[:, :].bitcast(F32), ALU.subtract)\
                .then_inc(router_split, 1)
            dve.memset(xb_pad[:, :, :], 0.0)
            dve.memset(xT_pad[:, :, :], 0.0)
            dve.memset(zero_row[:, :], 0.0).then_inc(dve_zeros, 1)
            split_lo(0)
            gate_logits(0)
            dve.wait_ge(dve_zeros, 2)
            dve.wait_ge(consts_made, 6)
            dve.tensor_copy(expert_no[:, :], expert_no_i[:, :])
            dve.tensor_copy(sel[:, :, :], sel_raw[:, :, :])
            dve.tensor_copy(wT[:, :], zero_row[:, :]).then_inc(dve_consts, 1)
            dve.wait_ge(dve_consts, 1)
            slot(0, True, None)
            with dve.Fori(1, N_CHUNK + 1) as s:
                slot(s, True, "A")
            with dve.Fori(N_CHUNK + 1, N_SLOT - 1) as s:
                slot(s, True, "T")
            slot(N_SLOT - 1, False, "T")
            combine(N_SLOT - 1, E)
            finish(N_SLOT - 1)
            for _, work in T_DVE:
                work(N_CHUNK - 1)

        @block.tensor
        def _(pe):
            def parity(s):
                return s % 2 if isinstance(s, int) else s & 1

            def three(dst, w_hi, w_lo, m_hi, m_lo, start, stop):
                pe.matmul(dst, w_hi, m_hi, start=start, stop=False)
                pe.matmul(dst, w_hi, m_lo, start=False, stop=False)
                return pe.matmul(dst, w_lo, m_hi, start=False, stop=stop)

            def z_tile(s, k):
                q, i = divmod(k, IT)
                if k == 0:
                    wait(pe, sf_read, prepared(s))
                if isinstance(s, int) and s == 0 and i == 0:
                    pe.wait_ge(w_split, 2 * q + 1)
                wait(pe, h_ready, s * STEPS + k + 1 - Z_BANKS)
                par = parity(s)
                three(z[k % Z_BANKS][:, :], w1_hi[:, q, i * P:(i + 1) * P], w1_lo[:, q, i * P:(i + 1) * P],
                      xT_hi[:, par, :], xT_lo[:, par, :], True, True).then_inc(z_ready, 1)

            def y_tile(s, k):
                q, i = divmod(k, IT)
                if isinstance(s, int) and s == 0 and i == 0:
                    pe.wait_ge(w_split, 2 * q + 2)
                if i == 0:
                    wait(pe, y_read, s * (Q + 1) + q + 1 - Y_BANKS)
                wait(pe, lo_ready, s * STEPS + k + 1)
                three(y[q % Y_BANKS][:, :], w2_hi[:, q, i, :], w2_lo[:, q, i, :],
                      h_hi[k % H_BUFS][:, :], h_lo[k % H_BUFS][:, :], i == 0, i == IT - 1).then_inc(y_step, 1)

            def turn_acc(s):
                wait(pe, acc_added, E * (s + 1))
                wait(pe, y_read, s * (Q + 1) + Q - 1)
                for t in range(TILES):
                    last = pe.transpose(tile(y[1], t), tile(acc, t), ident[:, :])
                last.then_inc(accT_ready, 1)

            def use_sf(s, use):
                wait(pe, sf_read, sf_at(s, use))

            def bc(s, q):
                use_sf(s, f"b{q}")
                pe.matmul(SF[:, :], sel[:, q, :], wT[:, :], start=True, stop=True).then_inc(sf_written, 1)

            def f_turn(n):
                use_sf(n - 1, "T")
                wait(pe, f_xh_done, n + 1)
                for t in range(TILES):
                    last = pe.transpose(tile(SF, t), tile(f_xh, t), ident[:, :])
                last.then_inc(sf_written, 1)

            def f_router(n):
                use_sf(n - 1, "R")
                par = parity(n)
                three(SF[:, :], wr1_hi[:, :], wr1_lo[:, :], xT_hi[:, par, :], xT_lo[:, par, :], True, True)\
                    .then_inc(sf_written, 1)

            def f_logits(n):
                use_sf(n - 1, "L")
                for t in range(TILES):
                    last = pe.matmul(SF[:, t * E:(t + 1) * E], tile(r1, t), wr2[:, :], start=True, stop=True)
                last.then_inc(sf_written, 1)

            def f_turn_w(n):
                use_sf(n - 1, "W")
                wait(pe, gate_w, n + 1)
                for t in range(TILES):
                    last = pe.transpose(SF[0:E, t * P:(t + 1) * P], w_tok[:, t, :], ident[:, :])
                last.then_inc(sf_written, 1)

            def turn_biases():
                n = IT * Q
                pe.wait_ge(biases_loaded, 16 * 2)
                pe.transpose(SA[:, 0:n], bias_rows[:, :], ident[0:n, 0:n]).then_inc(sa_written, 1)

            def turn_cols():
                n = ROWS - IT * Q
                pe.wait_ge(rows_loaded, 16 * (len(row_loads) - 2))
                pe.wait_ge(sa_read, sa_setup("cols"))
                pe.transpose(SA[:, 0:n], rows[:, :], ident[0:n, 0:n]).then_inc(sa_written, 1)

            def turn_small():
                pe.wait_ge(side_loaded, 16 * len(SIDE_LOADS))
                pe.wait_ge(sa_read, sa_setup("small"))
                pe.transpose(SA[:, 0:S], pos[:, :], ident[0:S, 0:S])
                pe.transpose(SA[0:RK, S:S + P], w_xp[:, :], ident[:, :])
                pe.transpose(SA[0:DS, S + P:S + 2 * P], w_bg[:, :], ident[:, :])
                pe.transpose(SA[0:DS, S + 2 * P:S + 3 * P], w_cg[:, :], ident[:, :]).then_inc(sa_written, 1)

            def turn_ffn1():
                pe.wait_ge(sa_read, sa_setup("ffn1"))
                for n in range(4):
                    last = pe.transpose(tile(SA, n), ffn_raw[:, n, :], ident[:, :])
                last.then_inc(sa_written, 1)

            def make_products():
                pe.wait_ge(sa_read, sa_setup("products"))
                for n, (wT_, w_) in enumerate(((w_xpT, w_dt[:, :]), (w_bgT, w_bp[:, :]), (w_cgT, w_cp[:, :]),
                                               (ffnT[:, 3, :], wo[:, :]))):
                    last = pe.matmul(tile(SA, n), wT_, w_, start=True, stop=True)
                last.then_inc(sa_written, 1)

            SETUP_PE = [
                ("pe turn_cols", turn_cols),
                ("pe turn_small", turn_small),
                ("pe turn_ffn1", turn_ffn1),
                ("pe make_products", make_products),
            ]

            def a_turn(j):
                wait(pe, sa_read, sa_a(j, "T"))
                wait(pe, s_xh_done, j + 1)
                for t in range(TILES):
                    last = pe.transpose(tile(SA, t), tile(a_xh2, t), ident[:, :])
                last.then_inc(sa_written, 1)

            def a_project(use, w, src):
                def work(j):
                    wait(pe, sa_read, sa_a(j, use))
                    if use == "dt":
                        wait(pe, a_act, j + 1)
                    pe.matmul(SA[:, :], w, src[:, :], start=True, stop=True).then_inc(sa_written, 1)
                return work

            def a_output(j):
                wait(pe, a_gated, j + 1)
                wait(pe, sa_read, sa_a(j, "out"))
                for t in range(TILES):
                    last = pe.matmul(tile(SA, t), tile(a_h, t), w_out[:, :], start=True, stop=True)
                last.then_inc(sa_written, 1)

            A_PE = [
                ("pe a_turn", a_turn),
                ("pe a_xb", a_project("xb", w_in[:, 0:C], a_xnT)),
                ("pe a_z", a_project("z", w_in[:, C:2 * C], a_xnT)),
                ("pe a_dt", a_project("dt", prod[:, 0, :], a_xact)),
                ("pe a_B", a_project("B", prod[:, 1, :], a_xact)),
                ("pe a_C", a_project("C", prod[:, 2, :], a_xact)),
                ("pe a_output", a_output),
            ]

            def t_turn(src, at_use, o):
                def work(j):
                    wait(pe, sa_read, at_use(j))
                    wait(pe, s_xh_done, N_CHUNK + j * 3 + o + 1)
                    for t in range(TILES):
                        last = pe.transpose(tile(SA, t), tile(src, t), ident[:, :])
                    last.then_inc(sa_written, 1)
                return work

            def r_key(o2):
                def work(j):
                    wait(pe, sa_read, sa_r(j, o2, "k"))
                    wait(pe, r_mixed, 4 * j + 2 * o2 + 1)
                    pe.matmul(SA[:, :], ffnT[:, 0, :], r_xk[:, :], start=True, stop=True).then_inc(sa_written, 1)
                return work

            def r_receptance(o2):
                def work(j):
                    wait(pe, sa_read, sa_r(j, o2, "r"))
                    wait(pe, r_mixed, 4 * j + 2 * o2 + 2)
                    for t in range(TILES):
                        last = pe.matmul(tile(SA, t), tile(r_xr, t), ffnT[:, 1, :], start=True, stop=True)
                    last.then_inc(sa_written, 1)
                return work

            def r_value(o2):
                def work(j):
                    wait(pe, sa_read, sa_r(j, o2, "v"))
                    wait(pe, r_sq, 2 * j + o2 + 1)
                    for t in range(TILES):
                        last = pe.matmul(tile(SA, t), tile(r_ka, t), ffnT[:, 2, :], start=True, stop=True)
                    last.then_inc(sa_written, 1)
                return work

            def l_products(j):
                wait(pe, sa_read, sa_l(j, "xp"))
                pe.matmul(SA[0:S, :], pT, l_xT[:, :], start=True, stop=False)
                wait(pe, l_sq_done, j + 1)
                pe.matmul(SA[0:S, :], nhalf[:, :], l_sq[:, :], start=False, stop=True).then_inc(sa_written, 1)

            def l_turn_E(j):
                wait(pe, sa_read, sa_l(j, "Et"))
                wait_apart(pe, l_exp, 2 * j + 2)
                for t in range(TILES):
                    last = pe.transpose(SA[:, t * S:(t + 1) * S], l_E[0:S, t * P:(t + 1) * P], ident[0:S, 0:S])
                last.then_inc(sa_written, 1)

            def l_moment(j):
                wait(pe, sa_read, sa_l(j, "MT"))
                for t in range(TILES):
                    b, i = divmod(t, SEQ // P)
                    last = pe.matmul(SA[:, b * S:(b + 1) * S], tile(l_xh, t), l_Et[:, t * S:(t + 1) * S],
                                     start=(i == 0), stop=(i == SEQ // P - 1))
                last.then_inc(sa_written, 1)

            def l_values(j):
                wait(pe, sa_read, sa_l(j, "B"))
                for b in range(SEQS):
                    last = pe.matmul(SA[0:S, b * P:(b + 1) * P], l_MT[:, b * S:(b + 1) * S], prod[:, 3, :],
                                     start=True, stop=True)
                last.then_inc(sa_written, 1)

            def l_row_sums(j):
                wait(pe, sa_read, sa_l(j, "sum"))
                wait(pe, l_gs, j + 1)
                for t in range(TILES):
                    b = t // (SEQ // P)
                    last = pe.matmul(SA[:, t:t + 1], l_E[0:S, t * P:(t + 1) * P], gsum2[:, b:b + 1],
                                     start=True, stop=True)
                last.then_inc(sa_written, 1)

            def l_output(j):
                wait(pe, sa_read, sa_l(j, "out"))
                for t in range(TILES):
                    b = t // (SEQ // P)
                    last = pe.matmul(tile(SA, t), l_E[0:S, t * P:(t + 1) * P], l_R2[0:S, b * P:(b + 1) * P],
                                     start=True, stop=True)
                last.then_inc(sa_written, 1)

            T_PE = [
                ("pe t_turn0", t_turn(r_xh, lambda j: sa_r(j, 0, "T"), 0)),
                ("pe r_key0", r_key(0)),
                ("pe r_receptance0", r_receptance(0)),
                ("pe r_value0", r_value(0)),
                ("pe t_turn1", t_turn(l_xh, lambda j: sa_l(j, "T"), 1)),
                ("pe l_products", l_products),
                ("pe l_turn_E", l_turn_E),
                ("pe l_moment", l_moment),
                ("pe l_values", l_values),
                ("pe l_row_sums", l_row_sums),
                ("pe l_output", l_output),
                ("pe t_turn2", t_turn(r_xh, lambda j: sa_r(j, 1, "T"), 2)),
                ("pe r_key1", r_key(1)),
                ("pe r_receptance1", r_receptance(1)),
                ("pe r_value1", r_value(1)),
            ]

            PREP_PE = [
                ("pe f_turn", f_turn),
                ("pe f_router", f_router),
                ("pe f_logits", f_logits),
                ("pe f_turn_w", f_turn_w),
            ]

            def slot(s, prep, side, more):
                first = isinstance(s, int) and s == 0
                for k in range(STEPS):
                    if k + LOOKAHEAD < STEPS:
                        z_tile(s, k + LOOKAHEAD)
                    elif more:
                        z_tile(s + 1, k + LOOKAHEAD - STEPS)
                    if k == STEP["pe turn_acc"] and not first:
                        turn_acc(s - 1)
                    if first and k == STEP["pe f_turn_w0"]:
                        pe.wait_ge(dve_consts, 1)
                        f_turn_w(0)
                        bc(0, 0)
                    if k % IT == STEP["pe bc"] and k // IT < E and not (first and k // IT == 0):
                        bc(s, k // IT)
                    if prep:
                        at_prep_step(PREP_PE, k, side, s + 1)
                    if first:
                        at_step(SETUP_PE, k)
                    if side == "A":
                        at_step(A_PE, k, s - 1)
                    if side == "T":
                        at_step(T_PE, k, s - (N_CHUNK + 1))
                    y_tile(s, k)

            pe.wait_ge(consts_made, 2)
            f_turn(0)
            turn_biases()
            z_tile(0, 0)
            pe.wait_ge(router_split, 1)
            f_router(0)
            for k in range(1, LOOKAHEAD):
                z_tile(0, k)
            f_logits(0)
            slot(0, True, None, True)
            with pe.Fori(1, N_CHUNK + 1) as s:
                slot(s, True, "A", True)
            with pe.Fori(N_CHUNK + 1, N_SLOT - 1) as s:
                slot(s, True, "T", True)
            slot(N_SLOT - 1, False, "T", False)
            turn_acc(N_SLOT - 1)
            for _, work in T_PE:
                work(N_CHUNK - 1)


_INS = [
    "L0_attn_x", "L0_attn_gamma", "L0_attn_beta", "L0_attn_W_in", "L0_attn_conv_w", "L0_attn_conv_b",
    "L0_attn_W_xp", "L0_attn_W_Bg", "L0_attn_W_Cg", "L0_attn_W_dt", "L0_attn_b_dt", "L0_attn_W_Bp",
    "L0_attn_W_Cp", "L0_attn_A", "L0_attn_D_skip", "L0_attn_W_out", "L0_ffn_Wr1", "L0_ffn_br1", "L0_ffn_Wr2",
    "L0_ffn_br2", "L0_ffn_Ws1", "L0_ffn_bs1", "L0_ffn_Ws2", "L0_ffn_bs2", "L0_ffn_We1", "L0_ffn_be1",
    "L0_ffn_We2", "L0_ffn_be2", "L1_attn_splat_positions", "L1_attn_splat_log_scales",
    "L1_attn_splat_amplitudes", "L1_attn_Wv", "L1_attn_Wo", "L1_ffn_W_r", "L1_ffn_W_k", "L1_ffn_W_v",
    "L1_ffn_mu_r", "L1_ffn_mu_k",
]


def kernel(**inputs):
    import numpy as _np
    import concourse.bacc as _bacc
    from concourse import mybir as _mybir
    from concourse.bass_utils import run_bass_kernel_spmd as _run

    nc = _bacc.Bacc("TRN2", target_bir_lowering=False, num_devices=1)
    arrays, aps = {}, {}
    for name in _INS:
        a = _np.ascontiguousarray(inputs[name])
        arrays[f"in_{name}_dram"] = a
        aps[name] = nc.dram_tensor(f"in_{name}_dram", a.shape, _mybir.dt.from_np(a.dtype),
                                   kind="ExternalInput").ap()
    x = arrays["in_L0_attn_x_dram"]
    out = nc.dram_tensor("out_0_dram", x.shape, _mybir.dt.from_np(x.dtype), kind="ExternalOutput").ap()
    macaron_kernel(nc, aps, out)
    r = _run(nc, [arrays], core_ids=[0])
    return r.results[0]["out_0_dram"]
```

```python
import math
from contextlib import ExitStack

import concourse.bass as bass
from concourse import mybir

ALU = mybir.AluOpType
ACT = mybir.ActivationFunctionType
AX = mybir.AxisListType
F32 = mybir.dt.float32
F32R = mybir.dt.float32r
U32 = mybir.dt.uint32

P = 128
CHUNK = 512
TILES = CHUNK // P
SEQ = 256
SEQS = CHUNK // SEQ
EPS = 1e-5
EPS_ATTN = 1e-8
LOOKAHEAD = 3
Z_BANKS = 4
H_BUFS = 4
SPLIT_BUFS = 6
W_BUFS = 4
Y_BANKS = 2


HI_ON_VECTOR = [
    [4, 6, 7, 12, 14, 16, 18, 21, 22, 23, 27, 28, 30, 33, 35],
    [0, 1, 5, 12, 13, 14, 15, 19, 23, 25, 31],
    [0, 1, 7, 13, 15, 17, 20, 25, 28, 29, 31],
]


SF_USES = ["T", "R", "L", "W"]
SA_SETUP = ["biases", "cols", "small", "ffn1", "products"]
SA_A = ["T", "xb", "z", "dt", "B", "C", "out"]
SA_R = ["T", "k", "r", "v"]
SA_L = ["T", "xp", "Et", "MT", "B", "sum", "out"]


STEP = {
    "pool a_rstd": 3,
    "pool a_residual": 11,
    "pool a_conv_mid": 15,
    "pool a_drive_x": 23,
    "pool a_gate": 25,
    "pool t_rstd0": 7,
    "pool r_shift0": 7,
    "pool t_rstd1": 8,
    "pool t_rstd2": 22,
    "pool r_shift1": 25,
    "act a_silu_z": 21,
    "act a_silu_x": 21,
    "act a_softplus": 24,
    "act r_evac0": 9,
    "act r_square0": 11,
    "act r_sigmoid0": 13,
    "act l_evac": 19,
    "act l_gauss": 21,
    "act l_evac_E": 22,
    "act r_evac1": 32,
    "act r_square1": 35,
    "act r_sigmoid1": 35,
    "dve setup_cols": 4,
    "dve setup_small": 13,
    "dve setup_ffn1": 24,
    "dve setup_scalars": 24,
    "dve setup_products": 27,
    "dve a_moments": 7,
    "dve a_norm": 12,
    "dve a_affine": 16,
    "dve a_pad": 18,
    "dve a_conv_sides": 19,
    "dve a_dt": 23,
    "dve a_delta_sum": 23,
    "dve a_times_B": 27,
    "dve a_recurrence": 28,
    "dve a_times_C": 32,
    "dve a_add": 35,
    "dve t_moments0": 4,
    "dve t_norm0": 5,
    "dve r_mix0": 9,
    "dve r_out0": 14,
    "dve t_moments1": 14,
    "dve t_norm1": 16,
    "dve l_distance": 20,
    "dve l_evac_M": 23,
    "dve l_evac_B": 25,
    "dve l_sums": 27,
    "dve l_out": 28,
    "dve t_moments2": 28,
    "dve t_norm2": 29,
    "dve r_mix1": 32,
    "dve r_out1": 35,
    "pe turn_cols": 0,
    "pe turn_small": 5,
    "pe turn_ffn1": 22,
    "pe make_products": 26,
    "pe a_turn": 13,
    "pe a_xb": 16,
    "pe a_z": 18,
    "pe a_dt": 21,
    "pe a_B": 23,
    "pe a_C": 29,
    "pe a_output": 33,
    "pe t_turn0": 6,
    "pe r_key0": 9,
    "pe r_receptance0": 10,
    "pe r_value0": 12,
    "pe t_turn1": 17,
    "pe l_products": 18,
    "pe l_turn_E": 20,
    "pe l_moment": 22,
    "pe l_values": 24,
    "pe l_row_sums": 25,
    "pe l_output": 26,
    "pe t_turn2": 30,
    "pe r_key1": 32,
    "pe r_receptance1": 33,
    "pe r_value1": 33,
    "pool f_rstd": [7, 3, 1],
    "pool gate_exponent": [22, 16, 14],
    "pool gate_ratio": [28, 17, 22],
    "act router_relu": [22, 16, 18],
    "act setup_scales": 29,
    "pe f_turn_w0": 3,
    "pool w1_lo": -3,
    "pool w2_lo": -2,
    "act w1_hi": -3,
    "act w2_hi": -3,
    "dve gate_top0": 1,
    "dve gate_weights0": 2,
    "dve gate_rows0": 4,
    "dve f_moments": [0, 1, 1],
    "dve f_norm": [10, 4, 10],
    "dve f_split": [16, 9, 15],
    "dve gate_logits": [22, 21, 17],
    "dve gate_top": [27, 24, 21],
    "dve gate_weights": [30, 28, 27],
    "dve gate_rows": [33, 35, 33],
    "pe f_turn": [14, 8, 13],
    "pe f_router": [20, 10, 16],
    "pe f_logits": [21, 16, 17],
    "pe f_turn_w": [32, 29, 29],
    "pe turn_acc": 2,
    "dve finish": 3,
}


def macaron_kernel(nc, d, out):
    x_in = d["L0_attn_x"]
    C = x_in.shape[2]
    N_TOK = x_in.shape[0] * x_in.shape[1]
    N_CHUNK = N_TOK // CHUNK
    E, _, I = d["L0_ffn_We1"].shape
    RH = d["L0_ffn_Wr1"].shape[1]
    Q = E + 1
    IT = I // P
    STEPS = Q * IT
    N_SLOT = 2 * N_CHUNK
    RK, DS = d["L0_attn_W_dt"].shape[0], d["L0_attn_W_Bp"].shape[0]
    S = d["L1_attn_splat_positions"].shape[0]
    assert C == P and x_in.shape[1] == SEQ and E == 8
    assert STEPS % Z_BANKS == 0 and STEPS % H_BUFS == 0 and STEPS % SPLIT_BUFS == 0

    with ExitStack() as ctx:
        def sb(name, shape, dt=F32):
            return ctx.enter_context(nc.sbuf_tensor(name, shape, dt))

        def sem(name):
            return ctx.enter_context(nc.semaphore(name))

        def bank(name):
            return ctx.enter_context(nc.psum_tensor(name, [P, CHUNK], F32))

        x = sb("x_res", [P, N_TOK])
        w1_raw = sb("w1_raw", [P, Q, I])
        w2_raw = sb("w2_raw", [P, Q, IT, C])
        w1_hi, w1_lo = sb("w1_hi", [P, Q, I], F32R), sb("w1_lo", [P, Q, I], F32R)
        w2_hi, w2_lo = sb("w2_hi", [P, Q, IT, C], F32R), sb("w2_lo", [P, Q, IT, C], F32R)
        ident = sb("ident", [P, P])
        f_stat, f_mv, f_rstd = sb("f_stat", [P, TILES, 6]), sb("f_mv", [P, TILES, 2]), sb("f_rstd", [P, TILES])
        f_xh = sb("f_xh", [P, CHUNK])
        xT_hi, xT_lo = sb("xT_hi", [P, 2, CHUNK], F32R), sb("xT_lo", [P, 2, CHUNK], F32R)
        h = [sb(f"h{i}", [P, CHUNK]) for i in range(H_BUFS)]
        h_hi = [sb(f"h_hi{i}", [P, CHUNK], F32R) for i in range(SPLIT_BUFS)]
        h_lo = [sb(f"h_lo{i}", [P, CHUNK], F32R) for i in range(SPLIT_BUFS)]
        acc = sb("acc", [P, CHUNK])
        weighted = [sb(f"weighted{i}", [P, CHUNK]) for i in range(2)]
        w_bc = [sb(f"w_bc{i}", [P, CHUNK]) for i in range(W_BUFS)]
        wr1_raw = sb("wr1_raw", [P, P])
        wr1_hi, wr1_lo = sb("wr1_hi", [P, P], F32R), sb("wr1_lo", [P, P], F32R)
        wr2 = sb("wr2", [RH + 1, E])
        br1 = sb("br1", [RH, 1])
        r1 = sb("r1", [RH + 1, CHUNK])
        base_e, base_root_e = sb("base_e", [P, TILES, E]), sb("base_root_e", [P, TILES])
        lg_max, ex = sb("lg_max", [P, TILES]), sb("ex", [P, TILES, E])
        lg = sb("lg", [P, TILES, E])
        ex_sum, ex_rec = sb("ex_sum", [P, TILES]), sb("ex_rec", [P, TILES])
        gates, top = sb("gates", [P, TILES, E]), sb("top", [P, TILES, 8])
        top_at, top_atf = sb("top_at", [P, TILES, 8], U32), sb("top_atf", [P, TILES, 2])
        diff, ratio, ratio1 = sb("diff", [P, TILES]), sb("ratio", [P, TILES]), sb("ratio1", [P, TILES])
        tw = sb("tw", [P, TILES, 2])
        expert_no_i, expert_no = sb("expert_no_i", [P, E], mybir.dt.int32), sb("expert_no", [P, E])
        pick = [sb(f"pick{i}", [P, TILES, E]) for i in range(2)]
        pickw = [sb(f"pickw{i}", [P, TILES, E]) for i in range(2)]
        w_tok = sb("w_tok", [P, TILES, E])
        wT = sb("wT", [E, CHUNK])
        w_rows = nc.dram_tensor("w_rows", [E, CHUNK], F32)
        ROWS = IT * Q + Q + 11
        bias_rows, rows = sb("bias_rows", [IT * Q, P]), sb("rows", [ROWS - IT * Q, P])
        cols = sb("cols", [P, ROWS])
        w_in = sb("w_in", [P, 2 * C])
        w_xp, w_bg, w_cg = sb("w_xp", [P, RK]), sb("w_bg", [P, DS]), sb("w_cg", [P, DS])
        w_dt, w_bp, w_cp = sb("w_dt", [RK, C]), sb("w_bp", [DS, C]), sb("w_cp", [DS, C])
        w_out = sb("w_out", [P, C])
        small = sb("small", [P, S + 3 * P])
        pT = small[:, 0:S]
        w_xpT, w_bgT, w_cgT = small[0:RK, S:S + P], small[0:DS, S + P:S + 2 * P], small[0:DS, S + 2 * P:S + 3 * P]
        ffn_raw = sb("ffn_raw", [P, 4, P])
        ffnT = sb("ffnT", [P, 4, P])
        wo = sb("wo", [P, P])
        prod = sb("prod", [P, 4, P])
        pos = sb("pos", [S, P])
        pos_sq = sb("pos_sq", [S, P])
        nhalf_p2, logs, amp = sb("nhalf_p2", [S, 1]), sb("logs", [S, 1]), sb("amp", [S, 1])
        amp2, inv_s2 = sb("amp2", [S, 1]), sb("inv_s2", [S, 1])
        nhalf = sb("nhalf", [P, S])
        mhalf_exp = sb("mhalf_exp", [P, TILES])
        s_stat, s_mv = sb("s_stat", [P, TILES, 6]), sb("s_mv", [P, TILES, 2])
        s_r1, s_r2, s_v2 = sb("s_r1", [P, TILES]), sb("s_r2", [P, TILES]), sb("s_v2", [P, TILES])
        assert I == CHUNK
        side = [w1_raw[:, q, :] for q in range(Q)] + [sb(f"side{i}", [P, CHUNK])[:, :] for i in range(3)]
        xb_pad = sb("xb_pad", [P, SEQS, SEQ + 2])
        xT_pad = xb_pad
        a_xh1, a_xh2, a_xnT, a_c, a_xact, a_sz, a_u, a_l, a_dl, a_dA, a_dB, a_h = side
        r_xh, r_d, r_xk, r_xr, r_rk, r_ka, r_rr, r_t = side[0:8]
        l_xh, l_xT, l_sq, l_dd, l_E, l_Et, l_MT, l_R2 = side[1:9]
        gsum, gsum2 = sb("gsum", [S, SEQS]), sb("gsum2", [S, SEQS])
        den, rden = sb("den", [P, TILES]), sb("rden", [P, TILES])

        z = [bank(f"z{i}") for i in range(Z_BANKS)]
        y = [bank(f"y{i}") for i in range(Y_BANKS)]
        SF, SA = bank("SF"), bank("SA")

        at = {}
        row_loads = []
        r0 = 0
        for name, view, n in [
            ("bs1", d["L0_ffn_bs1"].rearrange("(a b) -> a b", b=P), IT),
            ("be1", d["L0_ffn_be1"].rearrange("e (a b) -> (e a) b", b=P), E * IT),
            ("bs2", d["L0_ffn_bs2"].rearrange("(a b) -> a b", b=P), 1),
            ("be2", d["L0_ffn_be2"], E),
            ("conv_w", d["L0_attn_conv_w"].rearrange("k a c -> (k a) c"), 3),
            ("gamma", d["L0_attn_gamma"].rearrange("(a b) -> a b", b=P), 1),
            ("beta", d["L0_attn_beta"].rearrange("(a b) -> a b", b=P), 1),
            ("conv_b", d["L0_attn_conv_b"].rearrange("(a b) -> a b", b=P), 1),
            ("b_dt", d["L0_attn_b_dt"].rearrange("(a b) -> a b", b=P), 1),
            ("A", d["L0_attn_A"].rearrange("(a b) -> a b", b=P), 1),
            ("D", d["L0_attn_D_skip"].rearrange("(a b) -> a b", b=P), 1),
            ("mu_k", d["L1_ffn_mu_k"].rearrange("(a b) -> a b", b=P), 1),
            ("mu_r", d["L1_ffn_mu_r"].rearrange("(a b) -> a b", b=P), 1),
        ]:
            at[name] = r0
            row_loads.append((r0, n, view))
            r0 += n
        assert r0 == ROWS

        def col(name, i=0):
            return cols[:, at[name] + i:at[name] + i + 1]

        def col_of(name, k):
            return cols[:, at[name] + k:at[name] + k + 1]

        x_loaded, x_rest_loaded = sem("x_loaded"), sem("x_rest_loaded")
        LOTS = [0, 1, 2, 3, 4, 6, Q]
        w_loaded = {q: sem(f"w_loaded{q}") for q in LOTS[:-1]}
        biases_loaded, rows_loaded = sem("biases_loaded"), sem("rows_loaded")
        router_loaded, side_loaded = sem("router_loaded"), sem("side_loaded")
        consts_made = sem("consts_made")
        dve_consts, dve_zeros = sem("dve_consts"), sem("dve_zeros")
        w1_hi_made, w1_split = sem("w1_hi_made"), sem("w1_split")
        w2_hi_made, w2_split = sem("w2_hi_made"), sem("w2_split")
        w1_0_hi_made, w1_0_split = sem("w1_0_hi_made"), sem("w1_0_split")
        router_hi, router_split = sem("router_hi"), sem("router_split")
        setup_act = sem("setup_act")
        f_bn, f_stats, f_rstd_in, f_rstd_done, f_xh_done = (sem(n) for n in (
            "f_bn", "f_stats", "f_rstd_in", "f_rstd_done", "f_xh_done"))
        s_bn, s_stats, s_rstd_steps, s_rstd_done, s_xh_done = (sem(n) for n in (
            "s_bn", "s_stats", "s_rstd_steps", "s_rstd_done", "s_xh_done"))
        sf_written, sf_read = sem("sf_written"), sem("sf_read")
        sa_written, sa_read = sem("sa_written"), sem("sa_read")
        xT_hi_made, w_stored = sem("xT_hi_made"), sem("w_stored")
        w_bc_loaded = [sem(f"w_bc_loaded{i}") for i in range(W_BUFS)]
        gate_step, gate_exp, gate_ratio, gate_diff, gate_w = (sem(n) for n in (
            "gate_step", "gate_exp", "gate_ratio", "gate_diff", "gate_w"))
        z_ready, h_ready, hi_ready, lo_ready, y_step = (sem(n) for n in (
            "z_ready", "h_ready", "hi_ready", "lo_ready", "y_step"))
        y_read, acc_added, accT_ready = sem("y_read"), sem("acc_added"), sem("accT_ready")
        a_abs = sem("a_abs")
        a_res, a_mid, a_conv, a_act, a_soft, a_relu, a_delta, a_decay, a_drive, a_scan, a_y, a_gated = (sem(n) for n in (
            "a_res", "a_mid", "a_conv", "a_act", "a_soft", "a_relu", "a_delta", "a_decay", "a_drive",
            "a_scan", "a_y", "a_gated"))
        r_diff, r_mixed, r_sq, r_done = (sem(n) for n in ("r_diff", "r_mixed", "r_sq", "r_done"))
        l_exp, l_gs, l_rec = (sem(n) for n in ("l_exp", "l_gs", "l_rec"))
        shared_sems = (sa_written, sa_read, s_bn, s_stats, s_rstd_steps, s_rstd_done, s_xh_done,
                       r_diff, r_mixed, r_sq, r_done, l_exp, l_gs, l_rec)
        own_sems = tuple(sem("own_" + name) for name in (
            "written", "read", "bn", "stats", "rstd_steps", "rstd_done", "xh_done",
            "diff", "mixed", "sq", "done", "exp", "gs", "rec"))
        stored = sem("stored")
        wait_carried = sem("wait_carried")

        def wait(eng, s, value):
            if not isinstance(value, int) or value > 0:
                eng.wait_ge(s, value)

        def wait_apart(eng, s, value):
            wait(eng, s, value)
            if not isinstance(value, int):
                eng.sem_inc(wait_carried, 1)

        def sf_at(s, use):
            return len(SF_USES) * (s + 1) + SF_USES.index(use)

        SA_A0 = len(SA_SETUP)
        SA_T0 = SA_A0 + N_CHUNK * len(SA_A)
        SA_T = 2 * len(SA_R) + len(SA_L)

        def sa_setup(use):
            return SA_SETUP.index(use)

        def sa_a(j, use):
            return j * len(SA_A) + SA_A0 + SA_A.index(use)

        class Part:
            def __init__(self, j, b0=0, b1=SEQS, own=False):
                self.b0, self.b1 = b0, b1
                self.c, self.j = j, 0 if own else j
                self.t0, self.t1 = b0 * (SEQ // P), b1 * (SEQ // P)
                self.sa0, self.stats0, self.rstd0 = (0, 0, 0) if own else (SA_T0, N_CHUNK, 6 * N_CHUNK)
                self.bank = z[0] if own else SA
                self.own = own
                (self.written, self.read, self.bn, self.stats, self.rstd_steps, self.rstd_done, self.xh_done,
                 self.diff, self.mixed, self.sq, self.done, self.exp, self.gs, self.rec) = (
                    (own_sems if own else shared_sems))

            def cols(self, a, width=P):
                return a[:, self.t0 * width:self.t1 * width]

            def r(self, o, use):
                return self.j * SA_T + self.sa0 + o * (len(SA_R) + len(SA_L)) + SA_R.index(use)

            def l(self, use):
                return self.j * SA_T + self.sa0 + len(SA_R) + SA_L.index(use)

            def n(self, o, each=3):
                return self.j * each + o

            def x(self):
                return x[:, bass.ds(self.c * CHUNK + self.t0 * P, (self.t1 - self.t0) * P)]

        def xs(c, t=None):
            if t is None:
                return x[:, bass.ds(c * CHUNK, CHUNK)]
            return x[:, bass.ds(c * CHUNK + t * P, P)]

        def tile(a, t):
            return a[:, t * P:(t + 1) * P]

        def prepared(s):
            return sf_at(s - 1, "T") + 1

        LAST_PARTS = [Part(N_CHUNK - 1, 0, 1), Part(N_CHUNK - 1, 1, SEQS, own=True)]

        def in_parts(plan):
            for _, work in plan:
                for v in LAST_PARTS:
                    work(v)

        block = ctx.enter_context(nc.Block())

        PHASES = (None, "A", "T")

        def at_step(plan, k, *args):
            for name, work in plan:
                if STEP[name] == k:
                    work(*args)

        def at_prep_step(plan, k, side, *args):
            for name, work in plan:
                if STEP[name][PHASES.index(side)] == k:
                    work(*args)

        def at_expert(name, work, k=None):
            for q in range(1, Q):
                at = (q - 1) * IT + STEP[name]
                if at == k or (k is None and at < 0):
                    work(q)

        def lot_of(q):
            return max(first for first in LOTS[:-1] if first <= q)

        SIDE_LOADS = [
            (w_in[:, :], d["L0_attn_W_in"]), (w_xp[:, :], d["L0_attn_W_xp"]), (w_bg[:, :], d["L0_attn_W_Bg"]),
            (w_cg[:, :], d["L0_attn_W_Cg"]), (w_dt[:, :], d["L0_attn_W_dt"]), (w_bp[:, :], d["L0_attn_W_Bp"]),
            (w_cp[:, :], d["L0_attn_W_Cp"]), (w_out[:, :], d["L0_attn_W_out"]),
            (ffn_raw[:, 0, :], d["L1_ffn_W_k"]), (ffn_raw[:, 1, :], d["L1_ffn_W_r"]),
            (ffn_raw[:, 2, :], d["L1_ffn_W_v"]), (ffn_raw[:, 3, :], d["L1_attn_Wv"]), (wo[:, :], d["L1_attn_Wo"]),
            (pos[:, :], d["L1_attn_splat_positions"]),
            (logs[:, :], d["L1_attn_splat_log_scales"].rearrange("(a b) -> a b", b=1)),
            (amp[:, :], d["L1_attn_splat_amplitudes"].rearrange("(a b) -> a b", b=1)),
        ]

        @block.sync
        def _(sp):
            tok = x_in.rearrange("b s c -> (b s) c").rearrange("(t p) f -> p t f", p=P)

            def load_x(t0, t1, s):
                sp.dma_start(x[:, t0 * C:t1 * C].rearrange("p (t f) -> p t f", f=C), tok[:, t0:t1]).then_inc(s, 16)

            def load_experts(q0, q1):
                if q0 == 0:
                    sp.dma_start(w1_raw[:, 0, :], d["L0_ffn_Ws1"]).then_inc(w_loaded[0], 16)
                    sp.dma_start(w2_raw[:, 0, :, :], d["L0_ffn_Ws2"].rearrange("(i p) c -> p i c", p=P))\
                        .then_inc(w_loaded[0], 16)
                    return
                sp.dma_start(w1_raw[:, q0:q1, :], d["L0_ffn_We1"][q0 - 1:q1 - 1].rearrange("e p i -> p e i"))\
                    .then_inc(w_loaded[q0], 16)
                w2 = d["L0_ffn_We2"][q0 - 1:q1 - 1].rearrange("e (i p) c -> p (e i) c", p=P)
                sp.dma_start(w2_raw[:, q0:q1, :, :].rearrange("p e i c -> p (e i) c"), w2)\
                    .then_inc(w_loaded[q0], 16)

            load_x(0, TILES, x_loaded)
            load_experts(0, 1)
            for dst, src in ((wr1_raw[:, 0:RH], d["L0_ffn_Wr1"]),
                             (br1[:, :], d["L0_ffn_br1"].rearrange("(a b) -> a b", b=1)),
                             (wr2[0:RH, :], d["L0_ffn_Wr2"]),
                             (wr2[RH:RH + 1, :], d["L0_ffn_br2"].rearrange("(a b) -> a b", a=1))):
                sp.dma_start(dst, src).then_inc(router_loaded, 16)
            load_experts(1, 2)
            load_experts(2, 3)
            for r, n, view in row_loads[2:]:
                sp.dma_start(rows[r - IT * Q:r - IT * Q + n, :], view).then_inc(rows_loaded, 16)
            load_experts(3, 4)
            load_x(TILES, N_TOK // P, x_rest_loaded)
            for q0, q1 in zip(LOTS[4:-1], LOTS[5:]):
                load_experts(q0, q1)
            for dst, src in SIDE_LOADS:
                sp.dma_start(dst, src).then_inc(side_loaded, 16)
            def spread_weights(s):
                wait(sp, sf_read, sf_at(s - 1, "W") + 1)
                for i in range(W_BUFS):
                    wait(sp, w_bc_loaded[i], 16 * s * (E // W_BUFS))
                sp.dma_start(w_rows[:, :], wT[:, :]).then_inc(w_stored, 16)
                wait(sp, w_stored, 16 * (s + 1))
                for q in range(1, Q):
                    if q > W_BUFS:
                        wait(sp, y_read, s * (Q + 1) + q - W_BUFS + 1)
                    elif not (isinstance(s, int) and s == 0):
                        wait(sp, y_read, (s - 1) * (Q + 1) + q + E - W_BUFS + 1)
                    sp.dma_start(w_bc[(q - 1) % W_BUFS][:, :], w_rows[q - 1:q, :].to_broadcast([P, CHUNK]))\
                        .then_inc(w_bc_loaded[(q - 1) % W_BUFS], 16)

            spread_weights(0)
            with sp.Fori(1, N_SLOT) as s:
                spread_weights(s)

            res = out.rearrange("b s c -> (b s) c").rearrange("(c t p) f -> c p t f", p=P, t=TILES)
            for v in [Part(c) for c in range(N_CHUNK - 1)] + LAST_PARTS:
                sp.wait_ge(v.done, v.n(2, 2))
                sp.dma_start(res[v.c][:, v.t0:v.t1], v.x().rearrange("p (t f) -> p t f", f=C)).then_inc(stored, 16)
            sp.wait_ge(stored, 16 * (N_CHUNK - 1 + len(LAST_PARTS)))

        @block.gpsimd
        def _(pool):
            made = 0

            def const(ins):
                nonlocal made
                made += 1
                ins.then_inc(consts_made, 1)
                pool.wait_ge(consts_made, made)

            const(pool.memset(ident[:, :], 0.0))
            const(pool.affine_select(out=ident[:, :], in_=ident[:, :], compare_op=ALU.not_equal, fill=1.0, base=0,
                                     pattern=[[-1, P]], channel_multiplier=1))

            def f_rstd_of(n):
                wait_apart(pool, f_stats, n + 1)
                pool.tensor_scalar(f_rstd[:, :], f_mv[:, :, 1], EPS, None, ALU.add).then_inc(f_rstd_in, 1)
                wait(pool, f_rstd_in, n + 1)
                pool.tensor_tensor(f_rstd[:, :], f_rstd[:, :], mhalf_exp[:, :], ALU.pow).then_inc(f_rstd_done, 1)

            def gate_exponent(n):
                wait(pool, sf_read, sf_at(n - 1, "L") + 1)
                pool.tensor_tensor(ex[:, :, :], base_e[:, :, :], lg[:, :, :], ALU.pow).then_inc(gate_exp, 1)

            def gate_ratio_of(n):
                wait(pool, gate_diff, n + 1)
                pool.tensor_tensor(ratio[:, :], base_root_e[:, :], diff[:, :], ALU.pow).then_inc(gate_ratio, 1)

            def add(s, q):
                wait(pool, y_read, s * (Q + 1) + q + 1)
                wait(pool, acc_added, s * E + q - 1)
                pool.tensor_tensor(acc[:, :], acc[:, :], weighted[q % 2][:, :], ALU.add).then_inc(acc_added, 1)

            def w1_lo_of(q):
                pool.wait_ge(w1_hi_made, q)
                pool.tensor_tensor(w1_lo[:, q, :], w1_raw[:, q, :], w1_hi[:, q, :].bitcast(F32), ALU.subtract)\
                    .then_inc(w1_split, 1)

            def w2_lo_of(q):
                pool.wait_ge(w2_hi_made, q + 1)
                pool.tensor_tensor(w2_lo[:, q, :, :], w2_raw[:, q, :, :], w2_hi[:, q, :, :].bitcast(F32),
                                   ALU.subtract).then_inc(w2_split, 1)

            def a_rstd(j):
                n = j * 6
                wait_apart(pool, s_stats, j + 1)
                pool.tensor_scalar(s_r1[:, :], s_mv[:, :, 1], EPS, None, ALU.add).then_inc(s_rstd_steps, 1)
                wait(pool, s_rstd_steps, n + 1)
                pool.tensor_tensor(s_r1[:, :], s_r1[:, :], mhalf_exp[:, :], ALU.pow).then_inc(s_rstd_steps, 1)
                wait(pool, s_rstd_steps, n + 2)
                pool.tensor_tensor(s_v2[:, :], s_r1[:, :], s_r1[:, :], ALU.mult).then_inc(s_rstd_steps, 1)
                wait(pool, s_rstd_steps, n + 3)
                pool.tensor_tensor(s_v2[:, :], s_v2[:, :], s_mv[:, :, 1], ALU.mult).then_inc(s_rstd_steps, 1)
                wait_apart(pool, s_rstd_steps, n + 4)
                pool.tensor_scalar(s_v2[:, :], s_v2[:, :], EPS, None, ALU.add).then_inc(s_rstd_steps, 1)
                wait(pool, s_rstd_steps, n + 5)
                pool.tensor_tensor(s_v2[:, :], s_v2[:, :], mhalf_exp[:, :], ALU.pow).then_inc(s_rstd_steps, 1)
                wait(pool, s_rstd_steps, n + 6)
                pool.tensor_tensor(s_r2[:, :], s_v2[:, :], s_r1[:, :], ALU.mult).then_inc(s_rstd_done, 1)

            def a_residual(j):
                wait(pool, s_xh_done, j + 1)
                pool.tensor_tensor(xs(j), xs(j), a_xh1[:, :], ALU.add).then_inc(a_res, 1)

            def a_conv_mid(j):
                wait_apart(pool, sa_read, sa_a(j, "xb") + 1)
                pool.tensor_scalar(a_c[:, :].rearrange("p (b s) -> p b s", b=SEQS), xb_pad[:, :, 1:SEQ + 1],
                                   col("conv_w", 1), col("conv_b"), ALU.mult, ALU.add).then_inc(a_mid, 1)

            def a_drive_x(j):
                wait(pool, sa_read, sa_a(j, "B") + 1)
                wait(pool, a_act, j + 1)
                pool.tensor_tensor(a_dB[:, :], a_dB[:, :], a_xact[:, :], ALU.mult).then_inc(a_drive, 1)

            def a_gate(j):
                wait(pool, a_y, j + 1)
                wait(pool, sa_read, sa_a(j, "z") + 1)
                pool.tensor_tensor(a_h[:, :], a_h[:, :], a_sz[:, :], ALU.mult).then_inc(a_gated, 1)

            A_POOL = [
                ("pool a_rstd", a_rstd),
                ("pool a_residual", a_residual),
                ("pool a_conv_mid", a_conv_mid),
                ("pool a_drive_x", a_drive_x),
                ("pool a_gate", a_gate),
            ]

            def t_rstd(o):
                def work(v):
                    r1 = v.cols(s_r1, 1)
                    wait_apart(pool, v.stats, v.stats0 + v.n(o + 1))
                    pool.tensor_scalar(r1, s_mv[:, v.t0:v.t1, 1], EPS, None, ALU.add).then_inc(v.rstd_steps, 1)
                    wait(pool, v.rstd_steps, v.rstd0 + v.n(o + 1))
                    pool.tensor_tensor(r1, r1, v.cols(mhalf_exp, 1), ALU.pow).then_inc(v.rstd_done, 1)
                return work

            def r_shift(o2):
                def work(v):
                    wait(pool, v.read, v.r(o2, "T") + 1)
                    pool.tensor_tensor(v.cols(r_d).rearrange("p (b s) -> p b s", s=SEQ),
                                       xT_pad[:, v.b0:v.b1, 1:SEQ + 1], xT_pad[:, v.b0:v.b1, 0:SEQ],
                                       ALU.subtract).then_inc(v.diff, 1)
                return work

            T_POOL = [
                ("pool t_rstd0", t_rstd(0)),
                ("pool r_shift0", r_shift(0)),
                ("pool t_rstd1", t_rstd(1)),
                ("pool t_rstd2", t_rstd(2)),
                ("pool r_shift1", r_shift(1)),
            ]

            PREP_POOL = [
                ("pool f_rstd", f_rstd_of),
                ("pool gate_exponent", gate_exponent),
                ("pool gate_ratio", gate_ratio_of),
            ]

            def slot(s, prep, side):
                for k in range(STEPS):
                    if k == 1 and not (isinstance(s, int) and s == 0):
                        add(s - 1, E)
                    if k % IT == 1 and 2 <= k // IT:
                        add(s, k // IT - 1)
                    if prep:
                        at_prep_step(PREP_POOL, k, side, s + 1)
                    if isinstance(s, int) and s == 0:
                        at_expert("pool w1_lo", w1_lo_of, k)
                        at_expert("pool w2_lo", w2_lo_of, k)
                    if side == "A":
                        at_step(A_POOL, k, s - 1)
                    if side == "T":
                        at_step(T_POOL, k, Part(s - (N_CHUNK + 1)))

            pool.wait_ge(dve_zeros, 1)
            f_rstd_of(0)
            pool.wait_ge(router_loaded, 16 * 4)
            pool.tensor_copy(wr1_hi[:, :], wr1_raw[:, :]).then_inc(router_hi, 1)
            w2_lo_of(0)
            const(pool.iota(expert_no_i[:, :], pattern=[[1, E]], base=0, channel_multiplier=0))
            at_expert("pool w1_lo", w1_lo_of)
            at_expert("pool w2_lo", w2_lo_of)
            gate_ratio_of(0)
            slot(0, True, None)
            with pool.Fori(1, N_CHUNK + 1) as s:
                slot(s, True, "A")
            with pool.Fori(N_CHUNK + 1, N_SLOT - 1) as s:
                slot(s, True, "T")
            slot(N_SLOT - 1, False, "T")
            add(N_SLOT - 1, E)
            in_parts(T_POOL)

        @block.scalar
        def _(act):
            for r, n, view in row_loads[0:2]:
                act.dma_start(bias_rows[r:r + n, :], view).then_inc(biases_loaded, 16)

            def silu(s, k, phase):
                n = s * STEPS + k
                wait(act, z_ready, n + 1)
                wait(act, lo_ready, n + 1 - H_BUFS)
                if k not in HI_ON_VECTOR[phase]:
                    wait(act, y_step, n + 1 - SPLIT_BUFS)
                    act.activation(h_hi[k % SPLIT_BUFS][:, :], z[k % Z_BANKS][:, :], ACT.Silu,
                                   bias=col_of("bs1", k))
                act.activation(h[k % H_BUFS][:, :], z[k % Z_BANKS][:, :], ACT.Silu,
                               bias=col_of("bs1", k)).then_inc(h_ready, 1)

            def w1_hi_of(q):
                act.wait_ge(w_loaded[lot_of(q)], 32)
                act.activation(w1_hi[:, q, :], w1_raw[:, q, :], ACT.Copy).then_inc(w1_hi_made, 1)

            def w2_hi_of(q):
                act.wait_ge(w_loaded[lot_of(q)], 32)
                act.activation(w2_hi[:, q, :, :], w2_raw[:, q, :, :], ACT.Copy).then_inc(w2_hi_made, 1)

            def router_relu(n):
                wait(act, sf_written, sf_at(n - 1, "R") + 1)
                act.activation(r1[0:RH, :], SF[0:RH, :], ACT.Relu, bias=br1[:, :]).then_inc(sf_read, 1)

            def a_silu_z(j):
                wait(act, sa_written, sa_a(j, "z") + 1)
                act.activation(a_sz[:, :], SA[:, :], ACT.Silu).then_inc(sa_read, 1)

            def a_silu_x(j):
                wait(act, a_conv, 2 * j + 2)
                act.activation(a_xact[:, :], a_c[:, :], ACT.Silu).then_inc(a_act, 1)

            def a_softplus(j):
                act.preload_act_table_set("natural_log_exp_and_others")
                wait(act, a_abs, j + 1)
                act.activation(a_l[:, :], a_l[:, :], ACT.Exp).then_inc(a_soft, 1)
                wait(act, a_soft, 2 * j + 1)
                act.activation(a_l[:, :], a_l[:, :], ACT.Ln, bias=1.0).then_inc(a_soft, 1)
                wait(act, a_delta, j + 1)
                act.activation(a_dA[:, :], a_dl[:, :], ACT.Exp, scale=col("A")).then_inc(a_decay, 1)

            A_ACT = [
                ("act a_silu_z", a_silu_z),
                ("act a_silu_x", a_silu_x),
                ("act a_softplus", a_softplus),
            ]

            def r_evac(o2):
                def work(v):
                    wait(act, v.written, v.r(o2, "T") + 1)
                    act.activation(xT_pad[:, v.b0:v.b1, 1:SEQ + 1],
                                   v.cols(v.bank).rearrange("p (b s) -> p b s", s=SEQ), ACT.Copy)\
                        .then_inc(v.read, 1)
                return work

            def r_square(o2):
                def work(v):
                    wait(act, v.written, v.r(o2, "k") + 1)
                    act.activation(v.cols(r_rk), v.cols(v.bank), ACT.Relu).then_inc(v.read, 1)
                    wait(act, v.read, v.r(o2, "k") + 1)
                    act.activation(v.cols(r_ka), v.cols(r_rk), ACT.Square).then_inc(v.sq, 1)
                return work

            def r_sigmoid(o2):
                def work(v):
                    wait(act, v.written, v.r(o2, "r") + 1)
                    act.activation(v.cols(r_rr), v.cols(v.bank), ACT.Tanh, scale=0.5).then_inc(v.read, 1)
                return work

            def l_evac(v):
                wait(act, v.written, v.l("T") + 1)
                act.activation(v.cols(l_xT), v.cols(v.bank), ACT.Copy)
                act.activation(v.cols(l_sq), v.cols(v.bank), ACT.Square).then_inc(v.read, 1)

            def l_gauss(v):
                act.preload_act_table_set("exp_and_others")
                wait(act, v.read, v.l("xp") + 1)
                for b in range(v.b0, v.b1):
                    last = act.activation(l_E[0:S, b * SEQ:(b + 1) * SEQ], l_dd[0:S, b * SEQ:(b + 1) * SEQ], ACT.Exp,
                                          scale=inv_s2[:, :], accum_out=gsum[:, b:b + 1])
                last.then_inc(v.exp, 1)

            def l_evac_E(v):
                wait(act, v.written, v.l("Et") + 1)
                act.activation(v.cols(l_Et, S), v.cols(v.bank, S), ACT.Copy).then_inc(v.read, 1)

            T_ACT = [
                ("act r_evac0", r_evac(0)),
                ("act r_square0", r_square(0)),
                ("act r_sigmoid0", r_sigmoid(0)),
                ("act l_evac", l_evac),
                ("act l_gauss", l_gauss),
                ("act l_evac_E", l_evac_E),
                ("act r_evac1", r_evac(1)),
                ("act r_square1", r_square(1)),
                ("act r_sigmoid1", r_sigmoid(1)),
            ]

            def slot(s, prep, side):
                for k in range(STEPS):
                    silu(s, k, PHASES.index(side))
                    if prep:
                        at_prep_step([("act router_relu", router_relu)], k, side, s + 1)
                    if isinstance(s, int) and s == 0 and k == STEP["act setup_scales"]:
                        act.wait_ge(side_loaded, 16 * len(SIDE_LOADS))
                        act.activation(inv_s2[:, :], logs[:, :], ACT.Exp, scale=-2.0).then_inc(setup_act, 1)
                    if isinstance(s, int) and s == 0:
                        at_expert("act w1_hi", w1_hi_of, k)
                        at_expert("act w2_hi", w2_hi_of, k)
                    if side == "A":
                        at_step(A_ACT, k, s - 1)
                    if side == "T":
                        at_step(T_ACT, k, Part(s - (N_CHUNK + 1)))

            act.preload_act_table_set("exp_and_others")
            act.wait_ge(w_loaded[0], 32)
            act.activation(w1_hi[:, 0, :], w1_raw[:, 0, :], ACT.Copy).then_inc(w1_0_hi_made, 1)
            w2_hi_of(0)
            at_expert("act w1_hi", w1_hi_of)
            at_expert("act w2_hi", w2_hi_of)
            act.wait_ge(router_loaded, 16 * 4)
            router_relu(0)
            act.wait_ge(sf_read, sf_at(-1, "L") + 1)
            act.activation(ex[:, :, :], lg[:, :, :], ACT.Exp).then_inc(gate_exp, 1)
            act.wait_ge(sa_read, sa_setup("biases") + 1)
            slot(0, True, None)
            with act.Fori(1, N_CHUNK + 1) as s:
                slot(s, True, "A")
            with act.Fori(N_CHUNK + 1, N_SLOT - 1) as s:
                slot(s, True, "T")
            slot(N_SLOT - 1, False, "T")
            in_parts(T_ACT)

        @block.vector
        def _(dve):
            def norm_stats(c, stat, mv, bn, stats, count, t0=0, t1=TILES):
                for t in range(t0, t1):
                    last = dve.bn_stats(stat[:, t, :], xs(c, t))
                last.then_inc(bn, 1)
                wait_apart(dve, bn, count + 1)
                for t in range(t0, t1):
                    last = dve.bn_aggr(mv[:, t, :], stat[:, t, :])
                last.then_inc(stats, 1)

            def norm_apply(c, dst, mv, rstd, t0=0, t1=TILES):
                for t in range(t0, t1):
                    last = dve.tensor_scalar(tile(dst, t), xs(c, t), mv[:, t, 0:1], rstd[:, t:t + 1],
                                             ALU.subtract, ALU.mult)
                return last

            def chunk_of(n):
                return n % N_CHUNK if isinstance(n, int) else n & (N_CHUNK - 1)

            def f_moments(n):
                norm_stats(chunk_of(n), f_stat, f_mv, f_bn, f_stats, n)

            def f_norm(n):
                wait(dve, f_rstd_done, n + 1)
                norm_apply(chunk_of(n), f_xh, f_mv, f_rstd).then_inc(f_xh_done, 1)

            def f_split(n):
                wait(dve, sf_written, sf_at(n - 1, "T") + 1)
                par = n % 2 if isinstance(n, int) else n & 1
                dve.tensor_copy(xT_hi[:, par, :], SF[:, :]).then_inc(xT_hi_made, 1)
                wait(dve, xT_hi_made, n + 1)
                dve.tensor_tensor(xT_lo[:, par, :], SF[:, :], xT_hi[:, par, :].bitcast(F32), ALU.subtract)\
                    .then_inc(sf_read, 1)

            GATE = 14

            def gate_logits(n):
                wait(dve, sf_written, sf_at(n - 1, "L") + 1)
                logits = SF[:, 0:TILES * E].rearrange("p (t e) -> p t e", e=E)
                dve.tensor_reduce(lg_max[:, :], logits, AX.X, ALU.max).then_inc(gate_step, 1)
                wait(dve, gate_step, GATE * n + 1)
                dve.tensor_tensor(lg[:, :, :], logits, lg_max[:, :].unsqueeze(2).to_broadcast([P, TILES, E]),
                                  ALU.subtract).then_inc(sf_read, 1)

            def gate_top(n):
                g = GATE * n
                wait(dve, gate_exp, n + 1)
                dve.tensor_reduce(ex_sum[:, :], ex[:, :, :], AX.X, ALU.add).then_inc(gate_step, 1)
                wait(dve, gate_step, g + 2)
                dve.reciprocal(ex_rec[:, :], ex_sum[:, :]).then_inc(gate_step, 1)
                wait(dve, gate_step, g + 3)
                dve.tensor_tensor(gates[:, :, :], ex[:, :, :], ex_rec[:, :].unsqueeze(2).to_broadcast([P, TILES, E]),
                                  ALU.mult).then_inc(gate_step, 1)
                wait_apart(dve, gate_step, g + 4)
                for t in range(TILES):
                    last = dve.max(top[:, t, :], gates[:, t, :])
                last.then_inc(gate_step, 1)
                wait(dve, gate_step, g + 5)
                dve.tensor_tensor(diff[:, :], top[:, :, 1], top[:, :, 0], ALU.subtract).then_inc(gate_diff, 1)
                for t in range(TILES):
                    last = dve.max_index(top_at[:, t, :], top[:, t, :], gates[:, t, :])
                last.then_inc(gate_step, 1)
                wait(dve, gate_step, g + 6)
                dve.tensor_copy(top_atf[:, :, :], top_at[:, :, 0:2]).then_inc(gate_step, 1)
                wait(dve, gate_step, g + 7)
                for i in range(2):
                    dve.tensor_tensor(pick[i][:, :, :], expert_no[:, :].unsqueeze(1).to_broadcast([P, TILES, E]),
                                      top_atf[:, :, i:i + 1].to_broadcast([P, TILES, E]), ALU.is_equal)\
                        .then_inc(gate_step, 1)

            def gate_weights(n):
                g = GATE * n + 9
                wait(dve, gate_ratio, n + 1)
                dve.tensor_scalar(ratio1[:, :], ratio[:, :], 1.0, None, ALU.add).then_inc(gate_step, 1)
                wait(dve, gate_step, g + 1)
                dve.reciprocal(tw[:, :, 0], ratio1[:, :]).then_inc(gate_step, 1)
                wait(dve, gate_step, g + 2)
                dve.tensor_tensor(tw[:, :, 1], tw[:, :, 0], ratio[:, :], ALU.mult).then_inc(gate_step, 1)
                wait(dve, gate_step, g + 3)
                for i in range(2):
                    dve.tensor_tensor(pickw[i][:, :, :], pick[i][:, :, :], tw[:, :, i:i + 1].to_broadcast([P, TILES, E]),
                                      ALU.mult).then_inc(gate_step, 1)
                wait(dve, gate_step, g + 5)
                dve.tensor_tensor(w_tok[:, :, :], pickw[0][:, :, :], pickw[1][:, :, :], ALU.add).then_inc(gate_w, 1)

            def gate_rows(n):
                wait(dve, sf_written, sf_at(n - 1, "W") + 1)
                wait(dve, w_stored, 16 * n)
                dve.tensor_copy(wT[:, :], SF[0:E, :]).then_inc(sf_read, 1)

            def lo(s, k, phase):
                n = s * STEPS + k
                wait(dve, h_ready, n + 1)
                wait(dve, y_step, n + 1 - SPLIT_BUFS)
                if k in HI_ON_VECTOR[phase]:
                    dve.tensor_copy(h_hi[k % SPLIT_BUFS][:, :], h[k % H_BUFS][:, :]).then_inc(hi_ready, 1)
                    n0, n1, n2 = (len(tiles) for tiles in HI_ON_VECTOR)
                    before = (0, (s - 1) * n1 + n0, (s - 1 - N_CHUNK) * n2 + n0 + N_CHUNK * n1)[phase]
                    wait(dve, hi_ready, before + HI_ON_VECTOR[phase].index(k) + 1)
                dve.tensor_tensor(h_lo[k % SPLIT_BUFS][:, :], h[k % H_BUFS][:, :],
                                  h_hi[k % SPLIT_BUFS][:, :].bitcast(F32), ALU.subtract).then_inc(lo_ready, 1)

            def combine(s, q):
                wait(dve, y_step, s * STEPS + IT * (q + 1))
                if q == 0:
                    if isinstance(s, int) and s == 0:
                        dve.wait_ge(sa_read, sa_setup("cols") + 1)
                    dve.tensor_scalar(acc[:, :], y[0][:, :], col("bs2"), None, ALU.add).then_inc(y_read, 1)
                    return
                wait(dve, w_bc_loaded[(q - 1) % W_BUFS], 16 * (s * (E // W_BUFS) + (q - 1) // W_BUFS + 1))
                wait(dve, acc_added, s * E + q - 2)
                dve.scalar_tensor_tensor(weighted[q % 2][:, :], y[q % Y_BANKS][:, :], col_of("bs2", q),
                                         w_bc[(q - 1) % W_BUFS][:, :], ALU.add, ALU.mult).then_inc(y_read, 1)

            def finish(s):
                wait(dve, accT_ready, s + 1)
                dve.scalar_tensor_tensor(xs(chunk_of(s)), y[1][:, :], 0.5, xs(chunk_of(s)), ALU.mult, ALU.add)\
                    .then_inc(y_read, 1)

            def setup_cols():
                dve.wait_ge(sa_written, sa_setup("cols") + 1)
                dve.tensor_copy(cols[:, IT * Q:ROWS], SA[:, 0:ROWS - IT * Q]).then_inc(sa_read, 1)

            def setup_small():
                dve.wait_ge(sa_written, sa_setup("small") + 1)
                dve.tensor_copy(small[:, 0:S], SA[:, 0:S])
                dve.tensor_copy(w_xpT, SA[0:RK, S:S + P])
                dve.tensor_copy(w_bgT, SA[0:DS, S + P:S + 2 * P])
                dve.tensor_copy(w_cgT, SA[0:DS, S + 2 * P:S + 3 * P]).then_inc(sa_read, 1)

            def setup_ffn1():
                dve.wait_ge(sa_written, sa_setup("ffn1") + 1)
                dve.tensor_copy(ffnT[:, :, :], SA[:, :].rearrange("p (a b) -> p a b", a=4)).then_inc(sa_read, 1)

            def setup_products():
                dve.wait_ge(sa_written, sa_setup("products") + 1)
                dve.tensor_copy(prod[:, :, :], SA[:, :].rearrange("p (a b) -> p a b", a=4)).then_inc(sa_read, 1)

            def setup_scalars():
                dve.wait_ge(side_loaded, 16 * len(SIDE_LOADS))
                dve.tensor_tensor(amp2[:, :], amp[:, :], amp[:, :], ALU.mult)
                dve.tensor_tensor(pos_sq[:, :], pos[:, :], pos[:, :], ALU.mult).then_inc(dve_consts, 1)
                dve.wait_ge(dve_consts, 2)
                dve.tensor_reduce(nhalf_p2[:, :], pos_sq[:, :], AX.X, ALU.add).then_inc(dve_consts, 1)
                dve.wait_ge(dve_consts, 3)
                dve.tensor_scalar(nhalf_p2[:, :], nhalf_p2[:, :], -0.5, None, ALU.mult).then_inc(dve_consts, 1)

            SETUP_DVE = [
                ("dve setup_cols", setup_cols),
                ("dve setup_small", setup_small),
                ("dve setup_ffn1", setup_ffn1),
                ("dve setup_scalars", setup_scalars),
                ("dve setup_products", setup_products),
            ]

            def a_moments(j):
                wait_apart(dve, y_read, (Q + 1) * (j + 1))
                dve.wait_ge(w1_split, Q - 1)
                norm_stats(j, s_stat, s_mv, s_bn, s_stats, j)

            def a_norm(j):
                wait(dve, s_rstd_done, j + 1)
                norm_apply(j, a_xh2, s_mv, s_r2)
                norm_apply(j, a_xh1, s_mv, s_r1).then_inc(s_xh_done, 1)

            def a_affine(j):
                wait(dve, sa_written, sa_a(j, "T") + 1)
                dve.tensor_scalar(a_xnT[:, :], SA[:, :], col("gamma"), col("beta"), ALU.mult, ALU.add)\
                    .then_inc(sa_read, 1)

            def a_pad(j):
                wait(dve, sa_written, sa_a(j, "xb") + 1)
                dve.tensor_copy(xb_pad[:, :, 1:SEQ + 1], SA[:, :].rearrange("p (b s) -> p b s", b=SEQS))\
                    .then_inc(sa_read, 1)

            def a_conv_sides(j):
                c = a_c[:, :].rearrange("p (b s) -> p b s", b=SEQS)
                wait(dve, a_mid, j + 1)
                dve.scalar_tensor_tensor(c, xb_pad[:, :, 0:SEQ], col("conv_w", 0), c, ALU.mult, ALU.add)\
                    .then_inc(a_conv, 1)
                wait(dve, a_conv, 2 * j + 1)
                dve.scalar_tensor_tensor(c, xb_pad[:, :, 2:SEQ + 2], col("conv_w", 2), c, ALU.mult, ALU.add)\
                    .then_inc(a_conv, 1)

            def a_dt(j):
                wait(dve, sa_written, sa_a(j, "dt") + 1)
                dve.tensor_scalar(a_u[:, :], SA[:, :], col("b_dt"), None, ALU.add).then_inc(sa_read, 1)
                wait(dve, sa_read, sa_a(j, "dt") + 1)
                dve.scalar_tensor_tensor(a_l[:, :], a_u[:, :], -1.0, a_u[:, :], ALU.mult, ALU.min).then_inc(a_abs, 1)
                dve.tensor_scalar(a_dl[:, :], a_u[:, :], 0.0, None, ALU.max).then_inc(a_relu, 1)

            def a_delta_sum(j):
                wait(dve, a_soft, 2 * j + 2)
                wait(dve, a_relu, j + 1)
                dve.tensor_tensor(a_dl[:, :], a_dl[:, :], a_l[:, :], ALU.add).then_inc(a_delta, 1)

            def a_times_B(j):
                wait(dve, sa_written, sa_a(j, "B") + 1)
                wait(dve, a_delta, j + 1)
                dve.tensor_tensor(a_dB[:, :], SA[:, :], a_dl[:, :], ALU.mult).then_inc(sa_read, 1)

            def a_recurrence(j):
                wait(dve, a_drive, j + 1)
                wait(dve, a_decay, j + 1)
                for b in range(SEQS):
                    last = dve.tensor_tensor_scan(a_h[:, b * SEQ:(b + 1) * SEQ], a_dA[:, b * SEQ:(b + 1) * SEQ],
                                                  a_dB[:, b * SEQ:(b + 1) * SEQ], 0.0, ALU.mult, ALU.add)
                last.then_inc(a_scan, 1)

            def a_times_C(j):
                wait(dve, sa_written, sa_a(j, "C") + 1)
                wait(dve, a_scan, j + 1)
                dve.tensor_tensor(a_h[:, :], SA[:, :], a_h[:, :], ALU.mult).then_inc(sa_read, 1)
                wait(dve, sa_read, sa_a(j, "C") + 1)
                dve.scalar_tensor_tensor(a_h[:, :], a_xact[:, :], col("D"), a_h[:, :], ALU.mult, ALU.add)\
                    .then_inc(a_y, 1)

            def a_add(j):
                wait(dve, sa_written, sa_a(j, "out") + 1)
                wait(dve, a_res, j + 1)
                dve.tensor_tensor(xs(j), SA[:, :], xs(j), ALU.add).then_inc(sa_read, 1)

            A_DVE = [
                ("dve a_moments", a_moments),
                ("dve a_norm", a_norm),
                ("dve a_affine", a_affine),
                ("dve a_pad", a_pad),
                ("dve a_conv_sides", a_conv_sides),
                ("dve a_dt", a_dt),
                ("dve a_delta_sum", a_delta_sum),
                ("dve a_times_B", a_times_B),
                ("dve a_recurrence", a_recurrence),
                ("dve a_times_C", a_times_C),
                ("dve a_add", a_add),
            ]

            def t_moments(o, before):
                def work(v):
                    before(v)
                    norm_stats(v.c, s_stat, s_mv, v.bn, v.stats, v.stats0 + v.n(o), v.t0, v.t1)
                return work

            def t_norm(o, dst):
                def work(v):
                    wait(dve, v.rstd_done, v.stats0 + v.n(o + 1))
                    norm_apply(v.c, dst, s_mv, s_r1, v.t0, v.t1).then_inc(v.xh_done, 1)
                return work

            def mixture_in(v):
                wait_apart(dve, y_read, (Q + 1) * (v.c + N_CHUNK + 1))
                wait(dve, sa_read, SA_T0)

            def first_r_in(v):
                wait_apart(dve, v.done, v.n(1, 2))

            def splats_in(v):
                wait_apart(dve, v.read, v.l("out") + 1)

            def r_mix(o2):
                def work(v):
                    wait(dve, v.diff, v.n(o2 + 1, 2))
                    for dst, mu in ((r_xk, "mu_k"), (r_xr, "mu_r")):
                        dve.scalar_tensor_tensor(v.cols(dst).rearrange("p (b s) -> p b s", s=SEQ),
                                                 v.cols(r_d).rearrange("p (b s) -> p b s", s=SEQ), col(mu),
                                                 xT_pad[:, v.b0:v.b1, 0:SEQ], ALU.mult, ALU.add).then_inc(v.mixed, 1)
                return work

            def r_out(o2):
                def work(v):
                    wait(dve, v.written, v.r(o2, "v") + 1)
                    wait(dve, v.read, v.r(o2, "r") + 1)
                    dve.scalar_tensor_tensor(v.cols(r_t), v.cols(r_rr), 1.0, v.cols(v.bank), ALU.add, ALU.mult)\
                        .then_inc(v.read, 1)
                    wait(dve, v.read, v.r(o2, "v") + 1)
                    dve.scalar_tensor_tensor(v.x(), v.cols(r_t), 0.25, v.x(), ALU.mult, ALU.add).then_inc(v.done, 1)
                return work

            def l_distance(v):
                wait(dve, v.written, v.l("xp") + 1)
                dve.tensor_scalar(v.cols(l_dd)[0:S, :], v.cols(v.bank)[0:S, :], nhalf_p2[:, :], 0.0, ALU.add, ALU.min)\
                    .then_inc(v.read, 1)

            def l_evac_M(v):
                wait(dve, v.written, v.l("MT") + 1)
                dve.tensor_copy(l_MT[:, v.b0 * S:v.b1 * S], v.bank[:, v.b0 * S:v.b1 * S]).then_inc(v.read, 1)
                wait(dve, v.exp, v.n(1, 1))
                dve.tensor_scalar(gsum2[:, v.b0:v.b1], gsum[:, v.b0:v.b1], amp2[:, :], None, ALU.mult)\
                    .then_inc(v.gs, 1)

            def l_evac_B(v):
                wait(dve, v.written, v.l("B") + 1)
                dve.tensor_scalar(l_R2[0:S, v.b0 * P:v.b1 * P], v.bank[0:S, v.b0 * P:v.b1 * P], amp2[:, :], None,
                                  ALU.mult).then_inc(v.read, 1)

            def l_sums(v):
                wait(dve, v.written, v.l("sum") + 1)
                dve.tensor_scalar(v.cols(den, 1), v.cols(v.bank, 1), EPS_ATTN, None, ALU.add).then_inc(v.read, 1)
                wait(dve, v.read, v.l("sum") + 1)
                dve.reciprocal(v.cols(rden, 1), v.cols(den, 1)).then_inc(v.rec, 1)

            def l_out(v):
                wait(dve, v.written, v.l("out") + 1)
                wait(dve, v.rec, v.n(1, 1))
                for t in range(v.t0, v.t1):
                    last = dve.scalar_tensor_tensor(xs(v.c, t), tile(v.bank, t), rden[:, t:t + 1], xs(v.c, t),
                                                    ALU.mult, ALU.add)
                last.then_inc(v.read, 1)

            T_DVE = [
                ("dve t_moments0", t_moments(0, mixture_in)),
                ("dve t_norm0", t_norm(0, r_xh)),
                ("dve r_mix0", r_mix(0)),
                ("dve r_out0", r_out(0)),
                ("dve t_moments1", t_moments(1, first_r_in)),
                ("dve t_norm1", t_norm(1, l_xh)),
                ("dve l_distance", l_distance),
                ("dve l_evac_M", l_evac_M),
                ("dve l_evac_B", l_evac_B),
                ("dve l_sums", l_sums),
                ("dve l_out", l_out),
                ("dve t_moments2", t_moments(2, splats_in)),
                ("dve t_norm2", t_norm(2, r_xh)),
                ("dve r_mix1", r_mix(1)),
                ("dve r_out1", r_out(1)),
            ]

            def f_moments_next(n, side):
                if side is None:
                    dve.wait_ge(x_rest_loaded, 16)
                elif side == "A":
                    wait_apart(dve, sa_read, sa_a(n - 2, "T"))
                else:
                    dve.wait_ge(sa_read, SA_T0)
                f_moments(n)

            PREP_DVE = [
                ("dve f_moments", f_moments_next),
                ("dve f_norm", lambda n, side: f_norm(n)),
                ("dve f_split", lambda n, side: f_split(n)),
                ("dve gate_logits", lambda n, side: gate_logits(n)),
                ("dve gate_top", lambda n, side: gate_top(n)),
                ("dve gate_weights", lambda n, side: gate_weights(n)),
                ("dve gate_rows", lambda n, side: gate_rows(n)),
            ]

            def slot(s, prep, side):
                first = isinstance(s, int) and s == 0
                for k in range(STEPS):
                    lo(s, k, PHASES.index(side))
                    if k == 1 and not first:
                        combine(s - 1, E)
                    if k == STEP["dve finish"] and not first:
                        finish(s - 1)
                    if k % IT == 1 and 1 <= k // IT:
                        combine(s, k // IT - 1)
                    if first:
                        at_step([("dve gate_top0", gate_top), ("dve gate_weights0", gate_weights),
                                 ("dve gate_rows0", gate_rows)], k, 0)
                    if prep:
                        at_prep_step(PREP_DVE, k, side, s + 1, side)
                    if first:
                        at_step(SETUP_DVE, k)
                    if side == "A":
                        at_step(A_DVE, k, s - 1)
                    if side == "T":
                        at_step(T_DVE, k, Part(s - (N_CHUNK + 1)))

            for ap, value in ((mhalf_exp[:, :], -0.5), (base_e[:, :, :], math.e), (base_root_e[:, :], math.exp(0.5)),
                              (wr1_raw[:, RH:P], 0.0), (nhalf[:, :], -0.5), (r1[RH:RH + 1, :], 1.0)):
                last = dve.memset(ap, value)
            last.then_inc(dve_zeros, 1)
            dve.memset(xb_pad[:, :, :], 0.0)
            dve.wait_ge(x_loaded, 16)
            f_moments(0)
            dve.wait_ge(w1_0_hi_made, 1)
            dve.tensor_tensor(w1_lo[:, 0, :], w1_raw[:, 0, :], w1_hi[:, 0, :].bitcast(F32), ALU.subtract)\
                .then_inc(w1_0_split, 1)
            f_norm(0)
            dve.wait_ge(router_hi, 1)
            dve.tensor_tensor(wr1_lo[:, :], wr1_raw[:, :], wr1_hi[:, :].bitcast(F32), ALU.subtract)\
                .then_inc(router_split, 1)
            f_split(0)
            dve.wait_ge(sa_written, sa_setup("biases") + 1)
            dve.tensor_copy(cols[:, 0:IT * Q], SA[:, 0:IT * Q]).then_inc(sa_read, 1)
            gate_logits(0)
            dve.wait_ge(consts_made, 3)
            dve.tensor_copy(expert_no[:, :], expert_no_i[:, :]).then_inc(dve_consts, 1)
            dve.wait_ge(dve_consts, 1)
            slot(0, True, None)
            with dve.Fori(1, N_CHUNK + 1) as s:
                slot(s, True, "A")
            with dve.Fori(N_CHUNK + 1, N_SLOT - 1) as s:
                slot(s, True, "T")
            slot(N_SLOT - 1, False, "T")
            combine(N_SLOT - 1, E)
            finish(N_SLOT - 1)
            in_parts(T_DVE)

        @block.tensor
        def _(pe):
            def parity(s):
                return s % 2 if isinstance(s, int) else s & 1

            def three(dst, w_hi, w_lo, m_hi, m_lo, start, stop):
                pe.matmul(dst, w_hi, m_hi, start=start, stop=False)
                pe.matmul(dst, w_hi, m_lo, start=False, stop=False)
                return pe.matmul(dst, w_lo, m_hi, start=False, stop=stop)

            def z_tile(s, k):
                q, i = divmod(k, IT)
                if k == 0:
                    wait(pe, sf_read, prepared(s))
                if isinstance(s, int) and s == 0 and i == 0:
                    if q == 0:
                        pe.wait_ge(w1_0_split, 1)
                    else:
                        pe.wait_ge(w1_split, q)
                wait(pe, h_ready, s * STEPS + k + 1 - Z_BANKS)
                par = parity(s)
                three(z[k % Z_BANKS][:, :], w1_hi[:, q, i * P:(i + 1) * P], w1_lo[:, q, i * P:(i + 1) * P],
                      xT_hi[:, par, :], xT_lo[:, par, :], True, True).then_inc(z_ready, 1)

            def y_tile(s, k):
                q, i = divmod(k, IT)
                if isinstance(s, int) and s == 0 and i == 0:
                    pe.wait_ge(w2_split, q + 1)
                if i == 0:
                    wait(pe, y_read, s * (Q + 1) + q + 1 - Y_BANKS)
                wait(pe, lo_ready, s * STEPS + k + 1)
                three(y[q % Y_BANKS][:, :], w2_hi[:, q, i, :], w2_lo[:, q, i, :],
                      h_hi[k % SPLIT_BUFS][:, :], h_lo[k % SPLIT_BUFS][:, :], i == 0, i == IT - 1).then_inc(y_step, 1)

            def turn_acc(s):
                wait(pe, acc_added, E * (s + 1))
                wait(pe, y_read, s * (Q + 1) + Q - 1)
                for t in range(TILES):
                    last = pe.transpose(tile(y[1], t), tile(acc, t), ident[:, :])
                last.then_inc(accT_ready, 1)

            def use_sf(s, use):
                wait(pe, sf_read, sf_at(s, use))

            def f_turn(n):
                use_sf(n - 1, "T")
                wait(pe, f_xh_done, n + 1)
                for t in range(TILES):
                    last = pe.transpose(tile(SF, t), tile(f_xh, t), ident[:, :])
                last.then_inc(sf_written, 1)

            def f_router(n):
                use_sf(n - 1, "R")
                par = parity(n)
                three(SF[:, :], wr1_hi[:, :], wr1_lo[:, :], xT_hi[:, par, :], xT_lo[:, par, :], True, True)\
                    .then_inc(sf_written, 1)

            def f_logits(n):
                use_sf(n - 1, "L")
                for t in range(TILES):
                    last = pe.matmul(SF[:, t * E:(t + 1) * E], tile(r1, t), wr2[:, :], start=True, stop=True)
                last.then_inc(sf_written, 1)

            def f_turn_w(n):
                use_sf(n - 1, "W")
                wait(pe, gate_w, n + 1)
                for t in range(TILES):
                    last = pe.transpose(SF[0:E, t * P:(t + 1) * P], w_tok[:, t, :], ident[:, :])
                last.then_inc(sf_written, 1)

            def turn_biases():
                n = IT * Q
                pe.wait_ge(biases_loaded, 16 * 2)
                pe.transpose(SA[:, 0:n], bias_rows[:, :], ident[0:n, 0:n]).then_inc(sa_written, 1)

            def turn_cols():
                n = ROWS - IT * Q
                pe.wait_ge(rows_loaded, 16 * (len(row_loads) - 2))
                pe.wait_ge(sa_read, sa_setup("cols"))
                pe.transpose(SA[:, 0:n], rows[:, :], ident[0:n, 0:n]).then_inc(sa_written, 1)

            def turn_small():
                pe.wait_ge(side_loaded, 16 * len(SIDE_LOADS))
                pe.wait_ge(sa_read, sa_setup("small"))
                pe.transpose(SA[:, 0:S], pos[:, :], ident[0:S, 0:S])
                pe.transpose(SA[0:RK, S:S + P], w_xp[:, :], ident[:, :])
                pe.transpose(SA[0:DS, S + P:S + 2 * P], w_bg[:, :], ident[:, :])
                pe.transpose(SA[0:DS, S + 2 * P:S + 3 * P], w_cg[:, :], ident[:, :]).then_inc(sa_written, 1)

            def turn_ffn1():
                pe.wait_ge(sa_read, sa_setup("ffn1"))
                for n in range(4):
                    last = pe.transpose(tile(SA, n), ffn_raw[:, n, :], ident[:, :])
                last.then_inc(sa_written, 1)

            def make_products():
                pe.wait_ge(sa_read, sa_setup("products"))
                for n, (wT_, w_) in enumerate(((w_xpT, w_dt[:, :]), (w_bgT, w_bp[:, :]), (w_cgT, w_cp[:, :]),
                                               (ffnT[:, 3, :], wo[:, :]))):
                    last = pe.matmul(tile(SA, n), wT_, w_, start=True, stop=True)
                last.then_inc(sa_written, 1)

            SETUP_PE = [
                ("pe turn_cols", turn_cols),
                ("pe turn_small", turn_small),
                ("pe turn_ffn1", turn_ffn1),
                ("pe make_products", make_products),
            ]

            def a_turn(j):
                wait(pe, sa_read, sa_a(j, "T"))
                wait(pe, s_xh_done, j + 1)
                for t in range(TILES):
                    last = pe.transpose(tile(SA, t), tile(a_xh2, t), ident[:, :])
                last.then_inc(sa_written, 1)

            def a_project(use, w, src):
                def work(j):
                    wait(pe, sa_read, sa_a(j, use))
                    if use == "dt":
                        wait(pe, a_act, j + 1)
                    pe.matmul(SA[:, :], w, src[:, :], start=True, stop=True).then_inc(sa_written, 1)
                return work

            def a_output(j):
                wait(pe, a_gated, j + 1)
                wait(pe, sa_read, sa_a(j, "out"))
                for t in range(TILES):
                    last = pe.matmul(tile(SA, t), tile(a_h, t), w_out[:, :], start=True, stop=True)
                last.then_inc(sa_written, 1)

            A_PE = [
                ("pe a_turn", a_turn),
                ("pe a_xb", a_project("xb", w_in[:, 0:C], a_xnT)),
                ("pe a_z", a_project("z", w_in[:, C:2 * C], a_xnT)),
                ("pe a_dt", a_project("dt", prod[:, 0, :], a_xact)),
                ("pe a_B", a_project("B", prod[:, 1, :], a_xact)),
                ("pe a_C", a_project("C", prod[:, 2, :], a_xact)),
                ("pe a_output", a_output),
            ]

            def t_turn(src, at_use, o):
                def work(v):
                    wait(pe, v.read, at_use(v))
                    if v.own and o == 0:
                        pe.wait_ge(h_ready, N_SLOT * STEPS)
                    wait(pe, v.xh_done, v.stats0 + v.n(o + 1))
                    for t in range(v.t0, v.t1):
                        last = pe.transpose(tile(v.bank, t), tile(src, t), ident[:, :])
                    last.then_inc(v.written, 1)
                return work

            def r_key(o2):
                def work(v):
                    wait(pe, v.read, v.r(o2, "k"))
                    wait(pe, v.mixed, v.n(2 * o2 + 1, 4))
                    pe.matmul(v.cols(v.bank), ffnT[:, 0, :], v.cols(r_xk), start=True, stop=True)\
                        .then_inc(v.written, 1)
                return work

            def r_receptance(o2):
                def work(v):
                    wait(pe, v.read, v.r(o2, "r"))
                    wait(pe, v.mixed, v.n(2 * o2 + 2, 4))
                    for t in range(v.t0, v.t1):
                        last = pe.matmul(tile(v.bank, t), tile(r_xr, t), ffnT[:, 1, :], start=True, stop=True)
                    last.then_inc(v.written, 1)
                return work

            def r_value(o2):
                def work(v):
                    wait(pe, v.read, v.r(o2, "v"))
                    wait(pe, v.sq, v.n(o2 + 1, 2))
                    for t in range(v.t0, v.t1):
                        last = pe.matmul(tile(v.bank, t), tile(r_ka, t), ffnT[:, 2, :], start=True, stop=True)
                    last.then_inc(v.written, 1)
                return work

            def l_products(v):
                wait(pe, v.read, v.l("xp"))
                pe.matmul(v.cols(v.bank)[0:S, :], pT, v.cols(l_xT), start=True, stop=False)
                pe.matmul(v.cols(v.bank)[0:S, :], nhalf[:, :], v.cols(l_sq), start=False, stop=True)\
                    .then_inc(v.written, 1)

            def l_turn_E(v):
                wait(pe, v.read, v.l("Et"))
                wait_apart(pe, v.exp, v.n(1, 1))
                for t in range(v.t0, v.t1):
                    last = pe.transpose(v.bank[:, t * S:(t + 1) * S], l_E[0:S, t * P:(t + 1) * P], ident[0:S, 0:S])
                last.then_inc(v.written, 1)

            def l_moment(v):
                wait(pe, v.read, v.l("MT"))
                for t in range(v.t0, v.t1):
                    b, i = divmod(t, SEQ // P)
                    last = pe.matmul(v.bank[:, b * S:(b + 1) * S], tile(l_xh, t), l_Et[:, t * S:(t + 1) * S],
                                     start=(i == 0), stop=(i == SEQ // P - 1))
                last.then_inc(v.written, 1)

            def l_values(v):
                wait(pe, v.read, v.l("B"))
                for b in range(v.b0, v.b1):
                    last = pe.matmul(v.bank[0:S, b * P:(b + 1) * P], l_MT[:, b * S:(b + 1) * S], prod[:, 3, :],
                                     start=True, stop=True)
                last.then_inc(v.written, 1)

            def l_row_sums(v):
                wait(pe, v.read, v.l("sum"))
                wait(pe, v.gs, v.n(1, 1))
                for t in range(v.t0, v.t1):
                    b = t // (SEQ // P)
                    last = pe.matmul(v.bank[:, t:t + 1], l_E[0:S, t * P:(t + 1) * P], gsum2[:, b:b + 1],
                                     start=True, stop=True)
                last.then_inc(v.written, 1)

            def l_output(v):
                wait(pe, v.read, v.l("out"))
                for t in range(v.t0, v.t1):
                    b = t // (SEQ // P)
                    last = pe.matmul(tile(v.bank, t), l_E[0:S, t * P:(t + 1) * P], l_R2[0:S, b * P:(b + 1) * P],
                                     start=True, stop=True)
                last.then_inc(v.written, 1)

            T_PE = [
                ("pe t_turn0", t_turn(r_xh, lambda v: v.r(0, "T"), 0)),
                ("pe r_key0", r_key(0)),
                ("pe r_receptance0", r_receptance(0)),
                ("pe r_value0", r_value(0)),
                ("pe t_turn1", t_turn(l_xh, lambda v: v.l("T"), 1)),
                ("pe l_products", l_products),
                ("pe l_turn_E", l_turn_E),
                ("pe l_moment", l_moment),
                ("pe l_values", l_values),
                ("pe l_row_sums", l_row_sums),
                ("pe l_output", l_output),
                ("pe t_turn2", t_turn(r_xh, lambda v: v.r(1, "T"), 2)),
                ("pe r_key1", r_key(1)),
                ("pe r_receptance1", r_receptance(1)),
                ("pe r_value1", r_value(1)),
            ]

            PREP_PE = [
                ("pe f_turn", f_turn),
                ("pe f_router", f_router),
                ("pe f_logits", f_logits),
                ("pe f_turn_w", f_turn_w),
            ]

            def slot(s, prep, side, more):
                first = isinstance(s, int) and s == 0
                for k in range(STEPS):
                    if k + LOOKAHEAD < STEPS:
                        z_tile(s, k + LOOKAHEAD)
                    elif more:
                        z_tile(s + 1, k + LOOKAHEAD - STEPS)
                    if k == STEP["pe turn_acc"] and not first:
                        turn_acc(s - 1)
                    if first and k == STEP["pe f_turn_w0"]:
                        f_turn_w(0)
                    if prep:
                        at_prep_step(PREP_PE, k, side, s + 1)
                    if first:
                        at_step(SETUP_PE, k)
                    if side == "A":
                        at_step(A_PE, k, s - 1)
                    if side == "T":
                        at_step(T_PE, k, Part(s - (N_CHUNK + 1)))
                    y_tile(s, k)

            pe.wait_ge(consts_made, 2)
            f_turn(0)
            turn_biases()
            pe.wait_ge(router_split, 1)
            f_router(0)
            z_tile(0, 0)
            f_logits(0)
            for k in range(1, LOOKAHEAD):
                z_tile(0, k)
            slot(0, True, None, True)
            with pe.Fori(1, N_CHUNK + 1) as s:
                slot(s, True, "A", True)
            with pe.Fori(N_CHUNK + 1, N_SLOT - 1) as s:
                slot(s, True, "T", True)
            slot(N_SLOT - 1, False, "T", False)
            turn_acc(N_SLOT - 1)
            in_parts(T_PE)


_INS = [
    "L0_attn_x", "L0_attn_gamma", "L0_attn_beta", "L0_attn_W_in", "L0_attn_conv_w", "L0_attn_conv_b",
    "L0_attn_W_xp", "L0_attn_W_Bg", "L0_attn_W_Cg", "L0_attn_W_dt", "L0_attn_b_dt", "L0_attn_W_Bp",
    "L0_attn_W_Cp", "L0_attn_A", "L0_attn_D_skip", "L0_attn_W_out", "L0_ffn_Wr1", "L0_ffn_br1", "L0_ffn_Wr2",
    "L0_ffn_br2", "L0_ffn_Ws1", "L0_ffn_bs1", "L0_ffn_Ws2", "L0_ffn_bs2", "L0_ffn_We1", "L0_ffn_be1",
    "L0_ffn_We2", "L0_ffn_be2", "L1_attn_splat_positions", "L1_attn_splat_log_scales",
    "L1_attn_splat_amplitudes", "L1_attn_Wv", "L1_attn_Wo", "L1_ffn_W_r", "L1_ffn_W_k", "L1_ffn_W_v",
    "L1_ffn_mu_r", "L1_ffn_mu_k",
]


def kernel(**inputs):
    import numpy as _np
    import concourse.bacc as _bacc
    from concourse import mybir as _mybir
    from concourse.bass_utils import run_bass_kernel_spmd as _run

    nc = _bacc.Bacc("TRN2", target_bir_lowering=False, num_devices=1)
    arrays, aps = {}, {}
    for name in _INS:
        a = _np.ascontiguousarray(inputs[name])
        arrays[f"in_{name}_dram"] = a
        aps[name] = nc.dram_tensor(f"in_{name}_dram", a.shape, _mybir.dt.from_np(a.dtype),
                                   kind="ExternalInput").ap()
    x = arrays["in_L0_attn_x_dram"]
    out = nc.dram_tensor("out_0_dram", x.shape, _mybir.dt.from_np(x.dtype), kind="ExternalOutput").ap()
    macaron_kernel(nc, aps, out)
    r = _run(nc, [arrays], core_ids=[0])
    return r.results[0]["out_0_dram"]
```
